# Optimizing a Trainium2 kernel written in Bass

```python
import numpy as np
import jax
import jax.numpy as jnp

def _softmax(x, axis=-1):
    return jax.nn.softmax(x, axis=axis)

def _gelu(x):
    return jax.nn.gelu(x, approximate=True)

def _silu(x):
    return jax.nn.silu(x)

def _sigmoid(x):
    return jax.nn.sigmoid(x)

def _layernorm(x, axis=-1, eps=1e-05):
    m = jnp.mean(x, axis=axis, keepdims=True)
    v = jnp.var(x, axis=axis, keepdims=True)
    return (x - m) / jnp.sqrt(v + eps)

def _scatter_add(tgt, idx, src, axis=0):
    return tgt.at[idx].add(src)

def _segment_sum(src, seg, n):
    return jax.ops.segment_sum(src, seg, n)
kernel_name = 'mk_gnn_preln_d2_gnn_r32_3b4506'

def setup_inputs(seed: int=0):
    np.random.seed(seed)
    _w = jnp.asarray

    def _rec_inputs():
        import jax
        import jax.numpy as jnp
        _gk = jax.random.key(seed)
        x = -0.0003713 + 1 * jax.random.normal(jax.random.fold_in(_gk, 1), (50000, 256), jnp.float32)
        src = jax.random.randint(jax.random.fold_in(_gk, 2), (50000,), 0, 50000, jnp.int32)
        dst = jax.random.randint(jax.random.fold_in(_gk, 3), (50000,), 0, 50000, jnp.int32)
        _o = jnp.argsort(dst, stable=True)
        src = src[_o]
        dst = dst[_o]
        edge_attr_64 = -9.77346e-05 + 0.999888 * jax.random.normal(jax.random.fold_in(_gk, 12), (50000, 64), jnp.float32)
        return (x, src, dst, edge_attr_64)
    x, src, dst, edge_attr_64 = _rec_inputs()

    def _L0_gnn_setup():
        import jax, jax.numpy as jnp
        import numpy as np
        N_NODES = 50000
        N_EDGES = 25000
        IN_FEATS = 256
        HIDDEN = 256

        def _sage_conv(x, src, dst, Wl, bl, Wr):
            msg = x[src]
            agg = jax.ops.segment_sum(msg, dst, num_segments=N_NODES)
            cnt = jax.ops.segment_sum(jnp.ones((src.shape[0],), dtype=x.dtype), dst, num_segments=N_NODES)
            mean = agg / jnp.maximum(cnt, 1.0)[:, None]
            return mean @ Wl.T + bl + x @ Wr.T
        key = jax.random.key(seed)
        ks = jax.random.split(key, 8)
        x = jax.random.normal(ks[0], (N_NODES, IN_FEATS), dtype=jnp.float32)
        edge_index = jax.random.randint(ks[1], (2, N_EDGES), 0, N_NODES, dtype=jnp.int32)
        s = 1.0 / np.sqrt(IN_FEATS)
        W1l = jax.random.uniform(ks[2], (HIDDEN, IN_FEATS), minval=-s, maxval=s, dtype=jnp.float32)
        b1 = jax.random.uniform(ks[3], (HIDDEN,), minval=-s, maxval=s, dtype=jnp.float32)
        W1r = jax.random.uniform(ks[4], (HIDDEN, IN_FEATS), minval=-s, maxval=s, dtype=jnp.float32)
        s2 = 1.0 / np.sqrt(HIDDEN)
        W2l = jax.random.uniform(ks[5], (HIDDEN, HIDDEN), minval=-s2, maxval=s2, dtype=jnp.float32)
        b2 = jax.random.uniform(ks[6], (HIDDEN,), minval=-s2, maxval=s2, dtype=jnp.float32)
        W2r = jax.random.uniform(ks[7], (HIDDEN, HIDDEN), minval=-s2, maxval=s2, dtype=jnp.float32)
        return {'x': x, 'edge_index': edge_index, 'W1l': W1l, 'b1': b1, 'W1r': W1r, 'W2l': W2l, 'b2': b2, 'W2r': W2r}
    _L0_gnn_all = _L0_gnn_setup()
    _L0_gnn_in = {k: v for k, v in _L0_gnn_all.items() if k in ('W1l', 'b1', 'W1r', 'W2l', 'b2', 'W2r')}
    del _L0_gnn_all

    def _L1_gnn_setup():
        import jax, jax.numpy as jnp
        import numpy as np
        ALPHA = 0.2
        key = jax.random.key(seed)
        ks = jax.random.split(key, 6)
        N, E, F_IN, F_OUT, E_DIM = (50000, 25000, 256, 256, 64)
        h = jax.random.normal(ks[0], (N, F_IN), dtype=jnp.float32)
        e_feat = jax.random.normal(ks[1], (E, E_DIM), dtype=jnp.float32)
        W = jax.random.normal(ks[2], (F_OUT, F_IN), dtype=jnp.float32) * (1.0 / np.sqrt(F_IN))
        A = jax.random.normal(ks[3], (1, 2 * F_OUT + E_DIM), dtype=jnp.float32) * 0.05
        src = jax.random.randint(ks[4], (E,), 0, N, dtype=jnp.int32)
        dst = jax.random.randint(ks[5], (E,), 0, N, dtype=jnp.int32)
        return {'h': h, 'e_feat': e_feat, 'W': W, 'A': A, 'src': src, 'dst': dst}
    _L1_gnn_all = _L1_gnn_setup()
    _L1_gnn_in = {k: v for k, v in _L1_gnn_all.items() if k in ('W', 'A')}
    del _L1_gnn_all
    return {'x': x, 'src': src, 'dst': dst, 'edge_attr_64': edge_attr_64, 'L0_gnn_W1l': _L0_gnn_in['W1l'], 'L0_gnn_b1': _L0_gnn_in['b1'], 'L0_gnn_W1r': _L0_gnn_in['W1r'], 'L0_gnn_W2l': _L0_gnn_in['W2l'], 'L0_gnn_b2': _L0_gnn_in['b2'], 'L0_gnn_W2r': _L0_gnn_in['W2r'], 'L1_gnn_W': _L1_gnn_in['W'], 'L1_gnn_A': _L1_gnn_in['A']}

def reference(x, src, dst, edge_attr_64, L0_gnn_W1l, L0_gnn_b1, L0_gnn_W1r, L0_gnn_W2l, L0_gnn_b2, L0_gnn_W2r, L1_gnn_W, L1_gnn_A):
    import jax
    import jax.numpy as jnp

    def _L0_gnn_ref(x, edge_index, W1l, b1, W1r, W2l, b2, W2r):
        import jax, jax.numpy as jnp
        import numpy as np
        N_NODES = 50000
        N_EDGES = 25000
        IN_FEATS = 256
        HIDDEN = 256

        def _sage_conv(x, src, dst, Wl, bl, Wr):
            msg = x[src]
            agg = jax.ops.segment_sum(msg, dst, num_segments=N_NODES)
            cnt = jax.ops.segment_sum(jnp.ones((src.shape[0],), dtype=x.dtype), dst, num_segments=N_NODES)
            mean = agg / jnp.maximum(cnt, 1.0)[:, None]
            return mean @ Wl.T + bl + x @ Wr.T
        src, dst = (edge_index[0], edge_index[1])
        h = jax.nn.relu(_sage_conv(x, src, dst, W1l, b1, W1r))
        out = _sage_conv(h, src, dst, W2l, b2, W2r)
        return out

    def _L1_gnn_ref(h, e_feat, W, A, src, dst):
        import jax, jax.numpy as jnp
        import numpy as np
        ALPHA = 0.2
        N = h.shape[0]
        F_OUT = W.shape[0]
        z = h @ W.T
        z_src = z[src]
        z_dst = z[dst]
        a_src, a_dst, a_e = (A[0, :F_OUT], A[0, F_OUT:2 * F_OUT], A[0, 2 * F_OUT:])
        logits = z_src @ a_src + z_dst @ a_dst + e_feat @ a_e
        e = jax.nn.leaky_relu(logits, ALPHA)
        m = jax.ops.segment_max(e, dst, num_segments=N)
        ex = jnp.exp(e - m[dst])
        denom = jax.ops.segment_sum(ex, dst, num_segments=N)
        alpha = ex / denom[dst]
        h_out = jax.ops.segment_sum(alpha[:, None] * z_src, dst, num_segments=N)
        return h_out
    edge_index = jnp.stack([src, dst])
    h = jnp.maximum(_layernorm(x, axis=-1), 0.0)
    x = x + _L0_gnn_ref(h, edge_index, L0_gnn_W1l, L0_gnn_b1, L0_gnn_W1r, L0_gnn_W2l, L0_gnn_b2, L0_gnn_W2r)
    h = jnp.maximum(_layernorm(x, axis=-1), 0.0)
    x = x + _L1_gnn_ref(h, edge_attr_64, L1_gnn_W, L1_gnn_A, src, dst)
    return x

_drawn_inputs = setup_inputs


def setup_inputs(seed=0):
    import zlib

    import numpy as np

    out = dict(_drawn_inputs(seed))
    spreads = {}
    factors = {'L0_gnn_b1': 3.333}
    for name, (base, spread) in spreads.items():
        noise = np.random.default_rng([zlib.crc32(name.encode()), seed]).standard_normal(out[name].shape)
        drawn = base * np.exp(spread * noise) if base else spread * noise
        out[name] = jnp.asarray(drawn.astype(out[name].dtype))
    for name, factor in factors.items():
        out[name] = (out[name] * factor).astype(out[name].dtype)
    return out
```

```python
from contextlib import ExitStack

import numpy as np

import concourse.bass as bass
from concourse import mybir

F32 = mybir.dt.float32
BF16 = mybir.dt.bfloat16
I32 = mybir.dt.int32
ALU = mybir.AluOpType
ACT = mybir.ActivationFunctionType
AX_X = mybir.AxisListType.X

P = 128
U = 3
LN_G = 5
WIN = 256
CH = 64
KCH = WIN // CH
SLOTS = WIN // P
TG = 100
GR = 4
PAD_DST = 52000
SKIP = 1.0e6
BIG = 1.0e30
EPS = 1e-5
ALPHA = 0.2
LQ = 17


class Step:

    def __init__(self, i, j, n, u):
        self.i, self.j, self.n, self.u = i, j, n, u
        self.t = i * u + j

    def at(self, d):
        return Step(self.i + (self.j + d) // self.u, (self.j + d) % self.u, self.n, self.u)

    @property
    def real(self):
        return not isinstance(self.t, int) or 0 <= self.t < self.n

    @property
    def reuse(self):
        return not isinstance(self.t, int) or self.t >= self.u


def drive(eng, n, u, body, lead=1, flush=2):
    m = (n - 1 - u) // u
    for t in range(-lead, 2 * u):
        body(Step(t // u, t % u, n, u))
    with eng.Fori(2, m) as i:
        for j in range(u):
            body(Step(i, j, n, u))
    for t in range(u * m, n + flush):
        body(Step(t // u, t % u, n, u))


def uses(n, u, j):
    return (n - j + u - 1) // u


def gnn_program(nc, x, src, dst, edge_attr, W1l, b1, W1r, W2l, b2, W2r, W, A, out):
    N, D = x.shape
    E = src.shape[0]
    ED = edge_attr.shape[1]
    H = D // P
    NT = (N + P - 1) // P
    TAIL = N - (NT - 1) * P
    NP = NT * P
    EC = (E + P - 1) // P
    ETAIL = E - (EC - 1) * P
    EB = 4
    SR = TG * GR * 2
    LB = (NT - 1) // LN_G
    assert H == 2 and NT <= TG * GR and EC <= EB * P and (NT - 1) % LN_G == 0
    assert SR * CH > E + WIN and EC % LQ == 0 and PAD_DST >= TG * GR * P

    ctx = ExitStack()
    with ctx:
        def sb(name, shape, dt=F32):
            return ctx.enter_context(nc.sbuf_tensor(name, shape, dt))

        def sem(name):
            return ctx.enter_context(nc.semaphore(name))

        def dram(name, shape, dt=F32):
            return nc.dram_tensor(name, shape, dt, kind="Internal")

        rows_tab = [dram(f"rows_tab{k}", (NP, D)) for k in range(3)]
        sums_tab = [dram(f"sums_tab{k}", (NP, D)) for k in range(3)]
        x1_tab = dram("x1_tab", (NP, D))
        src_pad = dram("src_pad", (SR, CH), I32)
        dst_pad = dram("dst_pad", (SR, CH), I32)
        logit_tab = dram("logit_tab", (EB * P * P // CH, CH))
        score_src = dram("score_src", (EB * P * P, 1))
        score_dst = dram("score_dst", (EB * P * P, 1))
        maxden = dram("maxden", (NP, 2))

        ident = sb("ident", [P, P])
        lower = sb("lower", [P, P])
        iota_i = sb("iota_i", [P, P], I32)
        iota_n = sb("iota_n", [P, P])
        part_i = sb("part_i", [P, 1], I32)
        part_n = sb("part_n", [P, 1])
        tile0_i = sb("tile0_i", [TG, GR], I32)
        tile0 = sb("tile0", [TG, GR])
        zeros = sb("zeros", [P, D])
        ones = sb("ones", [P, P])
        ones_b = sb("ones_b", [P, P], BF16)
        eps = sb("eps", [P, 1])
        PADS = SR * CH - E
        pad_i = sb("pad_i", [16, PADS // 16], I32)
        pad_z = sb("pad_z", [16, PADS // 16], I32)

        mats = [W1l, W1r, W2l, W2r, W]
        w_nat = sb("w_nat", [P, 5, H, D])
        w_T = sb("w_T", [P, 5, H, D])
        bias_full = sb("bias_full", [P, 2, D])
        bias_rest = sb("bias_rest", [P, 2, D])
        bias_part = sb("bias_part", [P, 3, 2, D], BF16)
        bias_rows = sb("bias_rows", [P, 2, D], BF16)
        a_col = sb("a_col", [P, 2 * H])
        a_wide = sb("a_wide", [P, 2 * H, P])
        a_edge = sb("a_edge", [P, ED])
        v_rows = sb("v_rows", [P, 2, D])

        src_rows = sb("src_rows", [P, EB, P], I32)
        dst_rows = sb("dst_rows", [P, EB, P], I32)
        edge_f = sb("edge_f", [P, 2, EB, P])
        src_c = sb("src_c", [P, EB * P], I32)
        dst_c = sb("dst_c", [P, EB * P], I32)
        dst_f = sb("dst_f", [P, EB * P])
        logit_c = sb("logit_c", [P, EB * P])
        logit_r = sb("logit_r", [P, EB, P])

        firsts_i = sb("firsts_i", [1, SR], I32)
        firsts = sb("firsts", [1, SR])
        below = sb("below", [TG, SR])
        start = sb("start", [TG, GR])
        chunk_f = sb("chunk_f", [TG, GR, KCH])
        chunk = sb("chunk", [TG, GR, KCH], I32)
        src_w = sb("src_w", [TG, GR, WIN], I32)
        dst_w = sb("dst_w", [TG, GR, WIN], I32)
        srcf_w = sb("srcf_w", [TG, GR, WIN])
        dstf_w = sb("dstf_w", [TG, GR, WIN])
        loc_w = sb("loc_w", [TG, GR, WIN])
        valid_w = sb("valid_w", [TG, GR, WIN])
        same_w = sb("same_w", [TG, GR, WIN])
        next_w = sb("next_w", [TG, GR, WIN])
        run_a = sb("run_a", [TG, GR, WIN])
        run_b = sb("run_b", [TG, GR, WIN])
        rst_a, rst_b, logit_w = loc_w, dstf_w, srcf_w
        weight_w = sb("weight_w", [TG, GR, WIN])
        tally = sb("tally", [TG, 2])
        tally1 = sb("tally1", [1, 2])
        general_i = sb("general_i", [1, 1], I32)

        idx_c = sb("idx_c", [P, SLOTS, TG * GR], I32)
        idx_cf = sb("idx_cf", [P, SLOTS, TG * GR])
        loc_c = sb("loc_c", [P, SLOTS, TG * GR])
        wgt_c = sb("wgt_c", [P, SLOTS, TG * GR])

        ln_x = sb("ln_x", [P, U, LN_G, D])
        ln_h = sb("ln_h", [P, U, LN_G, D])
        ln_st = sb("ln_st", [P, U, LN_G, 6])
        ln_mv = sb("ln_mv", [P, U, LN_G, 2])
        ln_sd = sb("ln_sd", [P, U, LN_G])
        ln_rs = sb("ln_rs", [P, U, LN_G])
        ln_nm = sb("ln_nm", [P, U, LN_G])

        idx_t = sb("idx_t", [P, U, SLOTS], I32)
        own = sb("own", [P, U, D])
        res = sb("res", [P, U, D])
        rows = sb("rows", [P, U, SLOTS, D])
        sel = sb("sel", [P, U, SLOTS, P])
        oper = sb("oper", [P, U, 2 * D])
        h_out = sb("h_out", [P, U, D])
        x_out = sb("x_out", [P, U, D])
        t_st = sb("t_st", [P, U, 6])
        t_mv = sb("t_mv", [P, U, 2])
        t_sd = sb("t_sd", [P, U])
        t_rs = sb("t_rs", [P, U])
        t_nm = sb("t_nm", [P, U])
        prod = sb("prod", [P, 2, D])
        t_sc = sb("t_sc", [P, U, 2])
        score_c = sb("score_c", [P, 2, EB * P])
        score_r = edge_f

        idx_l = sb("idx_l", [P, 2, 2, LQ], I32)
        got_l = sb("got_l", [P, 2, 2, LQ])
        ea = sb("ea", [P, 2, LQ, ED])
        ea_p = sb("ea_p", [P, LQ, ED])
        ea_r = sb("ea_r", [P, LQ])

        g_idx = sb("g_idx", [P, 2], I32)
        g_msg = sb("g_msg", [P, D])
        g_acc = sb("g_acc", [P, D])
        g_md = sb("g_md", [P, 2])
        g_new = sb("g_new", [P, D])
        g_mdn = sb("g_mdn", [P, 2])
        g_dst = sb("g_dst", [P, 2])
        g_wide = sb("g_wide", [P, 2, P])
        g_eq = sb("g_eq", [P, P])
        g_t1 = sb("g_t1", [P, P])
        g_t2 = sb("g_t2", [P, P])
        g_wt = sb("g_wt", [P, P])
        g_mx = sb("g_mx", [P, 1])
        g_df = sb("g_df", [P, 2])
        g_ex = sb("g_ex", [P, 2])
        g_rk = sb("g_rk", [P, 1])
        g_to_f = sb("g_to_f", [P, 1])
        g_to = sb("g_to", [P, 1], I32)
        g_init = sb("g_init", [P, 2])
        g_all = sb("g_all", [P, NT, 2])

        psA = [ctx.enter_context(nc.psum_tensor(f"psA{j}", [P, 512], F32)) for j in range(U)]
        psB = [ctx.enter_context(nc.psum_tensor(f"psB{j}", [P, 512], F32)) for j in range(U)]
        psX = ctx.enter_context(nc.psum_tensor("psX", [P, 512], F32))
        psY = ctx.enter_context(nc.psum_tensor("psY", [P, 512], F32))
        banks = [psA[0], psA[1], psA[2], psB[0], psB[1]]

        s_const = sem("s_const")
        s_w = sem("s_w")
        s_edges = sem("s_edges")
        s_edges_f = sem("s_edges_f")
        s_pads = sem("s_pads")
        s_firsts = sem("s_firsts")
        s_firsts_f = sem("s_firsts_f")
        s_fbc = sem("s_fbc")
        s_chunk = sem("s_chunk")
        s_win = sem("s_win")
        s_tp = sem("s_tp")
        s_dv = sem("s_dv")
        s_mk = sem("s_mk")
        s_flag = sem("s_flag")
        s_turn = sem("s_turn")
        s_pl = sem("s_pl")
        ln_ld = [sem(f"ln_ld{j}") for j in range(U)]
        ln_stored = [sem(f"ln_stored{j}") for j in range(U)]
        ln_stats = sem("ln_stats")
        ln_aggr = sem("ln_aggr")
        ln_std = sem("ln_std")
        ln_scale = sem("ln_scale")
        ln_rcp = sem("ln_rcp")
        ln_done = sem("ln_done")

        dve_n = [0]

        def link(eng, ins, s=s_dv, count=dve_n):
            count[0] += 1
            ins.then_inc(s, 1)
            eng.wait_ge(s, count[0])

        class Layer:

            def __init__(self, k):
                self.k = k
                self.idx = sem(f"idx_copied{k}")
                self.own_ld = [sem(f"own_ld{k}_{j}") for j in range(U)]
                self.res_ld = [sem(f"res_ld{k}_{j}") for j in range(U)]
                self.rows_ld = [sem(f"rows_ld{k}_{j}") for j in range(U)]
                self.h_st = [sem(f"h_st{k}_{j}") for j in range(U)]
                self.x_st = [sem(f"x_st{k}_{j}") for j in range(U)]
                self.sel = sem(f"sel_made{k}")
                self.transposed = sem(f"own_transposed{k}")
                self.aggregated = sem(f"aggregated{k}")
                self.oper = sem(f"operands_copied{k}")
                self.dense = sem(f"dense{k}")
                self.h = sem(f"h_made{k}")
                self.x = sem(f"x_made{k}")
                self.ready = sem(f"windows_ready{k}")

        L = [Layer(k) for k in range(3)]
        ln2_stats = sem("ln2_stats")
        ln2_aggr = sem("ln2_aggr")
        ln2_std = sem("ln2_std")
        ln2_rcp = sem("ln2_rcp")
        ln2_scale = sem("ln2_scale")
        sc_prod = sem("sc_prod")
        sc_made = sem("sc_made")
        sc_kept = sem("sc_kept")
        s_score = sem("s_score")
        s_score_v = sem("s_score_v")
        s_score_st = sem("s_score_st")
        l_idx = sem("l_idx")
        l_got = [sem(f"l_got{j}") for j in range(2)]
        l_ea = [sem(f"l_ea{j}") for j in range(2)]
        l_dv = sem("l_dv")
        s_lt = sem("s_lt")
        s_lr = sem("s_lr")
        s_lst = sem("s_lst")
        s_lw = sem("s_lw")
        s_ex = sem("s_ex")

        def table_written(eng, k):
            if k == 0:
                for j in range(U):
                    eng.wait_ge(ln_stored[j], 16 * uses(LB + 1, U, j) + 16 * (j == 0))
            else:
                for j in range(U):
                    eng.wait_ge(L[k - 1].h_st[j], 16 * uses(NT, U, j))

        class General:
            def __init__(self, k):
                self.init = sem(f"g_init{k}")
                self.iv = sem(f"g_iv{k}")
                self.pool = sem(f"g_pool{k}")
                self.got = sem(f"g_got{k}")
                self.put = sem(f"g_put{k}")
                self.dve = sem(f"g_dve{k}")
                self.pe = sem(f"g_pe{k}")
                self.act = sem(f"g_act{k}")
                self.den = sem(f"g_den{k}")
                self.fin = sem(f"g_fin{k}")

        GEN = [General(k) for k in range(3)]
        GDV = 17

        def general_sync(sp, k):
            g = GEN[k]
            sp.wait_ge(g.iv, 1)
            sp.dma_start(sums_tab[k][:, :].rearrange("(t p) d -> p t d", p=P),
                         zeros[:, :].unsqueeze(1).to_broadcast([P, NT, D])).then_inc(g.init, 16)
            sp.dma_start(maxden[:, :].rearrange("(t p) d -> p t d", p=P),
                         g_init[:, :].unsqueeze(1).to_broadcast([P, NT, 2]),
                         allow_slow_non_contiguous=True).then_inc(g.init, 16)
            sp.wait_ge(g.put, 32 * EC)
            sp.dma_start(g_all[:, :, :], maxden[:, :].rearrange("(t p) d -> p t d", p=P),
                         allow_slow_non_contiguous=True).then_inc(g.den, 16)

        def general_pool(pool, k):
            g = GEN[k]
            pool.wait_ge(g.init, 32)
            last_row = pool.to_reg(NP - 1)
            with pool.Fori(0, EC) as c:
                nc.gpsimd.tensor_copy(g_idx[:, 0:1], src_c[:, bass.ds(c, 1)])
                nc.gpsimd.tensor_copy(g_idx[:, 1:2], dst_c[:, bass.ds(c, 1)]).then_inc(g.pool, 1)
                pool.wait_ge(g.pool, c + 1)
                pool.sem_inc(s_turn, 1)
                for buf, tab, n in ((g_msg, rows_tab[k], 0), (g_md, maxden, 1), (g_acc, sums_tab[k], 1)):
                    nc.gpsimd.indirect_dma_start(
                        out=buf[:, :], out_offset=None, in_=tab[:, :],
                        in_offset=bass.IndirectOffsetOnAxis(ap=g_idx[:, n:n + 1], axis=0),
                        bounds_check=last_row, oob_is_err=False).then_inc(g.got, 16)
                pool.wait_ge(g.dve, GDV * (c + 1))
                pool.sem_inc(s_turn, 1)
                for buf, tab in ((g_mdn, maxden), (g_new, sums_tab[k])):
                    nc.gpsimd.indirect_dma_start(
                        out=tab[:, :], out_offset=bass.IndirectOffsetOnAxis(ap=g_to[:, 0:1], axis=0),
                        in_=buf[:, :], in_offset=None,
                        bounds_check=last_row, oob_is_err=False).then_inc(g.put, 16)
                pool.wait_ge(g.put, 32 * (c + 1))
            pool.wait_ge(g.put, 32 * EC)
            nc.gpsimd.memset(idx_c[:, :, :], SKIP)
            nc.gpsimd.memset(loc_c[:, :, :], -1.0).then_inc(g.pool, 1)
            pool.wait_ge(g.pool, EC + 1)
            nc.gpsimd.iota(idx_c[:, 0, 0:NT], pattern=[[P, NT]], base=0,
                           channel_multiplier=1).then_inc(g.fin, 1)

        def general_tensor(pe, k):
            g = GEN[k]
            with pe.Fori(0, EC) as c:
                pe.wait_ge(g.dve, GDV * c + 2)
                nc.tensor.transpose(psX[:, 0:P], g_wide[:, 0, :], ident[:, :])
                nc.tensor.transpose(psX[:, P:2 * P], g_wide[:, 1, :], ident[:, :]).then_inc(g.pe, 1)
                pe.wait_ge(g.dve, GDV * c + 11)
                pe.wait_ge(g.got, 48 * (c + 1))
                nc.tensor.matmul(psY[:, 0:D], g_wt[:, :], g_msg[:, :], start=True, stop=True)
                nc.tensor.matmul(psY[:, D:D + 1], g_wt[:, :], ones[:, 0:1], start=True,
                                 stop=True).then_inc(g.pe, 1)

        def general_scalar(act, k):
            g = GEN[k]
            with act.Fori(0, EC) as c:
                act.wait_ge(g.dve, GDV * c + 10)
                nc.scalar.activation(g_ex[:, :], g_df[:, :], ACT.Exp).then_inc(g.act, 1)

        def general_vector(dve, k):
            g = GEN[k]
            nc.vector.memset(g_init[:, 0:1], -BIG)
            nc.vector.memset(g_init[:, 1:2], 0.0).then_inc(g.iv, 1)
            nc.vector.memset(g_msg[:, :], 0.0)
            nc.vector.memset(g_acc[:, :], 0.0)
            nc.vector.memset(g_md[:, :], 0.0)
            if k < 2:
                nc.vector.memset(logit_c[:, :], 0.0)
            nc.vector.drain().then_inc(g.iv, 1)
            dve.wait_ge(g.iv, 2)
            with dve.Fori(0, EC) as c:
                n = [0]

                def step(ins, wait=True):
                    n[0] += 1
                    ins.then_inc(g.dve, 1)
                    if wait:
                        dve.wait_ge(g.dve, GDV * c + n[0])

                step(nc.vector.tensor_scalar(g_wide[:, 0, :], dst_f[:, bass.ds(c, 1)].to_broadcast([P, P]), 0.0,
                                             None, ALU.add), False)
                step(nc.vector.tensor_copy(g_wide[:, 1, :], logit_c[:, bass.ds(c, 1)].to_broadcast([P, P])), False)
                step(nc.vector.tensor_copy(g_dst[:, 0:1], dst_f[:, bass.ds(c, 1)]), False)
                step(nc.vector.tensor_copy(g_dst[:, 1:2], logit_c[:, bass.ds(c, 1)]))
                dve.wait_ge(g.pe, 2 * c + 1)
                step(nc.vector.tensor_scalar(g_eq[:, :], psX[:, 0:P], g_dst[:, 0:1], None, ALU.is_equal))
                nc.vector.tensor_scalar(g_t1[:, :], g_eq[:, :], -1.0, BIG, ALU.add, ALU.mult)
                step(nc.vector.tensor_tensor(g_t2[:, :], g_eq[:, :], psX[:, P:2 * P], ALU.mult))
                step(nc.vector.tensor_tensor(g_t1[:, :], g_t1[:, :], g_t2[:, :], ALU.add))
                step(nc.vector.tensor_reduce(g_mx[:, :], g_t1[:, :], AX_X, ALU.max))
                dve.wait_ge(g.got, 48 * (c + 1))
                step(nc.vector.tensor_tensor(g_mdn[:, 0:1], g_mx[:, :], g_md[:, 0:1], ALU.max))
                nc.vector.tensor_tensor(g_df[:, 0:1], g_dst[:, 1:2], g_mdn[:, 0:1], ALU.subtract)
                step(nc.vector.tensor_tensor(g_df[:, 1:2], g_md[:, 0:1], g_mdn[:, 0:1], ALU.subtract))
                dve.wait_ge(g.act, c + 1)
                step(nc.vector.tensor_scalar(g_wt[:, :], g_eq[:, :], g_ex[:, 0:1], None, ALU.mult))
                step(nc.vector.tensor_tensor(g_t2[:, :], g_eq[:, :], lower[:, :], ALU.mult))
                step(nc.vector.tensor_reduce(g_rk[:, :], g_t2[:, :], AX_X, ALU.max))
                step(nc.vector.scalar_tensor_tensor(g_to_f[:, 0:1], g_rk[:, :], SKIP, g_dst[:, 0:1],
                                                    ALU.mult, ALU.add))
                step(nc.vector.tensor_copy(g_to[:, 0:1], g_to_f[:, 0:1]))
                dve.wait_ge(g.pe, 2 * c + 2)
                step(nc.vector.scalar_tensor_tensor(g_new[:, :], g_acc[:, :], g_ex[:, 1:2], psY[:, 0:D],
                                                    ALU.mult, ALU.add))
                step(nc.vector.scalar_tensor_tensor(g_mdn[:, 1:2], g_md[:, 1:2], g_ex[:, 1:2],
                                                    psY[:, D:D + 1], ALU.mult, ALU.add), False)
                assert n[0] == GDV
                dve.wait_ge(g.put, 32 * (c + 1))
            dve.wait_ge(g.den, 16)
            dve.wait_ge(g.fin, 1)
            nc.vector.tensor_scalar(g_all[:, :, 1], g_all[:, :, 1], 0.5, None, ALU.max).then_inc(g.fin, 1)
            dve.wait_ge(g.fin, 2)
            nc.vector.reciprocal(wgt_c[:, 0, 0:NT], g_all[:, :, 1])
            nc.vector.tensor_copy(loc_c[:, 0, 0:NT], part_n[:, 0:1].to_broadcast([P, NT])).then_inc(g.fin, 1)
            dve.wait_ge(g.fin, 3)

        def is_general(eng):
            eng.wait_ge(s_flag, 1)
            return eng.value_load(general_i[0:1, 0:1], min_val=0, max_val=1) != 0

        def layer_sync(sp, k):
            y = L[k]

            def load(T):
                if not T.real:
                    return
                if k < 2:
                    if T.reuse:
                        sp.wait_ge(y.transposed, T.t - U + 1)
                    sp.dma_start(own[:, T.j, :], rows_tab[k][bass.ds(T.t * P, P), :]).then_inc(y.own_ld[T.j], 16)
                if k > 0:
                    if T.reuse:
                        sp.wait_ge(y.x, T.t - U + 1)
                    last = isinstance(T.t, int) and T.t == NT - 1
                    n = TAIL if last and k == 1 else P
                    tab = x if k == 1 else x1_tab
                    sp.dma_start(res[0:n, T.j, :], tab[bass.ds(T.t * P, n), :]).then_inc(y.res_ld[T.j], 16)

            def store_h(T):
                sp.wait_ge(y.h, T.t + 1)
                sp.dma_start(rows_tab[k + 1][bass.ds(T.t * P, P), :], h_out[:, T.j, :]).then_inc(y.h_st[T.j], 16)

            def store_x(T):
                last = isinstance(T.t, int) and T.t == NT - 1
                n = TAIL if last and k == 2 else P
                tab = x1_tab if k == 1 else out
                sp.wait_ge(y.x, T.t + 1)
                sp.dma_start(tab[bass.ds(T.t * P, n), :], x_out[0:n, T.j, :]).then_inc(y.x_st[T.j], 16)

            def body(T):
                if T.real and k > 0:
                    store_x(T)
                load(T.at(U))
                if T.real and k == 0:
                    store_h(T)
                if k == 1 and T.at(-1).real:
                    store_h(T.at(-1))

            table_written(sp, k)
            if k == 2:
                for j in range(U):
                    sp.wait_ge(L[1].x_st[j], 16 * uses(NT, U, j))
            for t in range(U):
                load(Step(0, t, NT, U))
            drive(sp, NT, U, body, lead=0, flush=1)

        def layer_pool(pool, k, tab):
            y = L[k]
            last_row = pool.to_reg(NP - 1)

            def body(T):
                if not T.real:
                    return
                if T.reuse:
                    pool.wait_ge(y.aggregated, T.t - U + 1)
                    pool.sem_inc(s_turn, 1)
                nc.gpsimd.tensor_copy(idx_t[:, T.j, :], idx_c[:, :, bass.ds(T.t, 1)].rearrange("p s o -> p (s o)"))\
                    .then_inc(y.idx, 1)
                pool.wait_ge(y.idx, T.t + 1)
                pool.sem_inc(s_turn, 1)
                for s in range(SLOTS):
                    nc.gpsimd.indirect_dma_start(
                        out=rows[:, T.j, s, :], out_offset=None, in_=tab[:, :],
                        in_offset=bass.IndirectOffsetOnAxis(ap=idx_t[:, T.j, s:s + 1], axis=0),
                        bounds_check=last_row, oob_is_err=False).then_inc(y.rows_ld[T.j], 16)

            pool.wait_ge(y.ready, 1)
            drive(pool, NT, U, body, lead=0, flush=0)

        def layer_tensor(pe, k):
            y = L[k]
            left, right = ((0, 1), (2, 3), (4, None))[k]

            def first(T):
                if k < 2:
                    pe.wait_ge(y.own_ld[T.j], 16 * (T.i + 1))
                    for f in range(H):
                        last = nc.tensor.transpose(psA[T.j][:, D + f * P:D + (f + 1) * P],
                                                   own[:, T.j, f * P:(f + 1) * P], ident[:, :])
                    last.then_inc(y.transposed, 1)
                pe.wait_ge(y.rows_ld[T.j], 32 * (T.i + 1))
                pe.wait_ge(y.sel, T.t + 1)
                for f in range(H):
                    for s in range(SLOTS):
                        last = nc.tensor.matmul(psA[T.j][:, f * P:(f + 1) * P],
                                                rows[:, T.j, s, f * P:(f + 1) * P], sel[:, T.j, s, :],
                                                start=(s == 0), stop=(s == SLOTS - 1))
                last.then_inc(y.aggregated, 1)

            def second(T):
                if T.reuse:
                    pe.wait_ge(y.x if k else y.h, T.t - U + 1)
                pe.wait_ge(y.oper, T.t + 1)
                if k < 2:
                    nc.tensor.matmul(psB[T.j][:, 0:D], ones_b[:, :], bias_rows[:, k, :], start=True, stop=False)
                    for f in range(H):
                        nc.tensor.matmul(psB[T.j][:, 0:D], oper[:, T.j, D + f * P:D + (f + 1) * P],
                                         w_T[:, right, f, :], start=False, stop=False)
                for f in range(H):
                    last = nc.tensor.matmul(psB[T.j][:, 0:D], oper[:, T.j, f * P:(f + 1) * P], w_T[:, left, f, :],
                                            start=(k == 2 and f == 0), stop=(f == H - 1))
                last.then_inc(y.dense, 1)

            def body(T):
                if T.at(1).real:
                    first(T.at(1))
                if T.real:
                    second(T)

            if k:
                pe.wait_ge(L[k - 1].x if k == 2 else L[k - 1].h, NT)
            drive(pe, NT, U, body, lead=1, flush=0)

        def layer_scalar(act, k):
            y = L[k]

            def body(T):
                N1 = T.at(1)
                if N1.real:
                    act.wait_ge(y.aggregated, N1.t + 1)
                    if N1.reuse:
                        act.wait_ge(y.dense, N1.t - U + 1)
                    n = 2 * D if k < 2 else D
                    nc.scalar.activation(oper[:, N1.j, 0:n], psA[N1.j][:, 0:n], ACT.Copy).then_inc(y.oper, 1)
                if k == 1 and T.real:
                    act.wait_ge(ln2_aggr, T.t + 1)
                    nc.scalar.activation(t_sd[:, T.j:T.j + 1], t_mv[:, T.j, 1:2], ACT.Sqrt,
                                         bias=eps[:, 0:1]).then_inc(ln2_std, 1)
                B1 = T.at(-1)
                if k == 1 and B1.real:
                    act.wait_ge(ln2_scale, B1.t + 1)
                    if B1.reuse:
                        act.wait_ge(y.h_st[B1.j], 16 * B1.i)
                        act.wait_ge(sc_made, B1.t - U + 1)
                    nc.scalar.activation(h_out[:, B1.j, :], x_out[:, B1.j, :], ACT.Relu,
                                         bias=t_nm[:, B1.j:B1.j + 1],
                                         scale=t_rs[:, B1.j:B1.j + 1]).then_inc(y.h, 1)

            if k:
                act.wait_ge(L[k - 1].dense, NT)
            if k == 1:
                table_written(act, 1)
            drive(act, NT, U, body, lead=1, flush=1)

        def layer_vector(dve, k):
            y = L[k]

            def select(T):
                if T.reuse:
                    dve.wait_ge(y.aggregated, T.t - U + 1)
                for s in range(SLOTS):
                    last = nc.vector.tensor_scalar(sel[:, T.j, s, :], iota_n[:, :], loc_c[:, s, bass.ds(T.t, 1)],
                                                   wgt_c[:, s, bass.ds(T.t, 1)], ALU.is_equal, ALU.mult)
                last.then_inc(y.sel, 1)

            def relu(T):
                dve.wait_ge(y.dense, T.t + 1)
                if T.reuse:
                    dve.wait_ge(y.h_st[T.j], 16 * T.i)
                nc.vector.tensor_scalar(h_out[:, T.j, :], psB[T.j][:, 0:D], 0.0, None, ALU.max).then_inc(y.h, 1)

            def add_residual(T):
                dve.wait_ge(y.dense, T.t + 1)
                dve.wait_ge(y.res_ld[T.j], 16 * (T.i + 1))
                if T.reuse:
                    dve.wait_ge(y.x_st[T.j], 16 * T.i)
                    if k == 1:
                        dve.wait_ge(y.h, T.t - U + 1)
                nc.vector.tensor_tensor(x_out[:, T.j, :], psB[T.j][:, 0:D], res[:, T.j, :], ALU.add).then_inc(y.x, 1)

            def scale(T):
                dve.wait_ge(ln2_std, T.t + 1)
                nc.vector.reciprocal(t_rs[:, T.j:T.j + 1], t_sd[:, T.j:T.j + 1]).then_inc(ln2_rcp, 1)
                dve.wait_ge(ln2_rcp, T.t + 1)
                nc.vector.scalar_tensor_tensor(t_nm[:, T.j:T.j + 1], t_mv[:, T.j, 0:1], -1.0,
                                               t_rs[:, T.j:T.j + 1], ALU.mult, ALU.mult).then_inc(ln2_scale, 1)

            def keep_scores(T):
                dve.wait_ge(sc_made, T.t + 1)
                nc.vector.tensor_scalar(score_c[:, :, bass.ds(T.t, 1)].rearrange("p a o -> p (a o)"),
                                        t_sc[:, T.j, :], 0.0, None, ALU.add)

            def scores(T):
                dve.wait_ge(y.h, T.t + 1)
                for a in range(2):
                    last = nc.vector.tensor_tensor_reduce(out=prod[:, a, :], in0=h_out[:, T.j, :], in1=v_rows[:, a, :],
                                                          scale=1.0, scalar=0.0, op0=ALU.mult, op1=ALU.add,
                                                          accum_out=t_sc[:, T.j, a:a + 1])
                last.then_inc(sc_made, 1)

            def body(T):
                if k == 1 and T.at(-1).real:
                    scale(T.at(-1))
                if T.at(2).real:
                    select(T.at(2))
                if k == 0 and T.real:
                    relu(T)
                if k and T.real:
                    add_residual(T)
                if k == 1 and T.at(-2).real:
                    scores(T.at(-2))
                if k == 1 and T.real:
                    dve.wait_ge(y.x, T.t + 1)
                    nc.vector.bn_stats(t_st[:, T.j, :], x_out[:, T.j, :]).then_inc(ln2_stats, 1)
                    dve.wait_ge(ln2_stats, T.t + 1)
                if k == 1 and T.at(-2).real:
                    keep_scores(T.at(-2))
                if k == 1 and T.real:
                    nc.vector.bn_aggr(t_mv[:, T.j, :], t_st[:, T.j, :]).then_inc(ln2_aggr, 1)

            if k:
                dve.wait_ge(L[k - 1].dense, NT)
            if k == 2:
                for j in range(U):
                    dve.wait_ge(L[1].x_st[j], 16 * uses(NT, U, j))
            drive(dve, NT, U, body, lead=2, flush=2)

        def ln_rows(T):
            last = isinstance(T.t, int) and T.t == LB
            return (1, TAIL) if last else (LN_G, P)

        def ln_slice(tab, T):
            g, n = ln_rows(T)
            return tab[bass.ds(T.t * (LN_G * P), g * n), :].rearrange("(g p) d -> p g d", p=n)

        def ln_sync(sp):
            def load(T):
                if not T.real:
                    return
                g, n = ln_rows(T)
                if T.reuse:
                    sp.wait_ge(ln_done, T.t - U + 1)
                sp.dma_start(ln_x[0:n, T.j, 0:g, :], ln_slice(x, T)).then_inc(ln_ld[T.j], 16)

            def body(T):
                if not T.real:
                    return
                load(T.at(U))
                g, n = ln_rows(T)
                sp.wait_ge(ln_done, T.t + 1)
                sp.dma_start(ln_slice(rows_tab[0], T), ln_h[0:n, T.j, 0:g, :]).then_inc(ln_stored[T.j], 16)

            for t in range(U):
                load(Step(0, t, LB + 1, U))
            sp.wait_ge(s_const, 1)
            sp.dma_start(rows_tab[0][N:NP, :], zeros[0:NP - N, :]).then_inc(ln_stored[0], 16)
            drive(sp, LB + 1, U, body, lead=0, flush=0)

        def ln_vector(dve):
            def body(T):
                if T.real:
                    dve.wait_ge(ln_ld[T.j], 16 * (T.i + 1))
                    g, n = ln_rows(T)
                    for a in range(g):
                        last = nc.vector.bn_stats(ln_st[0:n, T.j, a, :], ln_x[0:n, T.j, a, :])
                    last.then_inc(ln_stats, 1)
                    dve.wait_ge(ln_stats, T.t + 1)
                B = T.at(-1)
                if B.real:
                    g, n = ln_rows(B)
                    dve.wait_ge(ln_std, B.t + 1)
                    if B.reuse:
                        dve.wait_ge(ln_done, B.t - U + 1)
                    nc.vector.reciprocal(ln_rs[0:n, B.j, 0:g], ln_sd[0:n, B.j, 0:g]).then_inc(ln_rcp, 1)
                    dve.wait_ge(ln_rcp, B.t + 1)
                    nc.vector.scalar_tensor_tensor(ln_nm[0:n, B.j, 0:g], ln_mv[0:n, B.j, 0:g, 0], -1.0,
                                                   ln_rs[0:n, B.j, 0:g], ALU.mult, ALU.mult).then_inc(ln_scale, 1)
                if T.real:
                    g, n = ln_rows(T)
                    for a in range(g):
                        last = nc.vector.bn_aggr(ln_mv[0:n, T.j, a, :], ln_st[0:n, T.j, a, :])
                    last.then_inc(ln_aggr, 1)

            drive(dve, LB + 1, U, body, lead=0, flush=1)

        def ln_scalar(act):
            def body(T):
                if T.real:
                    g, n = ln_rows(T)
                    act.wait_ge(ln_aggr, T.t + 1)
                    nc.scalar.activation(ln_sd[0:n, T.j, 0:g], ln_mv[0:n, T.j, 0:g, 1], ACT.Sqrt,
                                         bias=eps[0:n, 0:1]).then_inc(ln_std, 1)
                B = T.at(-1)
                if B.real:
                    g, n = ln_rows(B)
                    act.wait_ge(ln_scale, B.t + 1)
                    if B.reuse:
                        act.wait_ge(ln_stored[B.j], 16 * B.i + 16 * (B.j == 0))
                    for a in range(g):
                        last = nc.scalar.activation(ln_h[0:n, B.j, a, :], ln_x[0:n, B.j, a, :], ACT.Relu,
                                                    bias=ln_nm[0:n, B.j, a:a + 1], scale=ln_rs[0:n, B.j, a:a + 1])
                    last.then_inc(ln_done, 1)

            act.wait_ge(s_const, 1)
            drive(act, LB + 1, U, body, lead=0, flush=1)

        LN = EC // LQ
        LDV = 5

        def logits_sync(sp):
            def load(q, j, last):
                if last:
                    sp.dma_start(ea[:, j, 0:LQ - 1, :],
                                 edge_attr[bass.ds(q * (LQ * P), (LQ - 1) * P), :].rearrange("(c p) d -> p c d", p=P))\
                        .then_inc(l_ea[j], 16)
                    sp.dma_start(ea[0:ETAIL, j, LQ - 1, :], edge_attr[E - ETAIL:E, :]).then_inc(l_ea[j], 16)
                else:
                    sp.dma_start(ea[:, j, :, :],
                                 edge_attr[bass.ds(q * (LQ * P), LQ * P), :].rearrange("(c p) d -> p c d", p=P))\
                        .then_inc(l_ea[j], 16)

            load(0, 0, False)
            load(1, 1, False)
            with sp.Fori(1, LN // 2) as i:
                for j in range(2):
                    sp.wait_ge(l_dv, LDV * (2 * i + j - 1))
                    load(2 * i + j, j, False)
            assert LN % 2
            sp.wait_ge(l_dv, LDV * (LN - 2))
            load(LN - 1, 0, True)

        def logits_pool(pool):
            last_row = pool.to_reg(EB * P * P - 1)

            def step(i, j, q, reuse):
                if reuse:
                    pool.wait_ge(l_dv, LDV * (q - 1))
                    pool.sem_inc(s_turn, 1)
                nc.gpsimd.tensor_copy(idx_l[:, j, 0, :], src_c[:, bass.ds(q * LQ, LQ)])
                nc.gpsimd.tensor_copy(idx_l[:, j, 1, :], dst_c[:, bass.ds(q * LQ, LQ)]).then_inc(l_idx, 1)
                pool.wait_ge(l_idx, q + 1)
                pool.sem_inc(s_turn, 1)
                for a, tab in enumerate((score_src, score_dst)):
                    for c in range(LQ):
                        nc.gpsimd.indirect_dma_start(
                            out=got_l[:, j, a, c:c + 1], out_offset=None, in_=tab[:, :],
                            in_offset=bass.IndirectOffsetOnAxis(ap=idx_l[:, j, a, c:c + 1], axis=0),
                            bounds_check=last_row, oob_is_err=False).then_inc(l_got[j], 16)

            pool.wait_ge(s_score_st, 32 * EB)
            step(0, 0, 0, False)
            step(0, 1, 1, False)
            with pool.Fori(1, LN // 2) as i:
                for j in range(2):
                    step(i, j, 2 * i + j, True)
            step(LN // 2, 0, LN - 1, True)

        def logits_vector(dve):
            def step(i, j, q, last):
                n = [0]

                def chain(ins):
                    n[0] += 1
                    ins.then_inc(l_dv, 1)
                    dve.wait_ge(l_dv, LDV * q + n[0])

                dve.wait_ge(l_ea[j], 16 * (i + 1) + (16 if last else 0))
                chain(nc.vector.tensor_tensor(ea_p[:, :, :], ea[:, j, :, :],
                                              a_edge[:, :].unsqueeze(1).to_broadcast([P, LQ, ED]), ALU.mult))
                chain(nc.vector.tensor_reduce(ea_r[:, :], ea_p[:, :, :], AX_X, ALU.add))
                dve.wait_ge(l_got[j], 2 * LQ * 16 * (i + 1))
                chain(nc.vector.tensor_tensor(got_l[:, j, 0, :], got_l[:, j, 0, :], got_l[:, j, 1, :], ALU.add))
                chain(nc.vector.tensor_tensor(got_l[:, j, 0, :], got_l[:, j, 0, :], ea_r[:, :], ALU.add))
                chain(nc.vector.scalar_tensor_tensor(logit_c[:, bass.ds(q * LQ, LQ)], got_l[:, j, 0, :], ALPHA,
                                                     got_l[:, j, 0, :], ALU.mult, ALU.max))

            with dve.Fori(0, LN // 2) as i:
                for j in range(2):
                    step(i, j, 2 * i + j, False)
            step(LN // 2, 0, LN - 1, True)

        def flat(t):
            return t[:, :, :].rearrange("p g w -> p (g w)")

        def spread(dve, last_of_run, total):
            link(dve, nc.vector.tensor_tensor_scan(flat(total)[:, ::-1], flat(next_w)[:, ::-1],
                                                   flat(last_of_run)[:, ::-1], 0.0, ALU.mult, ALU.max))

        SPLIT = [(g, s) for g in range(GR) for s in range(SLOTS)]

        def to_columns_tensor(pe, source, bank0, bank1):
            for g, s in SPLIT:
                bank = (bank0, bank1)[s]
                last = nc.tensor.transpose(bank[:, g * TG:(g + 1) * TG], source[:, g, s * P:(s + 1) * P],
                                           ident[0:TG, 0:TG])
            last.then_inc(s_tp, 1)

        TP_SRC, TP_DST, TP_W, TP_V, TP_FIRST, TP_IDX, TP_LOC, TP_WGT, TP_TALLY, TP_SOFT = range(1, 11)

        block = ctx.enter_context(nc.Block())

        @block.sync
        def _(sp):
            for n, m in enumerate(mats):
                sp.dma_start(w_nat[:, n, :, :], m.rearrange("(h p) d -> p h d", p=P)).then_inc(s_w, 16)
            sp.wait_ge(s_const, 1)
            for tab, buf in ((src, src_rows), (dst, dst_rows)):
                full = (EC - 1) // P * P
                sp.dma_start(buf[:, 0:full // P, :],
                             tab[0:full * P].rearrange("(b p c) -> p b c", p=P, c=P)).then_inc(s_edges, 16)
                sp.dma_start(buf[0:EC - 1 - full, full // P, :],
                             tab[full * P:(EC - 1) * P].rearrange("(p c) -> p c", c=P)).then_inc(s_edges, 16)
                sp.dma_start(buf[EC - 1 - full:EC - full, full // P, 0:ETAIL],
                             tab[(EC - 1) * P:E].unsqueeze(0)).then_inc(s_edges, 16)
            for tab, pad, fill in ((src, src_pad, pad_z), (dst, dst_pad, pad_i)):
                flat_pad = pad[:, :].rearrange("r c -> (r c)")
                sp.dma_start(flat_pad[0:E].rearrange("(a c) -> a c", a=16),
                             tab[0:E].rearrange("(a c) -> a c", a=16)).then_inc(s_pads, 16)
                sp.dma_start(flat_pad[E:SR * CH].rearrange("(a c) -> a c", a=16), fill[:, :]).then_inc(s_pads, 16)
            for n, b in enumerate((b1, b2)):
                sp.dma_start(bias_full[:, n, :], b.unsqueeze(0).to_broadcast([P, D])).then_inc(s_w, 16)
            sp.dma_start(a_col[:, :], A[0, 0:2 * D].rearrange("(q p) -> p q", p=P),
                         allow_slow_non_contiguous=True).then_inc(s_w, 16)
            sp.dma_start(a_edge[:, :], A[0:1, 2 * D:2 * D + ED].to_broadcast([P, ED])).then_inc(s_w, 16)
            sp.wait_ge(s_pads, 64)
            sp.dma_start(firsts_i[:, :], dst_pad[:, 0:1].rearrange("r o -> o r"),
                         allow_slow_non_contiguous=True).then_inc(s_firsts, 16)
            ln_sync(sp)
            general = is_general(sp)
            for k in range(3):
                if k == 2:
                    sp.wait_ge(s_score_v, 2)
                    for a, tab in enumerate((score_src, score_dst)):
                        for b in range(EB):
                            sp.dma_start(tab[b * P * P:(b + 1) * P * P, :].rearrange("(r c) o -> r (c o)", c=P),
                                         score_r[:, a, b, :]).then_inc(s_score_st, 16)
                    logits_sync(sp)
                    sp.wait_ge(s_lr, 1)
                    sp.dma_start(logit_tab[:, :].rearrange("(b r h) c -> r b (h c)", b=EB, r=P),
                                 logit_r[:, :, :]).then_inc(s_lst, 16)
                table_written(sp, k)
                with sp.If(general):
                    general_sync(sp, k)
                layer_sync(sp, k)
            for j in range(U):
                sp.wait_ge(L[2].x_st[j], 16 * uses(NT, U, j))
            sp.wait_ge(s_lst, 16)

        @block.gpsimd
        def _(pool):
            pool_n = [0]

            def chain(ins):
                link(pool, ins, s_pl, pool_n)

            nc.gpsimd.memset(zeros[:, :], 0.0)
            nc.gpsimd.memset(eps[:, :], EPS)
            nc.gpsimd.memset(pad_i[:, :], PAD_DST)
            nc.gpsimd.memset(pad_z[:, :], 0)
            nc.gpsimd.memset(src_rows[:, :, :], 0)
            chain(nc.gpsimd.memset(dst_rows[:, :, :], PAD_DST))
            nc.gpsimd.memset(ones[:, :], 1.0)
            nc.gpsimd.memset(ones_b[:, :], 1.0)
            nc.gpsimd.iota(iota_i[:, :], pattern=[[1, P]], base=0, channel_multiplier=0)
            nc.gpsimd.iota(part_i[:, :], pattern=[[0, 1]], base=0, channel_multiplier=1)
            nc.gpsimd.iota(tile0_i[:, :], pattern=[[TG * P, GR]], base=0, channel_multiplier=P)
            nc.gpsimd.memset(rows[:, :, :, :], 0.0)
            nc.gpsimd.memset(got_l[:, :, :, :], 0.0)
            nc.gpsimd.memset(ea[:, :, :, :], 0.0)
            nc.gpsimd.memset(logit_c[:, :], 0.0)
            nc.gpsimd.memset(score_c[:, :, :], 0.0)
            nc.gpsimd.memset(bias_rows[:, :, :], 0.0)
            nc.gpsimd.memset(lower[:, :], 1.0)
            chain(nc.gpsimd.memset(ident[:, :], 0.0))
            nc.gpsimd.affine_select(out=ident[:, :], in_=ident[:, :], compare_op=ALU.not_equal, fill=1.0,
                                    base=0, pattern=[[-1, P]], channel_multiplier=1)
            chain(nc.gpsimd.affine_select(out=lower[:, :], in_=lower[:, :], compare_op=ALU.is_gt, fill=0.0,
                                          base=0, pattern=[[-1, P]], channel_multiplier=1))
            pool.sem_inc(s_const, 1)
            pool.wait_ge(s_chunk, 1)
            pool.wait_ge(s_pads, 64)
            last_chunk = pool.to_reg(SR - 1)
            for tab, buf in ((dst_pad, dst_w), (src_pad, src_w)):
                for g in range(GR):
                    for c in range(KCH):
                        nc.gpsimd.indirect_dma_start(
                            out=buf[:, g, c * CH:(c + 1) * CH], out_offset=None, in_=tab[:, :],
                            in_offset=bass.IndirectOffsetOnAxis(ap=chunk[:, g, c:c + 1], axis=0),
                            bounds_check=last_chunk, oob_is_err=False).then_inc(s_win, 16)
            general = is_general(pool)
            for k in range(3):
                if k == 2:
                    logits_pool(pool)
                table_written(pool, k)
                if k == 2:
                    pool.wait_ge(s_lst, 16)
                    for g in range(GR):
                        for c in range(KCH):
                            nc.gpsimd.indirect_dma_start(
                                out=logit_w[:, g, c * CH:(c + 1) * CH], out_offset=None, in_=logit_tab[:, :],
                                in_offset=bass.IndirectOffsetOnAxis(ap=chunk[:, g, c:c + 1], axis=0),
                                bounds_check=last_chunk, oob_is_err=False).then_inc(s_lw, 16)
                with pool.If(general):
                    general_pool(pool, k)
                    layer_pool(pool, k, sums_tab[k])
                with pool.Else():
                    layer_pool(pool, k, rows_tab[k])

        @block.scalar
        def _(act):
            ln_scalar(act)
            general = is_general(act)
            for k in range(3):
                if k == 2:
                    act.wait_ge(s_ex, 1)
                    nc.scalar.activation(flat(run_b), flat(run_a), ACT.Exp).then_inc(s_ex, 1)
                with act.If(general):
                    general_scalar(act, k)
                layer_scalar(act, k)

        @block.tensor
        def _(pe):
            pe.wait_ge(s_const, 1)
            pe.wait_ge(s_edges_f, 1)
            for a in range(2):
                bank = (psX, psY)[a]
                for b in range(EB):
                    last = nc.tensor.transpose(bank[:, b * P:(b + 1) * P], edge_f[:, a, b, :], ident[:, :])
                last.then_inc(s_tp, 1)
            pe.wait_ge(s_w, 16 * 9)
            for n in range(5):
                for ih in range(H):
                    for oh in range(H):
                        last = nc.tensor.transpose(banks[n][:, ih * D + oh * P:ih * D + (oh + 1) * P],
                                                   w_nat[:, n, oh, ih * P:(ih + 1) * P], ident[:, :])
            last.then_inc(s_tp, 1)
            pe.wait_ge(s_mk, 1)
            for a in range(2):
                for oh in range(H):
                    last = nc.tensor.matmul(psB[2][:, a * D:(a + 1) * D], a_wide[:, a * H + oh, :],
                                            w_nat[:, 4, oh, :], start=(oh == 0), stop=(oh == H - 1))
            last.then_inc(s_tp, 1)
            pe.wait_ge(s_firsts_f, 1)
            for c in range(2):
                last = nc.tensor.matmul((psX, psY)[c][0:TG, 0:SR // 2], ones[0:1, 0:TG],
                                        firsts[0:1, c * (SR // 2):(c + 1) * (SR // 2)], start=True, stop=True)
            last.then_inc(s_tp, 1)
            pe.wait_ge(s_mk, 2)
            to_columns_tensor(pe, srcf_w, psA[0], psA[1])
            to_columns_tensor(pe, loc_w, psA[2], psB[0])
            pe.wait_ge(s_mk, 3)
            to_columns_tensor(pe, weight_w, psB[1], psB[2])
            nc.tensor.matmul(psX[0:1, 0:2], ones[0:TG, 0:1], tally[:, :], start=True, stop=True).then_inc(s_tp, 1)
            general = is_general(pe)
            for k in range(3):
                if k == 2:
                    pe.wait_ge(s_score, 1)
                    for a in range(2):
                        for b in range(EB):
                            last = nc.tensor.transpose((psX, psY)[a][:, b * P:(b + 1) * P],
                                                       score_c[:, a, b * P:(b + 1) * P], ident[:, :])
                    last.then_inc(s_score, 1)
                    pe.wait_ge(s_lt, 1)
                    for b in range(EB):
                        last = nc.tensor.transpose(psX[:, b * P:(b + 1) * P], logit_c[:, b * P:(b + 1) * P],
                                                   ident[:, :])
                    last.then_inc(s_lt, 1)
                    pe.wait_ge(s_lr, 1)
                    pe.wait_ge(s_mk, 4)
                    to_columns_tensor(pe, weight_w, psX, psY)
                with pe.If(general):
                    general_tensor(pe, k)
                layer_tensor(pe, k)

        @block.vector
        def _(dve):
            def mark(ins, s):
                ins.then_inc(s, 1)

            dve.wait_ge(s_const, 1)
            dve.wait_ge(s_edges, 16 * 6)
            nc.vector.tensor_copy(edge_f[:, 0, :, :], src_rows[:, :, :])
            nc.vector.tensor_copy(edge_f[:, 1, :, :], dst_rows[:, :, :]).then_inc(s_edges_f, 1)
            nc.vector.tensor_copy(iota_n[:, :], iota_i[:, :])
            nc.vector.tensor_copy(part_n[:, :], part_i[:, :])
            link(dve, nc.vector.tensor_copy(tile0[:, :], tile0_i[:, :]))
            dve.wait_ge(s_w, 16 * 9)
            for q in range(2 * H):
                last = nc.vector.tensor_copy(a_wide[:, q, :], a_col[:, q:q + 1].to_broadcast([P, P]))
            last.then_inc(s_mk, 1)
            dve.wait_ge(s_firsts, 16)
            link(dve, nc.vector.tensor_copy(firsts[:, :], firsts_i[:, :]))
            link(dve, nc.vector.tensor_copy(bias_part[:, 0, :, :], bias_full[:, :, :]))
            link(dve, nc.vector.tensor_tensor(bias_rest[:, :, :], bias_full[:, :, :], bias_part[:, 0, :, :],
                                              ALU.subtract))
            link(dve, nc.vector.tensor_copy(bias_part[:, 1, :, :], bias_rest[:, :, :]))
            link(dve, nc.vector.tensor_tensor(bias_rest[:, :, :], bias_rest[:, :, :], bias_part[:, 1, :, :],
                                              ALU.subtract))
            link(dve, nc.vector.tensor_copy(bias_part[:, 2, :, :], bias_rest[:, :, :]))
            for n in range(3):
                nc.vector.tensor_copy(bias_rows[32 * n:32 * n + 1, :, :], bias_part[32 * n:32 * n + 1, n, :, :])
            dve.wait_ge(s_tp, TP_SRC)
            nc.vector.tensor_copy(src_c[:, :], psX[:, :])
            dve.wait_ge(s_tp, TP_DST)
            nc.vector.tensor_copy(dst_c[:, :], psY[:, :])
            nc.vector.tensor_copy(dst_f[:, :], psY[:, :]).then_inc(s_firsts_f, 1)
            dve.wait_ge(s_tp, TP_W)
            for n in range(5):
                nc.vector.tensor_copy(w_T[:, n, :, :].rearrange("p h d -> p (h d)"), banks[n][:, :])
            dve.wait_ge(s_tp, TP_V)
            nc.vector.tensor_copy(v_rows[:, :, :].rearrange("p a d -> p (a d)"), psB[2][:, :])
            dve.wait_ge(s_tp, TP_FIRST)
            for g in range(GR):
                for c in range(2):
                    half = below[:, c * (SR // 2):(c + 1) * (SR // 2)]
                    link(dve, nc.vector.tensor_scalar(half, (psX, psY)[c][0:TG, 0:SR // 2], tile0[:, g:g + 1],
                                                      None, ALU.is_lt))
                link(dve, nc.vector.tensor_reduce(start[:, g:g + 1], below[:, :], AX_X, ALU.add))
            link(dve, nc.vector.tensor_scalar(start[:, :], start[:, :], -1.0, 0.0, ALU.add, ALU.max))
            for c in range(KCH):
                last = nc.vector.tensor_scalar(chunk_f[:, :, c], start[:, :], float(c), None, ALU.add)
            link(dve, last)
            nc.vector.tensor_copy(chunk[:, :, :], chunk_f[:, :, :]).then_inc(s_chunk, 1)

            ln_vector(dve)

            dve.wait_ge(s_win, 16 * 2 * GR * KCH)
            nc.vector.tensor_copy(flat(srcf_w), flat(src_w))
            link(dve, nc.vector.tensor_copy(flat(dstf_w), flat(dst_w)))
            for g in range(GR):
                last = nc.vector.tensor_scalar(loc_w[:, g, :], dstf_w[:, g, :], tile0[:, g:g + 1], None,
                                               ALU.subtract)
            link(dve, last)
            link(dve, nc.vector.tensor_scalar(flat(run_a), flat(loc_w), 0.0, None, ALU.is_ge))
            link(dve, nc.vector.scalar_tensor_tensor(flat(valid_w), flat(loc_w), float(P), flat(run_a),
                                                     ALU.is_lt, ALU.mult))
            link(dve, nc.vector.tensor_scalar(flat(run_a), flat(valid_w), -SKIP, SKIP, ALU.mult, ALU.add))
            mark(nc.vector.tensor_tensor(flat(srcf_w), flat(srcf_w), flat(run_a), ALU.add), s_mk)
            link(dve, nc.vector.tensor_reduce(tally[:, 0:1], flat(valid_w), AX_X, ALU.add))
            nc.vector.memset(flat(same_w), 0.0)
            link(dve, nc.vector.memset(flat(next_w), 0.0))
            link(dve, nc.vector.tensor_tensor(same_w[:, :, 1:WIN], dstf_w[:, :, 1:WIN], dstf_w[:, :, 0:WIN - 1],
                                              ALU.is_equal))
            link(dve, nc.vector.tensor_copy(next_w[:, :, 0:WIN - 1], same_w[:, :, 1:WIN]))
            link(dve, nc.vector.memset(flat(run_b), 0.0))
            link(dve, nc.vector.tensor_tensor(run_b[:, :, 1:WIN], dstf_w[:, :, 0:WIN - 1], dstf_w[:, :, 1:WIN],
                                              ALU.is_gt))
            link(dve, nc.vector.tensor_reduce(tally[:, 1:2], flat(run_b), AX_X, ALU.add))
            link(dve, nc.vector.memset(flat(run_b), 1.0))
            link(dve, nc.vector.tensor_tensor_scan(flat(run_a), flat(same_w), flat(run_b), 0.0,
                                                   ALU.mult, ALU.add))
            spread(dve, run_a, run_b)
            mark(nc.vector.reciprocal(flat(weight_w), flat(run_b)), s_mk)
            dve.wait_ge(s_tp, TP_IDX)
            for s in range(SLOTS):
                nc.vector.tensor_copy(idx_c[:, s, :], psA[s][:, 0:TG * GR])
            dve.wait_ge(s_tp, TP_LOC)
            for s in range(SLOTS):
                nc.vector.tensor_copy(loc_c[:, s, :], (psA[2], psB[0])[s][:, 0:TG * GR])
            dve.wait_ge(s_tp, TP_WGT)
            for s in range(SLOTS):
                last = nc.vector.tensor_copy(wgt_c[:, s, :], (psB[1], psB[2])[s][:, 0:TG * GR])
            link(dve, last)
            dve.wait_ge(s_tp, TP_TALLY)
            link(dve, nc.vector.tensor_scalar(tally1[:, 0:1], psX[0:1, 0:1], float(E), None, ALU.not_equal))
            link(dve, nc.vector.tensor_scalar(tally1[:, 1:2], psX[0:1, 1:2], 0.0, None, ALU.is_gt))
            mark(nc.vector.tensor_tensor(general_i[:, :], tally1[:, 0:1], tally1[:, 1:2], ALU.max), s_flag)
            general = is_general(dve)
            for k in range(3):
                if k == 2:
                    nc.vector.drain().then_inc(s_score, 1)
                    dve.wait_ge(s_score, 2)
                    for a in range(2):
                        nc.vector.tensor_copy(score_r[:, a, :, :].rearrange("p b c -> p (b c)"),
                                              (psX, psY)[a][:, :]).then_inc(s_score_v, 1)
                    logits_vector(dve)
                    nc.vector.drain().then_inc(s_lt, 1)
                    dve.wait_ge(s_lt, 2)
                    mark(nc.vector.tensor_copy(logit_r[:, :, :].rearrange("p b c -> p (b c)"), psX[:, :]), s_lr)
                    dve.wait_ge(s_lw, 16 * GR * KCH)
                    nc.vector.tensor_scalar(flat(rst_a), flat(same_w), -1.0, BIG, ALU.add, ALU.mult)
                    link(dve, nc.vector.tensor_scalar(flat(rst_b), flat(next_w), -1.0, BIG, ALU.add, ALU.mult))
                    link(dve, nc.vector.tensor_tensor_scan(flat(run_a), flat(rst_a), flat(logit_w), 0.0,
                                                           ALU.add, ALU.max))
                    link(dve, nc.vector.tensor_tensor_scan(flat(run_b)[:, ::-1], flat(rst_b)[:, ::-1],
                                                           flat(run_a)[:, ::-1], 0.0, ALU.add, ALU.max))
                    mark(nc.vector.tensor_tensor(flat(run_a), flat(logit_w), flat(run_b), ALU.subtract), s_ex)
                    dve.wait_ge(s_ex, 2)
                    link(dve, nc.vector.tensor_tensor_scan(flat(run_a), flat(same_w), flat(run_b), 0.0,
                                                           ALU.mult, ALU.add))
                    spread(dve, run_a, rst_a)
                    link(dve, nc.vector.reciprocal(flat(rst_b), flat(rst_a)))
                    mark(nc.vector.tensor_tensor(flat(weight_w), flat(run_b), flat(rst_b), ALU.mult), s_mk)
                    dve.wait_ge(s_tp, TP_SOFT)
                    nc.vector.tensor_copy(wgt_c[:, 0, :], psX[:, 0:TG * GR])
                    link(dve, nc.vector.tensor_copy(wgt_c[:, 1, :], psY[:, 0:TG * GR]))
                with dve.If(general):
                    general_vector(dve, k)
                nc.vector.drain().then_inc(L[k].ready, 1)
                layer_vector(dve, k)


_INS = ['x', 'src', 'dst', 'edge_attr_64', 'L0_gnn_W1l', 'L0_gnn_b1', 'L0_gnn_W1r', 'L0_gnn_W2l', 'L0_gnn_b2',
        'L0_gnn_W2r', 'L1_gnn_W', 'L1_gnn_A']


def kernel(**inputs):
    import concourse.bacc as _bacc
    from concourse.bass_utils import run_bass_kernel_spmd as _run

    nc = _bacc.Bacc("TRN2", target_bir_lowering=False, num_devices=1)
    arrays, args = {}, []
    for name in _INS:
        a = np.ascontiguousarray(inputs[name])
        arrays[f"in_{name}"] = a
        args.append(nc.dram_tensor(f"in_{name}", a.shape, mybir.dt.from_np(a.dtype), kind="ExternalInput").ap())
    shape = inputs['x'].shape
    args.append(nc.dram_tensor("out", tuple(shape), F32, kind="ExternalOutput").ap())
    gnn_program(nc, *args)
    r = _run(nc, [arrays], core_ids=[0])
    return r.results[0]["out"]
```

```python
from contextlib import ExitStack

import numpy as np

import concourse.bass as bass
from concourse import mybir

F32 = mybir.dt.float32
F32R = mybir.dt.float32r
BF16 = mybir.dt.bfloat16
I32 = mybir.dt.int32
ALU = mybir.AluOpType
ACT = mybir.ActivationFunctionType
AX_X = mybir.AxisListType.X

P = 128
QT = 4
U = 2
NB = 4
SLOTS = 5
PAIRS = [(b + h, b) for b in range(QT) for h in range(2)]
WIN = SLOTS * P
CH = 16
KCH = WIN // CH
FRONT = P
LN_G = 5
PAD_DST = 52000
SKIP = 1.0e6
BIG = 1.0e30
EPS = 1e-5
ALPHA = 0.2
LQ = 17


class Step:

    def __init__(self, i, j, n, u):
        self.i, self.j, self.n, self.u = i, j, n, u
        self.t = i * u + j

    def at(self, d):
        return Step(self.i + (self.j + d) // self.u, (self.j + d) % self.u, self.n, self.u)

    @property
    def real(self):
        return not isinstance(self.t, int) or 0 <= self.t < self.n

    def after(self, n):
        return not isinstance(self.t, int) or self.t >= n


class Tile(Step):

    def __init__(self, i, j, n, u=U * QT):
        super().__init__(i, j, n, u)
        self.b, self.q = j % QT, j // QT
        self.g = i * U + self.q

    def at(self, d):
        return Tile(self.i + (self.j + d) // self.u, (self.j + d) % self.u, self.n)

    @property
    def reuse(self):
        return self.after(NB)


def drive(eng, kind, n, u, body, lead=0, flush=0, peel=1):
    m = (n - 1 - u) // u
    for t in range(-lead, peel * u):
        body(kind(t // u, t % u, n, u))
    with eng.Fori(peel, m) as i:
        for j in range(u):
            body(kind(i, j, n, u))
    for t in range(u * m, n + flush):
        body(kind(t // u, t % u, n, u))


def uses(n, u, j):
    return (n - j + u - 1) // u


def gnn_program(nc, x, src, dst, edge_attr, W1l, b1, W1r, W2l, b2, W2r, W, A, out):
    N, D = x.shape
    E = src.shape[0]
    ED = edge_attr.shape[1]
    H = D // P
    NT = (N + P - 1) // P
    TAIL = N - (NT - 1) * P
    NP = NT * P
    EC = (E + P - 1) // P
    ETAIL = E - (EC - 1) * P
    EB = 4
    NG = (NT + QT - 1) // QT
    LAST = NG * QT * P
    PADS = 1200
    SR = (FRONT + E + PADS) // CH
    FC = (E + PADS) // CH
    FB = (FC + 511) // 512
    LB = (NT - 1) // LN_G
    assert H == 2 and NG <= P and EC <= EB * P and (NT - 1) % LN_G == 0 and FB <= 7
    assert (FRONT + E + PADS) % CH == 0 and E % CH == 0 and PADS >= WIN and PADS % 16 == 0
    assert EC % LQ == 0 and PAD_DST >= LAST

    ctx = ExitStack()
    with ctx:
        def sb(name, shape, dt=F32):
            return ctx.enter_context(nc.sbuf_tensor(name, shape, dt))

        def sem(name):
            return ctx.enter_context(nc.semaphore(name))

        def dram(name, shape, dt=F32):
            return nc.dram_tensor(name, shape, dt, kind="Internal")

        rows_tab = [dram(f"rows_tab{k}", (NP, D)) for k in range(3)]
        sums_tab = [dram(f"sums_tab{k}", (NP, D)) for k in range(3)]
        own_tab = [dram(f"own_tab{k}", (NP, D)) for k in range(2)]
        x1_tab = dram("x1_tab", (NP, D))
        src_pad = dram("src_pad", (SR, CH), I32)
        dst_pad = dram("dst_pad", (SR, CH), I32)
        attr_tab = dram("attr_tab", (SR, CH))
        score_src = dram("score_src", (EB * P * P, 1))
        score_dst = dram("score_dst", (EB * P * P, 1))
        maxden = dram("maxden", (NP, 2))

        ident = sb("ident", [P, P])
        lower = sb("lower", [P, P])
        iota_i = sb("iota_i", [P, P], I32)
        iota_n = sb("iota_n", [P, P])
        part_i = sb("part_i", [P, 1], I32)
        part_n = sb("part_n", [P, 1])
        tile0_i = sb("tile0_i", [NG, QT + 1], I32)
        tile0 = sb("tile0", [NG, QT + 1])
        zeros = sb("zeros", [P, D])
        ones = sb("ones", [P, P])
        ones_b = sb("ones_b", [P, P], BF16)
        eps = sb("eps", [P, 1])
        pad_i = sb("pad_i", [16, PADS // 16], I32)
        pad_f = sb("pad_f", [16, FRONT // 16], I32)
        pad_z = sb("pad_z", [16, PADS // 16], I32)

        mats = [W1l, W1r, W2l, W2r, W]
        early_w = sb("early_w", [P, 5 * H * D])
        w_nat = early_w[:, :].rearrange("p (n h d) -> p n h d", n=5, h=H)
        w_hi = sb("w_hi", [P, 4, H, D], F32R)
        w_lo = sb("w_lo", [P, 4, H, D], F32R)
        bias_full = sb("bias_full", [P, 2, D])
        bias_rest = sb("bias_rest", [P, 2, D])
        bias_part = sb("bias_part", [P, 3, 2, D], BF16)
        bias_rows = sb("bias_rows", [P, 2, D], BF16)
        a_col = sb("a_col", [P, 2 * H])
        a_edge = sb("a_edge", [P, ED])
        w_att = sb("w_att", [P, H, D + 2])

        src_rows = sb("src_rows", [P, EB, P], I32)
        dst_rows = sb("dst_rows", [P, EB, P], I32)
        edge_f = sb("edge_f", [P, 2, EB, P])
        src_c = sb("src_c", [P, EB * P], I32)
        dst_c = sb("dst_c", [P, EB * P], I32)
        dst_f = sb("dst_f", [P, EB * P])
        attr_l = sb("attr_l", [125, 400])
        attr_r = sb("attr_r", [P, EB, P])
        logit_c = sb("logit_c", [P, EB * P])

        firsts_i = sb("firsts_i", [1, FC], I32)
        firsts = firsts_i[:, :].bitcast(F32)
        near = sb("near", [P, U, QT * P])
        near_p = sb("near_p", [P, 2 * QT, P])
        below = near[0:NG, :, :]
        counts = sb("counts", [NG, 2, FB])
        count2 = sb("count2", [NG, 2])
        start_f = sb("start_f", [NG, 1])
        start_i = sb("start_i", [NG, 1], I32)
        chunk_f = sb("chunk_f", [NG, KCH])
        chunk = sb("chunk", [NG, KCH], I32)
        src_w = sb("src_w", [NG, WIN], I32)
        dst_w = sb("dst_w", [NG, WIN], I32)
        attr_w = sb("attr_w", [NG, WIN])
        srcf_w = sb("srcf_w", [NG, WIN])
        dstf_w = sb("dstf_w", [NG, WIN])
        loc_w = sb("loc_w", [NG, 2 * QT, P])
        in_w = near[0:NG, :, :].rearrange("g u (b n) -> g (u b) n", n=P)
        valid_w = near_p[0:NG, :, :]
        early_z = sb("early_z", [P, 4 * WIN])
        any_w, run_a, run_b, weight_w = (early_z[0:NG, n * WIN:(n + 1) * WIN] for n in range(4))
        same_w = sb("same_w", [NG, WIN])
        next_w = sb("next_w", [NG, WIN])
        rst_a, rst_b, logit_w = any_w, dstf_w, srcf_w
        tally = sb("tally", [NG, 2])
        tally1 = sb("tally1", [1, 2])
        general_i = sb("general_i", [1, 1], I32)

        idx_c = sb("idx_c", [P, SLOTS, NG], I32)
        loc_c = sb("loc_c", [P, 2 * QT, NG])
        wgt_c = sb("wgt_c", [P, SLOTS, NG])

        ln_x = sb("ln_x", [P, 2, LN_G, D])
        early_h = sb("early_h", [P, 2 * LN_G * D])
        early_r = sb("early_r", [P, 2 * LN_G * D])
        ln_h = early_h[:, :].rearrange("p (j g d) -> p j g d", j=2, g=LN_G)
        ln_r = early_r[:, :].rearrange("p (j g d) -> p j g d", j=2, g=LN_G)
        ln_z = early_z[:, :].rearrange("p (j g d) -> p j g d", j=2, g=LN_G)
        T_hi = sb("T_hi", [P, 2, D], F32R)
        T_lo = sb("T_lo", [P, 2, D], F32R)
        ln_st = sb("ln_st", [P, 2, LN_G, 6])
        ln_mv = sb("ln_mv", [P, 2, LN_G, 2])
        ln_sd = sb("ln_sd", [P, 2, LN_G])
        ln_rs = sb("ln_rs", [P, 2, LN_G])
        ln_nm = sb("ln_nm", [P, 2, LN_G])

        idx_t = sb("idx_t", [P, U, SLOTS], I32)
        rows = ln_x
        assert U == 2 and SLOTS == LN_G
        row_hi = sb("row_hi", [P, U, SLOTS, D], F32R)
        row_lo = sb("row_lo", [P, U, SLOTS, D], F32R)
        sel = sb("sel", [P, NB, 2, P], F32R)
        early_e = sb("early_e", [P, 4 * 10 * ED])
        ea = early_e[:, 0:20 * ED].rearrange("p (j q e) -> p j q e", j=2, q=10)
        ea_p = early_e[:, 20 * ED:40 * ED].rearrange("p (j q e) -> p j q e", j=2, q=10)
        sel_w = early_e[:, 0:NB * 2 * P].rearrange("p (b h n) -> p b h n", b=NB, h=2)
        xin = early_r[:, 0:NB * D].rearrange("p (b d) -> p b d", b=NB)
        res = early_r[:, NB * D:2 * NB * D].rearrange("p (b d) -> p b d", b=NB)
        h_T = early_h[:, 0:NB * D].rearrange("p (b d) -> p b d", b=NB)
        own_out = early_h[:, NB * D:2 * NB * D].rearrange("p (b d) -> p b d", b=NB)
        h_out = early_w[:, 0:NB * D].rearrange("p (b d) -> p b d", b=NB)
        x_out = early_w[:, NB * D:2 * NB * D].rearrange("p (b d) -> p b d", b=NB)
        z_out = early_e[:, NB * 2 * P:NB * (2 * P + D + 2)].rearrange("p (b d) -> p b d", b=NB)
        t_st = sb("t_st", [P, NB, 6])
        t_mv = sb("t_mv", [P, NB, 2])
        t_sd = sb("t_sd", [P, NB])
        t_rs = sb("t_rs", [P, NB])
        t_nm = sb("t_nm", [P, NB])
        score_c = sb("score_c", [P, 2, EB * P])
        score_r = edge_f

        idx_l = sb("idx_l", [P, 2, 2, LQ], I32)
        got_l = sb("got_l", [P, 2, 2, LQ])
        idx_s = sb("idx_s", [P, U, SLOTS], I32)
        got_s = sb("got_s", [P, U, SLOTS])
        near_s = sb("near_s", [P, U, 2 * QT])
        ssrc_c = sb("ssrc_c", [P, SLOTS, NG])
        sdst_c = sb("sdst_c", [P, 2 * QT, NG])
        sum_c = sb("sum_c", [P, SLOTS, NG])

        g_idx = sb("g_idx", [P, 2], I32)
        g_msg = sb("g_msg", [P, D])
        g_acc = sb("g_acc", [P, D])
        g_md = sb("g_md", [P, 2])
        g_new = sb("g_new", [P, D])
        g_mdn = sb("g_mdn", [P, 2])
        g_dst = sb("g_dst", [P, 2])
        g_wide = sb("g_wide", [P, 2, P])
        g_eq = sb("g_eq", [P, P])
        g_t1 = sb("g_t1", [P, P])
        g_t2 = sb("g_t2", [P, P])
        g_wt = sb("g_wt", [P, P])
        g_mx = sb("g_mx", [P, 1])
        g_df = sb("g_df", [P, 2])
        g_ex = sb("g_ex", [P, 2])
        g_rk = sb("g_rk", [P, 1])
        g_to_f = sb("g_to_f", [P, 1])
        g_to = sb("g_to", [P, 1], I32)
        g_init = sb("g_init", [P, 2])
        g_all = early_h[:, 0:2 * NG * QT].rearrange("p (t o) -> p t o", o=2)
        assert 2 * NG * QT <= NB * D

        psA = [ctx.enter_context(nc.psum_tensor(f"psA{j}", [P, 512], F32)) for j in range(2)]
        psB = [ctx.enter_context(nc.psum_tensor(f"psB{j}", [P, 512], F32)) for j in range(4)]
        psX = ctx.enter_context(nc.psum_tensor("psX", [P, 512], F32))
        psY = ctx.enter_context(nc.psum_tensor("psY", [P, 512], F32))
        psT, psZ, psO, psG = psA, psB[0:2], [psX, psY], psB[2:4]
        banks = [psA[0], psA[1], psB[0], psB[1], psB[2], psB[3], psX]

        s_const = sem("s_const")
        s_w = sem("s_w")
        s_edges = sem("s_edges")
        s_edges_f = sem("s_edges_f")
        s_pads = sem("s_pads")
        s_firsts = sem("s_firsts")
        s_firsts_f = sem("s_firsts_f")
        s_chunk = sem("s_chunk")
        s_win = sem("s_win")
        s_tp = sem("s_tp")
        s_dv = sem("s_dv")
        s_mk = sem("s_mk")
        s_flag = sem("s_flag")
        s_turn = sem("s_turn")
        s_turn_a = sem("s_turn_a")
        s_pl = sem("s_pl")
        ln_ld = [sem(f"ln_ld{j}") for j in range(2)]
        ln_stored = [sem(f"ln_stored{j}") for j in range(2)]
        ln_rstored = [sem(f"ln_rstored{j}") for j in range(2)]
        ln_stats = sem("ln_stats")
        ln_aggr = sem("ln_aggr")
        ln_std = sem("ln_std")
        ln_scale = sem("ln_scale")
        ln_rcp = sem("ln_rcp")
        ln_done = sem("ln_done")
        ln_tp = sem("ln_tp")
        ln_hi = sem("ln_hi")
        ln_lo = sem("ln_lo")
        ln_dense = sem("ln_dense")
        ln_r_done = sem("ln_r_done")
        ln_z_done = sem("ln_z_done")

        dve_n = [0]

        def link(eng, ins, s=s_dv, count=dve_n):
            count[0] += 1
            ins.then_inc(s, 1)
            eng.wait_ge(s, count[0])

        class Layer:

            def __init__(self, k):
                self.k = k
                self.idx = sem(f"idx_copied{k}")
                self.rows_ld = [sem(f"rows_ld{k}_{j}") for j in range(U)]
                self.xin_ld = [sem(f"xin_ld{k}_{j}") for j in range(NB)] if k == 0 else None
                self.res_ld = [sem(f"res_ld{k}_{j}") for j in range(NB)]
                self.z_st = [sem(f"z_st{k}_{j}") for j in range(NB)] if k < 2 else None
                self.own_st = [sem(f"own_st{k}_{j}") for j in range(NB)] if k == 0 else None
                self.x_st = [sem(f"x_st{k}_{j}") for j in range(NB)] if k else None
                self.hi = sem(f"row_hi_made{k}") if k == 0 else None
                self.lo = sem(f"row_lo_made{k}") if k == 0 else None
                self.sel = sem(f"sel_made{k}")
                self.aggregated = sem(f"aggregated{k}")
                self.x = sem(f"x_made{k}")
                if k < 2:
                    self.h = sem(f"h_made{k}")
                    self.transposed = sem(f"h_transposed{k}")
                    self.operand = sem(f"h_T_copied{k}")
                    self.dense = sem(f"dense{k}")
                    self.z = sem(f"z_copied{k}")
                if k == 0:
                    self.low = sem("T_lo_made")
                    self.own = sem("own_made")
                self.ready = sem(f"windows_ready{k}")

        L = [Layer(k) for k in range(3)]
        ln2_stats = sem("ln2_stats")
        ln2_aggr = sem("ln2_aggr")
        ln2_std = sem("ln2_std")
        ln2_rcp = sem("ln2_rcp")
        ln2_scale = sem("ln2_scale")
        sc_kept = sem("sc_kept")
        s_score = sem("s_score")
        s_score_v = sem("s_score_v")
        s_score_st = sem("s_score_st")
        l_idx = sem("l_idx")
        l_got = [sem(f"l_got{j}") for j in range(2)]
        l_dv = sem("l_dv")
        a_ea = [sem(f"a_ea{j}") for j in range(2)]
        a_dv = sem("a_dv")
        l_tp = sem("l_tp")
        l_rows = sem("l_rows")
        l_attr = sem("l_attr")
        a_st = sem("a_st")
        a_win = sem("a_win")
        t_idx = sem("t_idx")
        t_got = [sem(f"t_got{j}") for j in range(U)]
        t_near = [sem(f"t_near{j}") for j in range(U)]
        t_pairs = sem("t_pairs")
        t_kept = sem("t_kept")
        s_sum = sem("s_sum")
        s_ex = sem("s_ex")

        def table_written(eng, k):
            if k == 0:
                for j in range(2):
                    eng.wait_ge(ln_stored[j], 16 * uses(LB + 1, 2, j))
            else:
                for j in range(NB):
                    eng.wait_ge(L[k - 1].z_st[j], 16 * uses(NT, NB, j))

        g_inited = sem("g_inited")
        g_set = sem("g_set")
        g_indexed = sem("g_indexed")
        g_got = sem("g_got")
        g_put = sem("g_put")
        g_dve = sem("g_dve")
        g_pe = sem("g_pe")
        g_act = sem("g_act")
        g_den = sem("g_den")
        g_fin = sem("g_fin")
        GDV = 17

        def general_sync(sp, k):
            c0 = k * EC
            sp.wait_ge(g_set, 2 * k + 1)
            sp.dma_start(sums_tab[k][:, :].rearrange("(t p) d -> p t d", p=P),
                         zeros[:, :].unsqueeze(1).to_broadcast([P, NT, D])).then_inc(g_inited, 16)
            sp.dma_start(maxden[:, :].rearrange("(t p) d -> p t d", p=P),
                         g_init[:, :].unsqueeze(1).to_broadcast([P, NT, 2]),
                         allow_slow_non_contiguous=True).then_inc(g_inited, 16)
            sp.wait_ge(g_put, 32 * (c0 + EC))
            sp.wait_ge(g_fin, 3 * k + 1)
            sp.dma_start(g_all[:, 0:NT, :], maxden[:, :].rearrange("(t p) d -> p t d", p=P),
                         allow_slow_non_contiguous=True).then_inc(g_den, 16)

        def general_pool(pool, k):
            c0 = k * EC
            pool.wait_ge(g_inited, 32 * (k + 1))
            pool.wait_ge(g_set, 2 * k + 2)
            last_row = pool.to_reg(NP - 1)
            with pool.Fori(0, EC) as c:
                nc.gpsimd.tensor_copy(g_idx[:, 0:1], src_c[:, bass.ds(c, 1)])
                nc.gpsimd.tensor_copy(g_idx[:, 1:2], dst_c[:, bass.ds(c, 1)]).then_inc(g_indexed, 1)
                pool.wait_ge(g_indexed, c + (c0 + k + 1))
                pool.sem_inc(s_turn, 1)
                for buf, tab, n in ((g_msg, rows_tab[k], 0), (g_md, maxden, 1), (g_acc, sums_tab[k], 1)):
                    nc.gpsimd.indirect_dma_start(
                        out=buf[:, :], out_offset=None, in_=tab[:, :],
                        in_offset=bass.IndirectOffsetOnAxis(ap=g_idx[:, n:n + 1], axis=0),
                        bounds_check=last_row, oob_is_err=False).then_inc(g_got, 16)
                pool.wait_ge(g_dve, GDV * (c + (c0 + 1)))
                pool.sem_inc(s_turn, 1)
                for buf, tab in ((g_mdn, maxden), (g_new, sums_tab[k])):
                    nc.gpsimd.indirect_dma_start(
                        out=tab[:, :], out_offset=bass.IndirectOffsetOnAxis(ap=g_to[:, 0:1], axis=0),
                        in_=buf[:, :], in_offset=None,
                        bounds_check=last_row, oob_is_err=False).then_inc(g_put, 16)
                pool.wait_ge(g_put, 32 * (c + (c0 + 1)))
            pool.wait_ge(g_put, 32 * (c0 + EC))
            nc.gpsimd.memset(idx_c[:, :, :], SKIP)
            nc.gpsimd.memset(wgt_c[:, :, :], 1.0)
            nc.gpsimd.memset(g_all[:, :, :], 1.0)
            nc.gpsimd.memset(loc_c[:, :, :], -1.0).then_inc(g_indexed, 1)
            pool.wait_ge(g_indexed, c0 + k + EC + 1)
            nc.gpsimd.iota(idx_c[:, 0:QT, :], pattern=[[P, QT], [QT * P, NG]], base=0,
                           channel_multiplier=1).then_inc(g_fin, 1)

        def general_tensor(pe, k):
            c0 = k * EC
            with pe.Fori(0, EC) as c:
                pe.wait_ge(g_dve, GDV * (c + c0) + 2)
                nc.tensor.transpose(psX[:, 0:P], g_wide[:, 0, :], ident[:, :])
                nc.tensor.transpose(psX[:, P:2 * P], g_wide[:, 1, :], ident[:, :]).then_inc(g_pe, 1)
                pe.wait_ge(g_dve, GDV * (c + c0) + 11)
                pe.wait_ge(g_got, 48 * (c + (c0 + 1)))
                nc.tensor.matmul(psY[:, 0:D], g_wt[:, :], g_msg[:, :], start=True, stop=True)
                nc.tensor.matmul(psY[:, D:D + 1], g_wt[:, :], ones[:, 0:1], start=True,
                                 stop=True).then_inc(g_pe, 1)

        def general_scalar(act, k):
            c0 = k * EC
            with act.Fori(0, EC) as c:
                act.wait_ge(g_dve, GDV * (c + c0) + 10)
                nc.scalar.activation(g_ex[:, :], g_df[:, :], ACT.Exp).then_inc(g_act, 1)

        def general_vector(dve, k):
            c0 = k * EC
            nc.vector.memset(g_init[:, 0:1], -BIG)
            nc.vector.memset(g_init[:, 1:2], 0.0).then_inc(g_set, 1)
            nc.vector.memset(g_msg[:, :], 0.0)
            nc.vector.memset(g_acc[:, :], 0.0)
            nc.vector.memset(g_md[:, :], 0.0)
            if k < 2:
                nc.vector.memset(logit_c[:, :], 0.0)
            nc.vector.drain().then_inc(g_set, 1)
            dve.wait_ge(g_set, 2 * k + 2)
            with dve.Fori(0, EC) as c:
                n = [0]

                def step(ins, wait=True):
                    n[0] += 1
                    ins.then_inc(g_dve, 1)
                    if wait:
                        dve.wait_ge(g_dve, GDV * (c + c0) + n[0])

                step(nc.vector.tensor_scalar(g_wide[:, 0, :], dst_f[:, bass.ds(c, 1)].to_broadcast([P, P]), 0.0,
                                             None, ALU.add), False)
                step(nc.vector.tensor_copy(g_wide[:, 1, :], logit_c[:, bass.ds(c, 1)].to_broadcast([P, P])), False)
                step(nc.vector.tensor_copy(g_dst[:, 0:1], dst_f[:, bass.ds(c, 1)]), False)
                step(nc.vector.tensor_copy(g_dst[:, 1:2], logit_c[:, bass.ds(c, 1)]))
                dve.wait_ge(g_pe, 2 * (c + c0) + 1)
                step(nc.vector.tensor_scalar(g_eq[:, :], psX[:, 0:P], g_dst[:, 0:1], None, ALU.is_equal))
                nc.vector.tensor_scalar(g_t1[:, :], g_eq[:, :], -1.0, BIG, ALU.add, ALU.mult)
                step(nc.vector.tensor_tensor(g_t2[:, :], g_eq[:, :], psX[:, P:2 * P], ALU.mult))
                step(nc.vector.tensor_tensor(g_t1[:, :], g_t1[:, :], g_t2[:, :], ALU.add))
                step(nc.vector.tensor_reduce(g_mx[:, :], g_t1[:, :], AX_X, ALU.max))
                dve.wait_ge(g_got, 48 * (c + (c0 + 1)))
                step(nc.vector.tensor_tensor(g_mdn[:, 0:1], g_mx[:, :], g_md[:, 0:1], ALU.max))
                nc.vector.tensor_tensor(g_df[:, 0:1], g_dst[:, 1:2], g_mdn[:, 0:1], ALU.subtract)
                step(nc.vector.tensor_tensor(g_df[:, 1:2], g_md[:, 0:1], g_mdn[:, 0:1], ALU.subtract))
                dve.wait_ge(g_act, c + (c0 + 1))
                step(nc.vector.tensor_scalar(g_wt[:, :], g_eq[:, :], g_ex[:, 0:1], None, ALU.mult))
                step(nc.vector.tensor_tensor(g_t2[:, :], g_eq[:, :], lower[:, :], ALU.mult))
                step(nc.vector.tensor_reduce(g_rk[:, :], g_t2[:, :], AX_X, ALU.max))
                step(nc.vector.scalar_tensor_tensor(g_to_f[:, 0:1], g_rk[:, :], SKIP, g_dst[:, 0:1],
                                                    ALU.mult, ALU.add))
                step(nc.vector.tensor_copy(g_to[:, 0:1], g_to_f[:, 0:1]))
                dve.wait_ge(g_pe, 2 * (c + c0) + 2)
                step(nc.vector.scalar_tensor_tensor(g_new[:, :], g_acc[:, :], g_ex[:, 1:2], psY[:, 0:D],
                                                    ALU.mult, ALU.add))
                step(nc.vector.scalar_tensor_tensor(g_mdn[:, 1:2], g_md[:, 1:2], g_ex[:, 1:2],
                                                    psY[:, D:D + 1], ALU.mult, ALU.add), False)
                assert n[0] == GDV
                dve.wait_ge(g_put, 32 * (c + (c0 + 1)))
            dve.wait_ge(g_den, 16 * (k + 1))
            dve.wait_ge(g_fin, 3 * k + 1)
            nc.vector.tensor_scalar(g_all[:, :, 1], g_all[:, :, 1], 0.5, None, ALU.max).then_inc(g_fin, 1)
            dve.wait_ge(g_fin, 3 * k + 2)
            by_tile = g_all[:, :, 1].rearrange("p (g b) -> p b g", b=QT)
            for b in range(QT):
                nc.vector.reciprocal(wgt_c[:, b, :], by_tile[:, b, :])
                last = nc.vector.tensor_copy(loc_c[:, 2 * b, :], part_n[:, 0:1].to_broadcast([P, NG]))
            last.then_inc(g_fin, 1)
            dve.wait_ge(g_fin, 3 * k + 3)

        def is_general(eng):
            eng.wait_ge(s_flag, 1)
            return eng.value_load(general_i[0:1, 0:1], min_val=0, max_val=1) != 0

        def layer_sync(sp, k):
            y = L[k]
            d = int(k == 1)

            def load_res(T):
                if T.reuse:
                    sp.wait_ge(y.x, T.t - NB + 1)
                tab = (own_tab[0], own_tab[1], x1_tab)[k]
                sp.dma_start(res[:, T.b, :], tab[bass.ds(T.t * P, P), :]).then_inc(y.res_ld[T.b], 16)

            def load_x(T):
                if T.reuse:
                    sp.wait_ge(y.own, T.t - NB + 1)
                last = isinstance(T.t, int) and T.t == NT - 1
                n = TAIL if last else P
                sp.dma_start(xin[0:n, T.b, :], x[bass.ds(T.t * P, n), :]).then_inc(y.xin_ld[T.b], 16)

            def store_z(T):
                sp.wait_ge(y.z, T.t + 1)
                sp.dma_start(rows_tab[k + 1][bass.ds(T.t * P, P), :], z_out[:, T.b, 0:D]).then_inc(y.z_st[T.b], 16)

            def store_own(T):
                sp.wait_ge(y.own, T.t + 1)
                sp.dma_start(own_tab[1][bass.ds(T.t * P, P), :], own_out[:, T.b, :]).then_inc(y.own_st[T.b], 16)

            def store_x(T):
                last = isinstance(T.t, int) and T.t == NT - 1
                n = TAIL if last and k == 2 else P
                tab = x1_tab if k == 1 else out
                sp.wait_ge(y.x, T.t + 1)
                sp.dma_start(tab[bass.ds(T.t * P, n), :], x_out[0:n, T.b, :]).then_inc(y.x_st[T.b], 16)

            def body(T):
                if T.real and k > 0:
                    store_x(T)
                if T.at(NB).real:
                    load_res(T.at(NB))
                Z = T.at(-4 - d)
                if k < 2 and Z.real:
                    store_z(Z)
                    if k == 0:
                        store_own(Z)
                if k == 0 and T.real:
                    load_x(T)

            if k == 0:
                for j in range(2):
                    sp.wait_ge(ln_rstored[j], 16 * uses(LB + 1, 2, j))
            for j in range(NB):
                if k == 1:
                    sp.wait_ge(L[0].own_st[j], 16 * uses(NT, NB, j))
                if k == 2:
                    sp.wait_ge(L[1].x_st[j], 16 * uses(NT, NB, j))
            for t in range(NB):
                load_res(Tile(0, t, NT))
            drive(sp, Tile, NT, U * QT, body, flush=4 + d)

        def layer_pool(pool, k, tab):
            y = L[k]
            last_row = pool.to_reg(NP - 1)

            def body(G):
                if G.after(U):
                    pool.wait_ge(y.rows_ld[G.j], 16 * SLOTS * G.i)
                    pool.sem_inc(s_turn, 1)
                nc.gpsimd.tensor_copy(idx_t[:, G.j, :], idx_c[:, :, bass.ds(G.t, 1)].rearrange("p s o -> p (s o)"))\
                    .then_inc(y.idx, 1)
                pool.wait_ge(y.idx, G.t + 1)
                for s in range(SLOTS):
                    if G.after(U):
                        if k == 0:
                            pool.wait_ge(y.lo, (G.t - U) * SLOTS + s + 1)
                        else:
                            pool.wait_ge(y.aggregated, (G.t - U) * QT + min(s + 1, QT))
                    pool.sem_inc(s_turn, 1)
                    nc.gpsimd.indirect_dma_start(
                        out=rows[:, G.j, s, :], out_offset=None, in_=tab[:, :],
                        in_offset=bass.IndirectOffsetOnAxis(ap=idx_t[:, G.j, s:s + 1], axis=0),
                        bounds_check=last_row, oob_is_err=False).then_inc(y.rows_ld[G.j], 16)

            pool.wait_ge(y.ready, 1)
            drive(pool, Step, NG, U, body)

        def split_slots(T):
            return ((0, 1), (2,), (3,), (4,))[T.b]

        def dense_parts(pe, par, m, bias):
            for f in range(H):
                cols = slice(f * P, (f + 1) * P)
                for n, (left, right) in enumerate(((T_hi, w_hi), (T_hi, w_lo), (T_lo, w_hi))):
                    for i, ps in enumerate((psZ, psO)):
                        nc.tensor.matmul(ps[par][:, 0:D], left[:, par, cols], right[:, m + i, f, :],
                                         start=(f == 0 and n == 0), stop=(f == H - 1 and n == 2 and i == 0))
            return nc.tensor.matmul(psO[par][:, 0:D], ones_b[:, :], bias_rows[:, bias, :], start=False, stop=True)

        def layer_tensor(pe, k):
            y = L[k]
            d = int(k == 1)

            def aggregate(T):
                pe.wait_ge(y.sel, T.t + 1)
                if k == 0:
                    pe.wait_ge(y.lo, T.g * SLOTS + T.b + 2)
                else:
                    pe.wait_ge(y.rows_ld[T.q], 16 * SLOTS * (T.i + 1))
                if T.after(2):
                    pe.wait_ge(y.x, T.t - 1)
                n = 0
                for h in range(2):
                    for part in (row_hi, row_lo) if k == 0 else (rows,):
                        mat = (sel_w if k else sel)[:, T.b, h, :]
                        last = nc.tensor.matmul(psG[T.b % 2][:, 0:D], mat, part[:, T.q, T.b + h, :],
                                                start=(n == 0), stop=(n == (3 if k == 0 else 1)))
                        n += 1
                last.then_inc(y.aggregated, 1)

            def transposes(T):
                pe.wait_ge(y.h, T.t + 1)
                if T.after(2):
                    pe.wait_ge(y.operand if k else y.low, T.t - 1)
                for f in range(H):
                    last = nc.tensor.transpose(psT[T.b % 2][:, f * P:(f + 1) * P], h_out[:, T.b, f * P:(f + 1) * P],
                                               ident[:, :])
                last.then_inc(y.transposed, 1)

            def products(T):
                pe.wait_ge(y.operand if k else y.low, T.t + 1)
                if T.after(2):
                    pe.wait_ge(y.z, T.t - 1)
                    if k == 0:
                        pe.wait_ge(y.own, T.t - 1)
                if k == 0:
                    last = dense_parts(pe, T.b % 2, 2, 1)
                else:
                    for f in range(H):
                        last = nc.tensor.matmul(psZ[T.b % 2][:, 0:D + 2], h_T[:, T.b, f * P:(f + 1) * P],
                                                w_att[:, f, :], start=(f == 0), stop=(f == H - 1))
                last.then_inc(y.dense, 1)

            def body(T):
                if T.at(1).real:
                    aggregate(T.at(1))
                if k < 2 and T.at(-1 - d).real:
                    transposes(T.at(-1 - d))
                if k < 2 and T.at(-2 - d).real:
                    products(T.at(-2 - d))

            if k:
                pe.wait_ge(L[k - 1].x, NT)
            drive(pe, Tile, NT, U * QT, body, lead=1, flush=2 + d if k < 2 else 0)

        def layer_scalar(act, k):
            y = L[k]
            d = int(k == 1)

            def split(T):
                G = T.at(QT)
                for s in split_slots(T):
                    if s == 0:
                        act.wait_ge(y.rows_ld[G.q], 16 * SLOTS * (G.i + 1))
                        if G.after(U * QT):
                            act.wait_ge(y.aggregated, (G.g - U + 1) * QT)
                        act.sem_inc(s_turn_a, 1)
                    nc.scalar.activation(row_hi[:, G.q, s, :], rows[:, G.q, s, :], ACT.Copy,
                                         scale=wgt_c[:, s, bass.ds(G.g, 1)]).then_inc(y.hi, 1)

            def std(T):
                act.wait_ge(ln2_aggr, T.t + 1)
                nc.scalar.activation(t_sd[:, T.b:T.b + 1], t_mv[:, T.b, 1:2], ACT.Sqrt,
                                     bias=eps[:, 0:1]).then_inc(ln2_std, 1)

            def make_h(T):
                act.wait_ge(ln2_scale if k else y.x, T.t + 1)
                if T.reuse:
                    act.wait_ge(y.transposed, T.t - NB + 1)
                if k:
                    nc.scalar.activation(h_out[:, T.b, :], x_out[:, T.b, :], ACT.Relu, bias=t_nm[:, T.b:T.b + 1],
                                         scale=t_rs[:, T.b:T.b + 1]).then_inc(y.h, 1)
                else:
                    nc.scalar.activation(h_out[:, T.b, :], x_out[:, T.b, :], ACT.Relu).then_inc(y.h, 1)

            def copy_operand(T):
                act.wait_ge(y.transposed, T.t + 1)
                n = NB if k else 2
                if T.after(n):
                    act.wait_ge(y.dense, T.t - n + 1)
                to = h_T[:, T.b, :] if k else T_hi[:, T.b % 2, :]
                nc.scalar.activation(to, psT[T.b % 2][:, 0:D], ACT.Copy).then_inc(y.operand, 1)

            def copy_z(T):
                n = D + 2 * k
                act.wait_ge(y.dense, T.t + 1)
                if T.reuse:
                    act.wait_ge(y.z_st[T.b], 16 * T.g)
                    if k:
                        act.wait_ge(sc_kept, T.t - NB + 1)
                nc.scalar.activation(z_out[:, T.b, 0:n], psZ[T.b % 2][:, 0:n], ACT.Copy).then_inc(y.z, 1)

            def body(T):
                if k == 0 and T.at(QT - T.b).real:
                    split(T)
                if k == 1 and T.at(-1).real:
                    std(T.at(-1))
                if T.at(-1 - d).real:
                    copy_operand(T.at(-1 - d))
                if T.at(-d).real:
                    make_h(T.at(-d))
                if T.at(-3 - d).real:
                    copy_z(T.at(-3 - d))

            if k == 1:
                act.wait_ge(L[0].dense, NT)
                table_written(act, 1)
            act.wait_ge(y.ready, 1)
            drive(act, Tile, NT, U * QT, body, lead=QT if k == 0 else 0, flush=3 + d)

        def layer_vector(dve, k):
            y = L[k]

            def split(T):
                G = T.at(QT)
                for s in split_slots(T):
                    dve.wait_ge(y.hi, G.g * SLOTS + s + 1)
                    nc.vector.scalar_tensor_tensor(row_lo[:, G.q, s, :], rows[:, G.q, s, :],
                                                   wgt_c[:, s, bass.ds(G.g, 1)],
                                                   row_hi[:, G.q, s, :].bitcast(F32),
                                                   ALU.mult, ALU.subtract).then_inc(y.lo, 1)

            def select(T):
                if T.reuse:
                    dve.wait_ge(y.aggregated, T.t - NB + 1)
                for h in range(2):
                    loc = loc_c[:, 2 * T.b + h, bass.ds(T.g, 1)]
                    if k == 0:
                        last = nc.vector.tensor_scalar(sel[:, T.b, h, :], iota_n[:, :], loc, None, ALU.is_equal)
                    else:
                        last = nc.vector.tensor_scalar(sel_w[:, T.b, h, :], iota_n[:, :], loc,
                                                       wgt_c[:, T.b + h, bass.ds(T.g, 1)], ALU.is_equal, ALU.mult)
                last.then_inc(y.sel, 1)

            def add_residual(T):
                dve.wait_ge(y.aggregated, T.t + 1)
                dve.wait_ge(y.res_ld[T.b], 16 * (T.g + 1))
                if T.reuse:
                    if k:
                        dve.wait_ge(y.x_st[T.b], 16 * T.g)
                    if k < 2:
                        dve.wait_ge(y.h, T.t - NB + 1)
                nc.vector.tensor_tensor(x_out[:, T.b, :], psG[T.b % 2][:, 0:D], res[:, T.b, :], ALU.add)\
                    .then_inc(y.x, 1)

            def make_low(T):
                dve.wait_ge(y.operand, T.t + 1)
                nc.vector.tensor_tensor(T_lo[:, T.b % 2, :], psT[T.b % 2][:, 0:D], T_hi[:, T.b % 2, :].bitcast(F32),
                                        ALU.subtract).then_inc(y.low, 1)

            def make_own(T):
                dve.wait_ge(y.dense, T.t + 1)
                dve.wait_ge(y.xin_ld[T.b], 16 * (T.g + 1))
                if T.reuse:
                    dve.wait_ge(y.own_st[T.b], 16 * T.g)
                nc.vector.tensor_tensor(own_out[:, T.b, :], psO[T.b % 2][:, 0:D], xin[:, T.b, :], ALU.add)\
                    .then_inc(y.own, 1)

            def scale(T):
                dve.wait_ge(ln2_std, T.t + 1)
                nc.vector.reciprocal(t_rs[:, T.b:T.b + 1], t_sd[:, T.b:T.b + 1]).then_inc(ln2_rcp, 1)
                dve.wait_ge(ln2_rcp, T.t + 1)
                nc.vector.scalar_tensor_tensor(t_nm[:, T.b:T.b + 1], t_mv[:, T.b, 0:1], -1.0,
                                               t_rs[:, T.b:T.b + 1], ALU.mult, ALU.mult).then_inc(ln2_scale, 1)

            def keep_scores(T):
                dve.wait_ge(y.z, T.t + 1)
                nc.vector.tensor_scalar(score_c[:, :, bass.ds(T.t, 1)].rearrange("p a o -> p (a o)"),
                                        z_out[:, T.b, D:D + 2], 0.0, None, ALU.add).then_inc(sc_kept, 1)

            def body(T):
                if T.real:
                    add_residual(T)
                if k == 1 and T.at(-1).real:
                    scale(T.at(-1))
                if k == 1 and T.real:
                    dve.wait_ge(y.x, T.t + 1)
                    nc.vector.bn_stats(t_st[:, T.b, :], x_out[:, T.b, :]).then_inc(ln2_stats, 1)
                if T.at(3).real:
                    select(T.at(3))
                if k == 1 and T.real:
                    dve.wait_ge(ln2_stats, T.t + 1)
                if k == 1 and T.at(-5).real:
                    keep_scores(T.at(-5))
                if k == 1 and T.real:
                    nc.vector.bn_aggr(t_mv[:, T.b, :], t_st[:, T.b, :]).then_inc(ln2_aggr, 1)
                if k == 0 and T.at(QT - T.b).real:
                    split(T)
                if k == 0 and T.at(-1).real:
                    make_low(T.at(-1))
                if k == 0 and T.at(-3).real:
                    make_own(T.at(-3))

            if k:
                dve.wait_ge(L[k - 1].aggregated, NT)
                dve.wait_ge(L[k - 1].h, NT)
            if k == 2:
                for j in range(NB):
                    dve.wait_ge(L[1].x_st[j], 16 * uses(NT, NB, j))
            drive(dve, Tile, NT, U * QT, body, lead=QT, flush=(3, 5, 0)[k])

        def ln_rows(T):
            last = isinstance(T.t, int) and T.t == LB
            return (1, TAIL) if last else (LN_G, P)

        def ln_slice(tab, T):
            g, n = ln_rows(T)
            return tab[bass.ds(T.t * (LN_G * P), g * n), :].rearrange("(g p) d -> p g d", p=n)

        def ln_sync(sp):
            def load(T):
                if not T.real:
                    return
                g, n = ln_rows(T)
                if T.after(2):
                    sp.wait_ge(ln_done, (T.t - 1) * LN_G)
                sp.dma_start(ln_x[0:n, T.j, 0:g, :], ln_slice(x, T)).then_inc(ln_ld[T.j], 16)

            def body(T):
                B = T.at(-1)
                if T.real:
                    load(T.at(2))
                if B.real:
                    g, n = ln_rows(B)
                    sp.wait_ge(ln_r_done, B.t * LN_G + g)
                    to = own_tab[0][bass.ds(B.t * (LN_G * P), g * P), :].rearrange("(g p) d -> p g d", p=P)
                    sp.dma_start(to, ln_r[:, B.j, 0:g, :]).then_inc(ln_rstored[B.j], 16)
                    sp.wait_ge(ln_z_done, B.t * LN_G + g)
                    to = rows_tab[0][bass.ds(B.t * (LN_G * P), g * P), :].rearrange("(g p) d -> p g d", p=P)
                    sp.dma_start(to, ln_z[:, B.j, 0:g, :]).then_inc(ln_stored[B.j], 16)

            for t in range(2):
                load(Step(0, t, LB + 1, 2))
            drive(sp, Step, LB + 1, 2, body, flush=1, peel=2)

        def ln_vector(dve):
            def copy_own(T, a):
                dve.wait_ge(ln_dense, T.t * LN_G + a + 1)
                if a == 0 and T.after(2):
                    dve.wait_ge(ln_rstored[T.j], 16 * T.i)
                nc.vector.tensor_copy(ln_r[:, T.j, a, :], psO[(T.j * LN_G + a) % 2][:, 0:D]).then_inc(ln_r_done, 1)

            def body(T):
                B = T.at(-1)
                if B.real:
                    g, n = ln_rows(B)
                    dve.wait_ge(ln_std, B.t + 1)
                    if B.after(2):
                        dve.wait_ge(ln_done, (B.t - 1) * LN_G)
                    nc.vector.reciprocal(ln_rs[0:n, B.j, 0:g], ln_sd[0:n, B.j, 0:g]).then_inc(ln_rcp, 1)
                    dve.wait_ge(ln_rcp, B.t + 1)
                    nc.vector.scalar_tensor_tensor(ln_nm[0:n, B.j, 0:g], ln_mv[0:n, B.j, 0:g, 0], -1.0,
                                                   ln_rs[0:n, B.j, 0:g], ALU.mult, ALU.mult).then_inc(ln_scale, 1)
                C, Z = T.at(-2), T.at(-3)
                for a in range(LN_G):
                    now = [b for b in ((), (0, 1), (2, 3), (4,), ())[a] if T.real and b < ln_rows(T)[0]]
                    if now:
                        g, n = ln_rows(T)
                        dve.wait_ge(ln_ld[T.j], 16 * (T.i + 1))
                        for b in now:
                            last = nc.vector.bn_stats(ln_st[0:n, T.j, b, :], ln_x[0:n, T.j, b, :])
                        if now[-1] == g - 1:
                            last.then_inc(ln_stats, 1)
                            dve.wait_ge(ln_stats, T.t + 1)
                    if C.real and a < ln_rows(C)[0]:
                        dve.wait_ge(ln_hi, C.t * LN_G + a + 1)
                        par = (C.j * LN_G + a) % 2
                        nc.vector.tensor_tensor(T_lo[:, par, :], psT[par][:, 0:D], T_hi[:, par, :].bitcast(F32),
                                                ALU.subtract).then_inc(ln_lo, 1)
                    if now and now[-1] == g - 1:
                        for b in range(g):
                            last = nc.vector.bn_aggr(ln_mv[0:n, T.j, b, :], ln_st[0:n, T.j, b, :])
                        last.then_inc(ln_aggr, 1)
                    if a == 0 and Z.real:
                        copy_own(Z, ln_rows(Z)[0] - 1)
                    if a and C.real and a < ln_rows(C)[0]:
                        copy_own(C, a - 1)

            drive(dve, Step, LB + 1, 2, body, flush=3, peel=2)

        def ln_tensor(pe):
            def transposes(T, a):
                par = (T.j * LN_G + a) % 2
                n = T.t * LN_G + a
                pe.wait_ge(ln_done, n + 1)
                if a >= 2 or T.after(1):
                    pe.wait_ge(ln_lo, n - 1)
                for f in range(H):
                    last = nc.tensor.transpose(psA[par][:, f * P:(f + 1) * P],
                                               ln_h[:, T.j, a, f * P:(f + 1) * P], ident[:, :])
                last.then_inc(ln_tp, 1)

            def product(T, a):
                par = (T.j * LN_G + a) % 2
                n = T.t * LN_G + a
                pe.wait_ge(ln_lo, n + 1)
                if a >= 2 or T.after(1):
                    pe.wait_ge(ln_r_done, n - 1)
                    pe.wait_ge(ln_z_done, n - 1)
                last = dense_parts(pe, par, 0, 0)
                last.then_inc(ln_dense, 1)

            def body(T):
                if T.real:
                    for a in range(ln_rows(T)[0]):
                        transposes(T, a)
                        if a:
                            product(T, a - 1)
                        elif T.at(-1).real:
                            product(T.at(-1), ln_rows(T.at(-1))[0] - 1)
                elif T.at(-1).real:
                    product(T.at(-1), ln_rows(T.at(-1))[0] - 1)

            drive(pe, Step, LB + 1, 2, body, flush=1, peel=2)

        def ln_scalar(act):
            def copy_z(T, a):
                act.wait_ge(ln_dense, T.t * LN_G + a + 1)
                if a == 0 and T.after(2):
                    act.wait_ge(ln_stored[T.j], 16 * T.i)
                nc.scalar.activation(ln_z[:, T.j, a, :], psZ[(T.j * LN_G + a) % 2][:, 0:D], ACT.Copy)\
                    .then_inc(ln_z_done, 1)

            def body(T):
                B, C, Z = T.at(-1), T.at(-2), T.at(-3)
                for a in range(LN_G):
                    if C.real and a < ln_rows(C)[0]:
                        n = C.t * LN_G + a
                        act.wait_ge(ln_tp, n + 1)
                        if a >= 2 or C.after(1):
                            act.wait_ge(ln_dense, n - 1)
                        par = (C.j * LN_G + a) % 2
                        nc.scalar.activation(T_hi[:, par, :], psT[par][:, 0:D], ACT.Copy).then_inc(ln_hi, 1)
                    if a == 0 and Z.real:
                        copy_z(Z, ln_rows(Z)[0] - 1)
                    if a and C.real and a < ln_rows(C)[0]:
                        copy_z(C, a - 1)
                    if a == 0 and B.real:
                        act.wait_ge(ln_scale, B.t + 1)
                        if B.after(2):
                            act.wait_ge(ln_tp, (B.t - 1) * LN_G)
                    for b in ((0, 1), (2, 3), (4,), (), ())[a]:
                        if B.real and b < ln_rows(B)[0]:
                            g, n = ln_rows(B)
                            nc.scalar.activation(ln_h[0:n, B.j, b, :], ln_x[0:n, B.j, b, :], ACT.Relu,
                                                 bias=ln_nm[0:n, B.j, b:b + 1], scale=ln_rs[0:n, B.j, b:b + 1])\
                                .then_inc(ln_done, 1)
                if T.real:
                    g, n = ln_rows(T)
                    act.wait_ge(ln_aggr, T.t + 1)
                    nc.scalar.activation(ln_sd[0:n, T.j, 0:g], ln_mv[0:n, T.j, 0:g, 1], ACT.Sqrt,
                                         bias=eps[0:n, 0:1]).then_inc(ln_std, 1)

            act.wait_ge(s_const, 1)
            drive(act, Step, LB + 1, 2, body, flush=3, peel=2)

        AR, AQ = 125, 10
        AN = E // AR // AQ
        ALINKS = ED.bit_length()
        assert AR * AQ * AN == E and AN % 2 == 0

        def attr_pool(pool):
            by_part = edge_attr.rearrange("(p c) d -> p c d", p=AR)

            def load(q, j):
                nc.gpsimd.dma_start(ea[0:AR, j, :, :], by_part[:, bass.ds(q * AQ, AQ), :]).then_inc(a_ea[j], 16)

            def step(i, j, q, more):
                pool.wait_ge(a_ea[j], 16 * (i + 1))
                nc.gpsimd.tensor_tensor(ea_p[0:AR, j, :, :], ea[0:AR, j, :, :],
                                        a_edge[0:AR, :].unsqueeze(1).to_broadcast([AR, AQ, ED]),
                                        ALU.mult).then_inc(a_dv, 1)
                n, w = 1, ED // 2
                while w:
                    pool.wait_ge(a_dv, ALINKS * q + n)
                    if w == 1:
                        pool.sem_inc(s_turn, 1)
                    to = ea_p[0:AR, j, :, 0:w] if w > 1 else attr_l[0:AR, bass.ds(q * AQ, AQ)].unsqueeze(2)
                    nc.gpsimd.tensor_tensor(to, ea_p[0:AR, j, :, 0:w], ea_p[0:AR, j, :, w:2 * w],
                                            ALU.add).then_inc(a_dv, 1)
                    n, w = n + 1, w // 2
                assert n == ALINKS
                if more:
                    load(q + 2, j)

            pool.wait_ge(s_w, 16 * 9)
            for j in range(2):
                load(j, j)
            with pool.Fori(0, AN // 2 - 1) as i:
                for j in range(2):
                    step(i, j, 2 * i + j, True)
            for j in range(2):
                step(AN // 2 - 1, j, AN - 2 + j, False)
            pool.drain().then_inc(a_dv, 1)
            pool.wait_ge(a_dv, ALINKS * AN + 1)
            lin = attr_tab[:, :].rearrange("r c -> (r c)")
            nc.gpsimd.dma_start(lin[FRONT:FRONT + E].rearrange("(p c) -> p c", p=AR), attr_l[0:AR, :])\
                .then_inc(a_st, 16)
            nc.gpsimd.dma_start(lin[0:FRONT].rearrange("(p c) -> p c", p=16), zeros[0:16, 0:FRONT // 16])\
                .then_inc(a_st, 16)
            nc.gpsimd.dma_start(lin[FRONT + E:SR * CH].rearrange("(p c) -> p c", p=16),
                                zeros[0:16, 0:PADS // 16]).then_inc(a_st, 16)
            pool.wait_ge(a_st, 48)
            windows_of(pool, attr_tab, attr_w, a_win)

        def windows_of(pool, tab, buf, s):
            last_chunk = pool.to_reg(SR - 1)
            for c in range(KCH):
                nc.gpsimd.indirect_dma_start(
                    out=buf[:, c * CH:(c + 1) * CH], out_offset=None, in_=tab[:, :],
                    in_offset=bass.IndirectOffsetOnAxis(ap=chunk[:, c:c + 1], axis=0),
                    bounds_check=last_chunk, oob_is_err=False).then_inc(s, 16)

        LN = EC // LQ
        LDV = 3

        def rows_of_edges(sp, lin, buf, s):
            full = (EC - 1) // P * P
            sp.dma_start(buf[:, 0:full // P, :],
                         lin[0:full * P].rearrange("(b p c) -> p b c", p=P, c=P)).then_inc(s, 16)
            sp.dma_start(buf[0:EC - 1 - full, full // P, :],
                         lin[full * P:(EC - 1) * P].rearrange("(p c) -> p c", c=P)).then_inc(s, 16)
            sp.dma_start(buf[EC - 1 - full:EC - full, full // P, 0:ETAIL],
                         lin[(EC - 1) * P:E].unsqueeze(0)).then_inc(s, 16)

        def logits_pool(pool):
            last_row = pool.to_reg(EB * P * P - 1)

            def step(i, j, q, reuse):
                if reuse:
                    pool.wait_ge(l_dv, LDV * (q - 1))
                    pool.sem_inc(s_turn, 1)
                nc.gpsimd.tensor_copy(idx_l[:, j, 0, :], src_c[:, bass.ds(q * LQ, LQ)])
                nc.gpsimd.tensor_copy(idx_l[:, j, 1, :], dst_c[:, bass.ds(q * LQ, LQ)]).then_inc(l_idx, 1)
                pool.wait_ge(l_idx, q + 1)
                pool.sem_inc(s_turn, 1)
                for a, tab in enumerate((score_src, score_dst)):
                    for c in range(LQ):
                        nc.gpsimd.indirect_dma_start(
                            out=got_l[:, j, a, c:c + 1], out_offset=None, in_=tab[:, :],
                            in_offset=bass.IndirectOffsetOnAxis(ap=idx_l[:, j, a, c:c + 1], axis=0),
                            bounds_check=last_row, oob_is_err=False).then_inc(l_got[j], 16)

            step(0, 0, 0, False)
            step(0, 1, 1, False)
            with pool.Fori(1, LN // 2) as i:
                for j in range(2):
                    step(i, j, 2 * i + j, True)
            step(LN // 2, 0, LN - 1, True)

        def logits_vector(dve):
            def step(i, j, q):
                n = [0]

                def chain(ins):
                    n[0] += 1
                    ins.then_inc(l_dv, 1)
                    dve.wait_ge(l_dv, LDV * q + n[0])

                dve.wait_ge(l_got[j], 2 * LQ * 16 * (i + 1))
                chain(nc.vector.tensor_tensor(got_l[:, j, 0, :], got_l[:, j, 0, :], got_l[:, j, 1, :], ALU.add))
                chain(nc.vector.tensor_tensor(got_l[:, j, 0, :], got_l[:, j, 0, :],
                                              logit_c[:, bass.ds(q * LQ, LQ)], ALU.add))
                chain(nc.vector.scalar_tensor_tensor(logit_c[:, bass.ds(q * LQ, LQ)], got_l[:, j, 0, :], ALPHA,
                                                     got_l[:, j, 0, :], ALU.mult, ALU.max))

            dve.wait_ge(l_tp, 1)
            link(dve, nc.vector.tensor_copy(logit_c[:, :], psX[:, :]))
            with dve.Fori(0, LN // 2) as i:
                for j in range(2):
                    step(i, j, 2 * i + j)
            step(LN // 2, 0, LN - 1)

        def attention_sync(sp):
            def body(G):
                if G.after(U):
                    sp.wait_ge(t_pairs, G.t - U + 1)
                sp.dma_start(near[:, G.j, :], score_dst[bass.ds(G.t * (QT * P), QT * P), :]
                             .rearrange("n o -> o n").to_broadcast([P, QT * P])).then_inc(t_near[G.j], 16)

            sp.wait_ge(s_score_st, 32 * EB)
            drive(sp, Step, NG, U, body)

        def attention_pool(pool):
            last_row = pool.to_reg(EB * P * P - 1)

            def body(G):
                if G.after(U):
                    pool.wait_ge(t_kept, G.t - U + 1)
                    pool.sem_inc(s_turn, 1)
                nc.gpsimd.tensor_copy(idx_s[:, G.j, :], idx_c[:, :, bass.ds(G.t, 1)].rearrange("p s o -> p (s o)"))\
                    .then_inc(t_idx, 1)
                pool.wait_ge(t_idx, G.t + 1)
                pool.sem_inc(s_turn, 1)
                for s in range(SLOTS):
                    nc.gpsimd.indirect_dma_start(
                        out=got_s[:, G.j, s:s + 1], out_offset=None, in_=score_src[:, :],
                        in_offset=bass.IndirectOffsetOnAxis(ap=idx_s[:, G.j, s:s + 1], axis=0),
                        bounds_check=last_row, oob_is_err=False).then_inc(t_got[G.j], 16)

            pool.wait_ge(s_score_st, 32 * EB)
            drive(pool, Step, NG, U, body)

        def attention_vector(dve):
            def body(G):
                dve.wait_ge(t_near[G.j], 16 * (G.i + 1))
                for n in range(2 * QT):
                    b = n // 2
                    last = nc.vector.scalar_tensor_tensor(near_p[:, n, :], iota_n[:, :], loc_c[:, n, bass.ds(G.t, 1)],
                                                          near[:, G.j, b * P:(b + 1) * P], ALU.is_equal, ALU.mult,
                                                          accum_out=near_s[:, G.j, n:n + 1])
                last.then_inc(t_pairs, 1)
                dve.wait_ge(t_pairs, G.t + 1)
                nc.vector.tensor_scalar(sdst_c[:, :, bass.ds(G.t, 1)].rearrange("p s o -> p (s o)"),
                                        near_s[:, G.j, :], 0.0, None, ALU.add)
                dve.wait_ge(t_got[G.j], 16 * SLOTS * (G.i + 1))
                nc.vector.tensor_scalar(ssrc_c[:, :, bass.ds(G.t, 1)].rearrange("p s o -> p (s o)"),
                                        got_s[:, G.j, :], 0.0, None, ALU.add).then_inc(t_kept, 1)

            drive(dve, Step, NG, U, body)
            dve.wait_ge(t_kept, NG)
            for s in range(SLOTS):
                n = max(2 * s - 1, 0)
                last = nc.vector.tensor_tensor(sum_c[:, s, :], ssrc_c[:, s, :], sdst_c[:, n, :], ALU.add)
            link(dve, last)
            last = nc.vector.tensor_tensor(sum_c[:, 1:SLOTS - 1, :], sum_c[:, 1:SLOTS - 1, :],
                                           sdst_c[:, 2:2 * QT - 1:2, :], ALU.add)
            last.then_inc(s_sum, 1)

        def spread(dve, last_of_run, total):
            link(dve, nc.vector.tensor_tensor_scan(total[:, ::-1], next_w[:, ::-1], last_of_run[:, ::-1], 0.0,
                                                   ALU.mult, ALU.max))

        def to_columns(pe, parts):
            for bank, n, source in parts:
                last = nc.tensor.transpose(bank[:, n * NG:(n + 1) * NG], source, ident[0:NG, 0:NG])
            last.then_inc(s_tp, 1)

        TP_SRC, TP_DST, TP_W, TP_V, TP_FIRST, TP_IDX, TP_LOC, TP_WGT, TP_TALLY, TP_SUM, TP_SOFT = range(1, 12)

        block = ctx.enter_context(nc.Block())

        @block.sync
        def _(sp):
            sp.wait_ge(s_const, 1)
            for tab, pad, fill, front in ((dst, dst_pad, pad_i, pad_f), (src, src_pad, pad_z, pad_z)):
                lin = pad[:, :].rearrange("r c -> (r c)")
                sp.dma_start(lin[FRONT:FRONT + E].rearrange("(a c) -> a c", a=16),
                             tab[0:E].rearrange("(a c) -> a c", a=16)).then_inc(s_pads, 16)
                sp.dma_start(lin[FRONT + E:SR * CH].rearrange("(a c) -> a c", a=16), fill[:, :]).then_inc(s_pads, 16)
                sp.dma_start(lin[0:FRONT].rearrange("(a c) -> a c", a=16), front[:, 0:FRONT // 16])\
                    .then_inc(s_pads, 16)
            for n, m in enumerate(mats):
                sp.dma_start(w_nat[:, n, :, :], m.rearrange("(h p) d -> p h d", p=P)).then_inc(s_w, 16)
            for n, b in enumerate((b1, b2)):
                sp.dma_start(bias_full[:, n, :], b.unsqueeze(0).to_broadcast([P, D])).then_inc(s_w, 16)
            sp.dma_start(a_col[:, :], A[0, 0:2 * D].rearrange("(q p) -> p q", p=P),
                         allow_slow_non_contiguous=True).then_inc(s_w, 16)
            sp.dma_start(a_edge[:, :], A[0:1, 2 * D:2 * D + ED].to_broadcast([P, ED])).then_inc(s_w, 16)
            sp.wait_ge(s_pads, 96)
            sp.dma_start(firsts_i[:, :], dst_pad[FRONT // CH:SR, 0:1].rearrange("r o -> o r"),
                         allow_slow_non_contiguous=True).then_inc(s_firsts, 16)
            for tab, buf in ((src, src_rows), (dst, dst_rows)):
                rows_of_edges(sp, tab, buf, s_edges)
            ln_sync(sp)
            general = is_general(sp)
            for k in range(3):
                if k == 2:
                    sp.wait_ge(s_score_v, 2)
                    for a, tab in enumerate((score_src, score_dst)):
                        for b in range(EB):
                            sp.dma_start(tab[b * P * P:(b + 1) * P * P, :].rearrange("(r c) o -> r (c o)", c=P),
                                         score_r[:, a, b, :]).then_inc(s_score_st, 16)
                    attention_sync(sp)
                with sp.If(general):
                    if k == 2:
                        sp.wait_ge(a_st, 48)
                        sp.wait_ge(l_attr, 1)
                        rows_of_edges(sp, attr_tab[:, :].rearrange("r c -> (r c)")[FRONT:FRONT + E], attr_r, l_rows)
                    general_sync(sp, k)
                layer_sync(sp, k)
            for j in range(NB):
                sp.wait_ge(L[2].x_st[j], 16 * uses(NT, NB, j))

        @block.gpsimd
        def _(pool):
            pool_n = [0]

            def chain(ins):
                link(pool, ins, s_pl, pool_n)

            nc.gpsimd.memset(zeros[:, :], 0.0)
            nc.gpsimd.memset(eps[:, :], EPS)
            nc.gpsimd.memset(pad_i[:, :], PAD_DST)
            nc.gpsimd.memset(pad_f[:, :], -1)
            nc.gpsimd.memset(pad_z[:, :], 0)
            nc.gpsimd.memset(src_rows[:, :, :], 0)
            chain(nc.gpsimd.memset(dst_rows[:, :, :], PAD_DST))
            pool.sem_inc(s_const, 1)
            nc.gpsimd.memset(lower[:, :], 1.0)
            chain(nc.gpsimd.memset(ident[:, :], 0.0))
            nc.gpsimd.affine_select(out=ident[:, :], in_=ident[:, :], compare_op=ALU.not_equal, fill=1.0,
                                    base=0, pattern=[[-1, P]], channel_multiplier=1)
            nc.gpsimd.affine_select(out=lower[:, :], in_=lower[:, :], compare_op=ALU.is_gt, fill=0.0,
                                    base=0, pattern=[[-1, P]], channel_multiplier=1)
            nc.gpsimd.memset(ones[:, :], 1.0)
            nc.gpsimd.memset(ones_b[:, :], 1.0)
            nc.gpsimd.iota(iota_i[:, :], pattern=[[1, P]], base=0, channel_multiplier=0)
            nc.gpsimd.iota(part_i[:, :], pattern=[[0, 1]], base=0, channel_multiplier=1)
            nc.gpsimd.iota(tile0_i[:, :], pattern=[[P, QT + 1]], base=0, channel_multiplier=QT * P)
            chain(nc.gpsimd.memset(bias_rows[:, :, :], 0.0))
            pool.sem_inc(s_const, 1)
            nc.gpsimd.memset(got_l[:, :, :, :], 0.0)
            nc.gpsimd.memset(got_s[:, :, :], 0.0)
            chain(nc.gpsimd.memset(score_c[:, :, :], 0.0))
            pool.wait_ge(s_chunk, 1)
            pool.wait_ge(s_pads, 96)
            windows_of(pool, dst_pad, dst_w, s_win)
            windows_of(pool, src_pad, src_w, s_win)
            attr_pool(pool)
            general = is_general(pool)
            for k in range(3):
                if k == 2:
                    attention_pool(pool)
                table_written(pool, k)
                with pool.If(general):
                    if k == 2:
                        logits_pool(pool)
                    general_pool(pool, k)
                    layer_pool(pool, k, sums_tab[k])
                with pool.Else():
                    layer_pool(pool, k, rows_tab[k])

        @block.scalar
        def _(act):
            ln_scalar(act)
            general = is_general(act)
            for k in range(3):
                if k == 2:
                    act.wait_ge(s_ex, 1)
                    nc.scalar.activation(run_b[:, :], run_a[:, :], ACT.Exp).then_inc(s_ex, 1)
                with act.If(general):
                    general_scalar(act, k)
                if k < 2:
                    layer_scalar(act, k)

        @block.tensor
        def _(pe):
            pe.wait_ge(s_const, 2)
            pe.wait_ge(s_edges_f, 1)
            for a in range(2):
                for b in range(EB):
                    last = nc.tensor.transpose((psX, psY)[a][:, b * P:(b + 1) * P], edge_f[:, a, b, :], ident[:, :])
                last.then_inc(s_tp, 1)
            pe.wait_ge(s_w, 16 * 9)
            for n in range(5):
                for ih in range(H):
                    for oh in range(H):
                        last = nc.tensor.transpose(banks[n][:, ih * D + oh * P:ih * D + (oh + 1) * P],
                                                   w_nat[:, n, oh, ih * P:(ih + 1) * P], ident[:, :])
            last.then_inc(s_tp, 1)
            for a in range(2):
                for ih in range(H):
                    for oh in range(H):
                        last = nc.tensor.matmul(psB[3][:, 2 * ih + a:2 * ih + a + 1],
                                                w_nat[:, 4, oh, ih * P:(ih + 1) * P],
                                                a_col[:, a * H + oh:a * H + oh + 1],
                                                start=(oh == 0), stop=(oh == H - 1))
            last.then_inc(s_tp, 1)
            pe.wait_ge(s_firsts_f, 1)
            for c in range(FB):
                n = min(512, FC - 512 * c)
                last = nc.tensor.matmul(banks[c][0:NG, 0:n], ones[0:1, 0:NG], firsts[0:1, 512 * c:512 * c + n],
                                        start=True, stop=True)
            last.then_inc(s_tp, 1)
            pe.wait_ge(s_chunk, 1)
            ln_tensor(pe)
            pe.wait_ge(ln_z_done, NT)
            pe.wait_ge(s_mk, 1)
            to_columns(pe, [(psA[0], s, srcf_w[:, s * P:(s + 1) * P]) for s in range(SLOTS)])
            to_columns(pe, [((psA[1], psB[0])[n // 5], n % 5, loc_w[:, n, :]) for n in range(2 * QT)])
            pe.wait_ge(s_mk, 2)
            to_columns(pe, [(psB[1], s, weight_w[:, s * P:(s + 1) * P]) for s in range(SLOTS)])
            nc.tensor.matmul(psX[0:1, 0:2], ones[0:NG, 0:1], tally[:, :], start=True, stop=True).then_inc(s_tp, 1)
            general = is_general(pe)
            for k in range(3):
                if k == 2:
                    pe.wait_ge(s_score, 1)
                    for a in range(2):
                        for b in range(EB):
                            last = nc.tensor.transpose((psX, psY)[a][:, b * P:(b + 1) * P],
                                                       score_c[:, a, b * P:(b + 1) * P], ident[:, :])
                    last.then_inc(s_score, 1)
                    pe.wait_ge(s_sum, 1)
                    for s in range(SLOTS):
                        last = nc.tensor.transpose((psX, psY)[s // 4][0:NG, s % 4 * P:(s % 4 + 1) * P],
                                                   sum_c[:, s, :], ident[:, :])
                    last.then_inc(s_tp, 1)
                    pe.wait_ge(s_mk, 3)
                    to_columns(pe, [(psX, s, weight_w[:, s * P:(s + 1) * P]) for s in range(SLOTS)])
                with pe.If(general):
                    if k == 2:
                        pe.wait_ge(l_attr, 2)
                        for b in range(EB):
                            last = nc.tensor.transpose(psX[:, b * P:(b + 1) * P], attr_r[:, b, :], ident[:, :])
                        last.then_inc(l_tp, 1)
                    general_tensor(pe, k)
                layer_tensor(pe, k)

        @block.vector
        def _(dve):
            def mark(ins, s):
                ins.then_inc(s, 1)

            dve.wait_ge(s_const, 2)
            nc.vector.tensor_copy(iota_n[:, :], iota_i[:, :])
            nc.vector.tensor_copy(part_n[:, :], part_i[:, :])
            link(dve, nc.vector.tensor_copy(tile0[:, :], tile0_i[:, :]))
            dve.wait_ge(s_w, 16 * 9)
            link(dve, nc.vector.tensor_copy(bias_part[:, 0, :, :], bias_full[:, :, :]))
            link(dve, nc.vector.tensor_tensor(bias_rest[:, :, :], bias_full[:, :, :], bias_part[:, 0, :, :],
                                              ALU.subtract))
            link(dve, nc.vector.tensor_copy(bias_part[:, 1, :, :], bias_rest[:, :, :]))
            link(dve, nc.vector.tensor_tensor(bias_rest[:, :, :], bias_rest[:, :, :], bias_part[:, 1, :, :],
                                              ALU.subtract))
            link(dve, nc.vector.tensor_copy(bias_part[:, 2, :, :], bias_rest[:, :, :]))
            for n in range(3):
                nc.vector.tensor_copy(bias_rows[32 * n:32 * n + 1, :, :], bias_part[32 * n:32 * n + 1, n, :, :])
            dve.wait_ge(s_edges, 16 * 6)
            nc.vector.tensor_copy(edge_f[:, 0, :, :], src_rows[:, :, :])
            nc.vector.tensor_copy(edge_f[:, 1, :, :], dst_rows[:, :, :]).then_inc(s_edges_f, 1)
            dve.wait_ge(s_firsts, 16)
            link(dve, nc.vector.tensor_copy(firsts[:, :], firsts_i[:, :]))
            link(dve, nc.vector.memset(firsts[:, E // CH:LAST // CH], float(LAST - 1)))
            dve.wait_ge(s_tp, TP_SRC)
            nc.vector.tensor_copy(src_c[:, :], psX[:, :])
            dve.wait_ge(s_tp, TP_DST)
            nc.vector.tensor_copy(dst_c[:, :], psY[:, :])
            nc.vector.tensor_copy(dst_f[:, :], psY[:, :])
            dve.wait_ge(s_tp, TP_W)
            for n in range(4):
                last = nc.vector.tensor_copy(w_hi[:, n, :, :].rearrange("p h d -> p (h d)"), banks[n][:, :])
            link(dve, last)
            for n in range(4):
                nc.vector.tensor_tensor(w_lo[:, n, :, :].rearrange("p h d -> p (h d)"), banks[n][:, :],
                                        w_hi[:, n, :, :].rearrange("p h d -> p (h d)").bitcast(F32), ALU.subtract)
            nc.vector.tensor_copy(w_att[:, :, 0:D], banks[4][:, :].rearrange("p (h d) -> p h d", h=H))
            dve.wait_ge(s_tp, TP_V)
            link(dve, nc.vector.tensor_copy(w_att[:, :, D:D + 2],
                                            psB[3][:, 0:2 * H].rearrange("p (h a) -> p h a", h=H)))
            dve.sem_inc(s_firsts_f, 1)
            dve.wait_ge(s_tp, TP_FIRST)
            for c in range(FB):
                n = min(512, FC - 512 * c)
                for h in range(2):
                    link(dve, nc.vector.tensor_scalar(below[:, h, 0:n], banks[c][0:NG, 0:n],
                                                      tile0[:, QT * h:QT * h + 1], 0.0, ALU.is_lt, ALU.add,
                                                      accum_out=counts[:, h, c:c + 1]))
            link(dve, nc.vector.tensor_reduce(count2[:, :], counts[:, :, :], AX_X, ALU.add))
            link(dve, nc.vector.tensor_tensor(start_f[:, :], count2[:, 0:1], count2[:, 1:2], ALU.add))
            link(dve, nc.vector.tensor_scalar(start_f[:, :], start_f[:, :], 0.5,
                                              float(FRONT // CH - KCH // 2) - 0.5, ALU.mult, ALU.add))
            link(dve, nc.vector.tensor_scalar(start_f[:, :], start_f[:, :], 0.0, None, ALU.max))
            link(dve, nc.vector.tensor_copy(start_i[:, :], start_f[:, :]))
            link(dve, nc.vector.tensor_copy(start_f[:, :], start_i[:, :]))
            link(dve, nc.vector.tensor_scalar(chunk_f[:, :], iota_n[0:NG, 0:KCH], start_f[:, 0:1], None, ALU.add))
            nc.vector.tensor_copy(chunk[:, :], chunk_f[:, :]).then_inc(s_chunk, 1)

            ln_vector(dve)

            dve.wait_ge(s_win, 16 * 2 * KCH)
            table_written(dve, 0)
            nc.vector.tensor_copy(srcf_w[:, :], src_w[:, :])
            link(dve, nc.vector.tensor_copy(dstf_w[:, :], dst_w[:, :]))
            for n, (s, b) in enumerate(PAIRS):
                last = nc.vector.tensor_scalar(loc_w[:, n, :], dstf_w[:, s * P:(s + 1) * P], tile0[:, b:b + 1],
                                               None, ALU.subtract)
            link(dve, last)
            link(dve, nc.vector.tensor_scalar(in_w[:, :, :], loc_w[:, :, :], 0.0, None, ALU.is_ge))
            link(dve, nc.vector.scalar_tensor_tensor(valid_w[:, :, :], loc_w[:, :, :], float(P), in_w[:, :, :],
                                                     ALU.is_lt, ALU.mult))
            nc.vector.tensor_copy(any_w[:, 0:P], valid_w[:, 0, :])
            nc.vector.tensor_copy(any_w[:, WIN - P:WIN], valid_w[:, 2 * QT - 1, :])
            link(dve, nc.vector.tensor_tensor(any_w[:, P:WIN - P].rearrange("g (s c) -> g s c", c=P),
                                              valid_w[:, 1:2 * QT - 1:2, :], valid_w[:, 2:2 * QT - 1:2, :], ALU.add))
            link(dve, nc.vector.tensor_scalar(any_w[:, :], any_w[:, :], -SKIP, SKIP, ALU.mult, ALU.add))
            mark(nc.vector.tensor_tensor(srcf_w[:, :], srcf_w[:, :], any_w[:, :], ALU.add), s_mk)
            link(dve, nc.vector.tensor_reduce(tally[:, 0:1], valid_w[:, :, :].rearrange("g n c -> g (n c)"),
                                              AX_X, ALU.add))
            nc.vector.memset(same_w[:, 0:1], 0.0)
            nc.vector.memset(next_w[:, WIN - 1:WIN], 0.0)
            link(dve, nc.vector.tensor_tensor(same_w[:, 1:WIN], dstf_w[:, 1:WIN], dstf_w[:, 0:WIN - 1],
                                              ALU.is_equal))
            link(dve, nc.vector.tensor_copy(next_w[:, 0:WIN - 1], same_w[:, 1:WIN]))
            link(dve, nc.vector.tensor_tensor(run_b[:, 1:WIN], dstf_w[:, 0:WIN - 1], dstf_w[:, 1:WIN], ALU.is_gt))
            link(dve, nc.vector.tensor_reduce(tally[:, 1:2], run_b[:, 1:WIN], AX_X, ALU.add))
            link(dve, nc.vector.memset(run_b[:, :], 1.0))
            link(dve, nc.vector.tensor_tensor_scan(run_a[:, :], same_w[:, :], run_b[:, :], 0.0, ALU.mult, ALU.add))
            spread(dve, run_a, run_b)
            mark(nc.vector.reciprocal(weight_w[:, :], run_b[:, :]), s_mk)
            dve.wait_ge(s_tp, TP_IDX)
            nc.vector.tensor_copy(idx_c[:, :, :].rearrange("p s g -> p (s g)"), psA[0][:, 0:SLOTS * NG])
            dve.wait_ge(s_tp, TP_LOC)
            nc.vector.tensor_copy(loc_c[:, 0:5, :].rearrange("p s g -> p (s g)"), psA[1][:, 0:5 * NG])
            nc.vector.tensor_copy(loc_c[:, 5:2 * QT, :].rearrange("p s g -> p (s g)"),
                                  psB[0][:, 0:(2 * QT - 5) * NG])
            dve.wait_ge(s_tp, TP_WGT)
            link(dve, nc.vector.tensor_copy(wgt_c[:, :, :].rearrange("p s g -> p (s g)"), psB[1][:, 0:SLOTS * NG]))
            dve.wait_ge(s_tp, TP_TALLY)
            link(dve, nc.vector.tensor_scalar(tally1[:, 0:1], psX[0:1, 0:1], float(E), None, ALU.not_equal))
            link(dve, nc.vector.tensor_scalar(tally1[:, 1:2], psX[0:1, 1:2], 0.0, None, ALU.is_gt))
            mark(nc.vector.tensor_tensor(general_i[:, :], tally1[:, 0:1], tally1[:, 1:2], ALU.max), s_flag)
            general = is_general(dve)
            for k in range(3):
                if k == 2:
                    nc.vector.drain().then_inc(s_score, 1)
                    dve.wait_ge(s_score, 2)
                    for a in range(2):
                        nc.vector.tensor_copy(score_r[:, a, :, :].rearrange("p b c -> p (b c)"),
                                              (psX, psY)[a][:, :]).then_inc(s_score_v, 1)
                    attention_vector(dve)
                    dve.wait_ge(s_tp, TP_SUM)
                    dve.wait_ge(a_win, 16 * KCH)
                    nc.vector.tensor_tensor(run_a[:, 0:4 * P], psX[0:NG, :], attr_w[:, 0:4 * P], ALU.add)
                    link(dve, nc.vector.tensor_tensor(run_a[:, 4 * P:WIN], psY[0:NG, 0:P], attr_w[:, 4 * P:WIN],
                                                      ALU.add))
                    link(dve, nc.vector.scalar_tensor_tensor(logit_w[:, :], run_a[:, :], ALPHA, run_a[:, :],
                                                             ALU.mult, ALU.max))
                    nc.vector.tensor_scalar(rst_a[:, :], same_w[:, :], -1.0, BIG, ALU.add, ALU.mult)
                    link(dve, nc.vector.tensor_scalar(rst_b[:, :], next_w[:, :], -1.0, BIG, ALU.add, ALU.mult))
                    link(dve, nc.vector.tensor_tensor_scan(run_a[:, :], rst_a[:, :], logit_w[:, :], 0.0,
                                                           ALU.add, ALU.max))
                    link(dve, nc.vector.tensor_tensor_scan(run_b[:, ::-1], rst_b[:, ::-1], run_a[:, ::-1], 0.0,
                                                           ALU.add, ALU.max))
                    mark(nc.vector.tensor_tensor(run_a[:, :], logit_w[:, :], run_b[:, :], ALU.subtract), s_ex)
                    dve.wait_ge(s_ex, 2)
                    link(dve, nc.vector.tensor_tensor_scan(run_a[:, :], same_w[:, :], run_b[:, :], 0.0,
                                                           ALU.mult, ALU.add))
                    spread(dve, run_a, rst_a)
                    link(dve, nc.vector.reciprocal(rst_b[:, :], rst_a[:, :]))
                    mark(nc.vector.tensor_tensor(weight_w[:, :], run_b[:, :], rst_b[:, :], ALU.mult), s_mk)
                    dve.wait_ge(s_tp, TP_SOFT)
                    link(dve, nc.vector.tensor_copy(wgt_c[:, :, :].rearrange("p s g -> p (s g)"),
                                                    psX[:, 0:SLOTS * NG]))
                with dve.If(general):
                    if k == 2:
                        nc.vector.memset(attr_r[:, :, :], 0.0).then_inc(l_attr, 1)
                        dve.wait_ge(l_rows, 48)
                        dve.sem_inc(l_attr, 1)
                        logits_vector(dve)
                        nc.vector.drain().then_inc(l_attr, 1)
                        dve.wait_ge(l_attr, 3)
                    general_vector(dve, k)
                nc.vector.drain().then_inc(L[k].ready, 1)
                layer_vector(dve, k)


_INS = ['x', 'src', 'dst', 'edge_attr_64', 'L0_gnn_W1l', 'L0_gnn_b1', 'L0_gnn_W1r', 'L0_gnn_W2l', 'L0_gnn_b2',
        'L0_gnn_W2r', 'L1_gnn_W', 'L1_gnn_A']


def kernel(**inputs):
    import concourse.bacc as _bacc
    from concourse.bass_utils import run_bass_kernel_spmd as _run

    nc = _bacc.Bacc("TRN2", target_bir_lowering=False, num_devices=1)
    arrays, args = {}, []
    for name in _INS:
        a = np.ascontiguousarray(inputs[name])
        arrays[f"in_{name}"] = a
        args.append(nc.dram_tensor(f"in_{name}", a.shape, mybir.dt.from_np(a.dtype), kind="ExternalInput").ap())
    shape = inputs['x'].shape
    args.append(nc.dram_tensor("out", tuple(shape), F32, kind="ExternalOutput").ap())
    gnn_program(nc, *args)
    r = _run(nc, [arrays], core_ids=[0])
    return r.results[0]["out"]
```

```python
from contextlib import ExitStack

import numpy as np

import concourse.bass as bass
from concourse import mybir

F32 = mybir.dt.float32
F32R = mybir.dt.float32r
BF16 = mybir.dt.bfloat16
I32 = mybir.dt.int32
ALU = mybir.AluOpType
ACT = mybir.ActivationFunctionType
AX_X = mybir.AxisListType.X

P = 128
QT = 4
U = 2
BT = U * QT
NB = 4
SLOTS = 5
PAIRS = [(b + h, b) for b in range(QT) for h in range(2)]
WIN = SLOTS * P
CH = 16
KCH = WIN // CH
FRONT = P
LN_G = 5
PAD_DST = 52000
SKIP = 1.0e6
BIG = 1.0e30
EPS = 1e-5
ALPHA = 0.2
LQ = 17


class Step:

    def __init__(self, i, j, n, u):
        self.i, self.j, self.n, self.u = i, j, n, u
        self.t = i * u + j

    def at(self, d):
        return Step(self.i + (self.j + d) // self.u, (self.j + d) % self.u, self.n, self.u)

    @property
    def real(self):
        return not isinstance(self.t, int) or 0 <= self.t < self.n

    def after(self, n):
        return not isinstance(self.t, int) or self.t >= n


class Tile(Step):

    def __init__(self, i, j, n, u=U * QT):
        super().__init__(i, j, n, u)
        self.b, self.q = j % QT, j // QT
        self.g = i * U + self.q

    def at(self, d):
        return Tile(self.i + (self.j + d) // self.u, (self.j + d) % self.u, self.n)

    @property
    def reuse(self):
        return self.after(NB)


def drive(eng, kind, n, u, body, lead=0, flush=0, peel=1):
    m = (n - 1 - u) // u
    for t in range(-lead, peel * u):
        body(kind(t // u, t % u, n, u))
    with eng.Fori(peel, m) as i:
        for j in range(u):
            body(kind(i, j, n, u))
    for t in range(u * m, n + flush):
        body(kind(t // u, t % u, n, u))


def uses(n, u, j):
    return (n - j + u - 1) // u


def gnn_program(nc, x, src, dst, edge_attr, W1l, b1, W1r, W2l, b2, W2r, W, A, out):
    N, D = x.shape
    E = src.shape[0]
    ED = edge_attr.shape[1]
    H = D // P
    NT = (N + P - 1) // P
    TAIL = N - (NT - 1) * P
    NP = NT * P
    EC = (E + P - 1) // P
    ETAIL = E - (EC - 1) * P
    EB = 4
    NG = (NT + QT - 1) // QT
    LAST = NG * QT * P
    WPAIR = 2 * P + 1
    NBAT = NG // U
    PADS = 1200
    SR = (FRONT + E + PADS) // CH
    FC = (E + PADS) // CH
    FB = (FC + 511) // 512
    LB = (NT - 1) // LN_G
    assert H == 2 and NG <= P and EC <= EB * P and (NT - 1) % LN_G == 0 and FB <= 7
    assert (FRONT + E + PADS) % CH == 0 and E % CH == 0 and PADS >= WIN and PADS % 16 == 0
    assert NG % U == 0 and EC % LQ == 0 and PAD_DST >= LAST

    ctx = ExitStack()
    with ctx:
        def sb(name, shape, dt=F32):
            return ctx.enter_context(nc.sbuf_tensor(name, shape, dt))

        def sem(name):
            return ctx.enter_context(nc.semaphore(name))

        def dram(name, shape, dt=F32):
            return nc.dram_tensor(name, shape, dt, kind="Internal")

        rows_tab = [dram(f"rows_tab{k}", (NP, D + 2 * (k == 2))) for k in range(3)]
        sums_tab = [dram(f"sums_tab{k}", (NP, D)) for k in range(3)]
        own_tab = [dram(f"own_tab{k}", (NP, D)) for k in range(2)]
        x1_tab = dram("x1_tab", (NP, D))
        src_pad = dram("src_pad", (SR, CH), I32)
        dst_pad = dram("dst_pad", (SR, CH), I32)
        attr_tab = dram("attr_tab", (SR, CH))
        score_src = dram("score_src", (EB * P * P, 1))
        score_dst = dram("score_dst", (EB * P * P, 1))
        pair_tab = dram("pair_tab", (NG * QT, 2, WPAIR))
        maxden = dram("maxden", (NP, 2))

        ident = sb("ident", [P, P])
        lower = sb("lower", [P, P])
        iota_i = sb("iota_i", [P, P], I32)
        iota_n = sb("iota_n", [P, P])
        part_i = sb("part_i", [P, 1], I32)
        part_n = sb("part_n", [P, 1])
        tile0_i = sb("tile0_i", [NG, QT + 1], I32)
        tile0 = sb("tile0", [NG, QT + 1])
        zeros = sb("zeros", [P, D])
        ones = sb("ones", [P, P])
        ones_b = sb("ones_b", [P, P], BF16)
        eps = sb("eps", [P, 1])
        pad_i = sb("pad_i", [16, PADS // 16], I32)
        pad_f = sb("pad_f", [16, FRONT // 16], I32)
        pad_z = sb("pad_z", [16, PADS // 16], I32)

        mats = [W1l, W1r, W2l, W2r, W]
        early_w = sb("early_w", [P, 5 * H * D])
        w_nat = early_w[:, :].rearrange("p (n h d) -> p n h d", n=5, h=H)
        w_hi = sb("w_hi", [P, 4, H, D], F32R)
        w_lo = sb("w_lo", [P, 4, H, D], F32R)
        bias_full = sb("bias_full", [P, 2, D])
        bias_rest = sb("bias_rest", [P, 2, D])
        bias_part = sb("bias_part", [P, 3, 2, D], BF16)
        bias_rows = sb("bias_rows", [P, 2, D], BF16)
        a_col = sb("a_col", [P, 2 * H])
        a_edge = sb("a_edge", [P, ED])
        w_att = sb("w_att", [P, H, D + 2])

        src_rows = sb("src_rows", [P, EB, P], I32)
        dst_rows = sb("dst_rows", [P, EB, P], I32)
        edge_f = sb("edge_f", [P, 2, EB, P])
        src_c = sb("src_c", [P, EB * P], I32)
        dst_c = sb("dst_c", [P, EB * P], I32)
        dst_f = sb("dst_f", [P, EB * P])
        attr_l = sb("attr_l", [125, 400])
        attr_r = sb("attr_r", [P, EB, P])
        logit_c = sb("logit_c", [P, EB * P])

        firsts_i = sb("firsts_i", [1, FC], I32)
        firsts = firsts_i[:, :].bitcast(F32)
        early_s = sb("early_s", [P, 3 * 2 * QT * P + 2 * WIN])
        below = early_s[0:NG, 0:2 * QT * P].rearrange("g (u n) -> g u n", u=2)
        counts = sb("counts", [NG, 2, FB])
        count2 = sb("count2", [NG, 2])
        start_f = sb("start_f", [NG, 1])
        start_i = sb("start_i", [NG, 1], I32)
        chunk_f = sb("chunk_f", [NG, KCH])
        chunk = sb("chunk", [NG, KCH], I32)
        src_w = sb("src_w", [NG, WIN], I32)
        dst_w = sb("dst_w", [NG, WIN], I32)
        attr_w = sb("attr_w", [NG, WIN])
        in_w, valid_w, loc_w = (early_s[0:NG, n * 2 * QT * P:(n + 1) * 2 * QT * P].rearrange("g (b n) -> g b n", n=P)
                                for n in range(3))
        srcf_w, dstf_w = (early_s[0:NG, 6 * QT * P + n * WIN:6 * QT * P + (n + 1) * WIN] for n in range(2))
        arena = sb("arena", [P, 8 * WIN + 4 * P])
        early_z = arena[:, 4 * WIN:8 * WIN]
        any_w, run_a, run_b, weight_w = (early_z[0:NG, n * WIN:(n + 1) * WIN] for n in range(4))
        same_w = sb("same_w", [NG, WIN + 1])
        rst_w = sb("rst_w", [NG, WIN + 1])
        next_w = sb("next_w", [NG, WIN])
        tally = sb("tally", [NG, 2])
        tally1 = sb("tally1", [1, 2])
        general_i = sb("general_i", [1, 1], I32)

        idx_c = sb("idx_c", [P, SLOTS, NG], I32)
        loc_c = sb("loc_c", [P, 2 * QT, NG])
        wgt_c = sb("wgt_c", [P, SLOTS, NG])

        assert 2 * LN_G * D == 4 * WIN
        ln_x = arena[:, 0:4 * WIN].rearrange("p (j g d) -> p j g d", j=2, g=LN_G)
        early_h = sb("early_h", [P, 2 * LN_G * D])
        early_r = sb("early_r", [P, 2 * LN_G * D])
        ln_h = early_h[:, :].rearrange("p (j g d) -> p j g d", j=2, g=LN_G)
        ln_r = early_r[:, :].rearrange("p (j g d) -> p j g d", j=2, g=LN_G)
        ln_z = early_z[:, :].rearrange("p (j g d) -> p j g d", j=2, g=LN_G)
        T_hi = sb("T_hi", [P, 2, D], F32R)
        T_lo = sb("T_lo", [P, 2, D], F32R)
        ln_st = sb("ln_st", [P, 2, LN_G, 6])
        ln_mv = sb("ln_mv", [P, 2, LN_G, 2])
        ln_sd = sb("ln_sd", [P, 2, LN_G])
        ln_rs = sb("ln_rs", [P, 2, LN_G])
        ln_nm = sb("ln_nm", [P, 2, LN_G])

        idx_t = sb("idx_t", [P, U, SLOTS], I32)
        rows = ln_x
        assert U == 2 and SLOTS == LN_G
        row_hi = sb("row_hi", [P, U, SLOTS, D], F32R)
        row_lo = sb("row_lo", [P, U, SLOTS, D], F32R)
        sel = sb("sel", [P, NB, 2, P], F32R)
        early_e = sb("early_e", [P, 4 * 10 * ED])
        ea = early_e[:, 0:20 * ED].rearrange("p (j q e) -> p j q e", j=2, q=10)
        ea_p = early_e[:, 20 * ED:40 * ED].rearrange("p (j q e) -> p j q e", j=2, q=10)
        sel_w = early_e[:, 0:NB * 2 * P].rearrange("p (b h n) -> p b h n", b=NB, h=2)
        xin = early_r[:, 0:NB * D].rearrange("p (b d) -> p b d", b=NB)
        res = early_r[:, NB * D:2 * NB * D].rearrange("p (b d) -> p b d", b=NB)
        h_T = early_h[:, 0:NB * D].rearrange("p (b d) -> p b d", b=NB)
        own_out = early_h[:, NB * D:2 * NB * D].rearrange("p (b d) -> p b d", b=NB)
        x_out = early_w[:, 0:NB * D].rearrange("p (b d) -> p b d", b=NB)
        h_out = early_w[:, NB * D:2 * NB * D].rearrange("p (b d) -> p b d", b=NB)
        z_out = early_e[:, NB * 2 * P:NB * (2 * P + D + 2)].rearrange("p (b d) -> p b d", b=NB)
        t_st = sb("t_st", [P, NB, 6])
        t_mv = sb("t_mv", [P, NB, 2])
        t_sd = sb("t_sd", [P, NB])
        t_rs = sb("t_rs", [P, NB])
        t_nm = sb("t_nm", [P, NB])
        score_c = sb("score_c", [P, 2, EB * P])
        score_r = edge_f

        idx_l = sb("idx_l", [P, 2, 2, LQ], I32)
        got_l = sb("got_l", [P, 2, 2, LQ])
        g_idx = sb("g_idx", [P, 2], I32)
        g_msg = sb("g_msg", [P, D + 2])
        g_acc = sb("g_acc", [P, D])
        g_md = sb("g_md", [P, 2])
        g_new = sb("g_new", [P, D])
        g_mdn = sb("g_mdn", [P, 2])
        g_dst = sb("g_dst", [P, 2])
        g_wide = sb("g_wide", [P, 2, P])
        g_eq = sb("g_eq", [P, P])
        g_t1 = sb("g_t1", [P, P])
        g_t2 = sb("g_t2", [P, P])
        g_wt = sb("g_wt", [P, P])
        g_mx = sb("g_mx", [P, 1])
        g_df = sb("g_df", [P, 2])
        g_ex = sb("g_ex", [P, 2])
        g_rk = sb("g_rk", [P, 1])
        g_to_f = sb("g_to_f", [P, 1])
        g_to = sb("g_to", [P, 1], I32)
        g_init = sb("g_init", [P, 2])
        g_all = early_h[:, 0:2 * NG * QT].rearrange("p (t o) -> p t o", o=2)
        assert 2 * NG * QT <= NB * D

        psA = [ctx.enter_context(nc.psum_tensor(f"psA{j}", [P, 512], F32)) for j in range(2)]
        psB = [ctx.enter_context(nc.psum_tensor(f"psB{j}", [P, 512], F32)) for j in range(4)]
        psX = ctx.enter_context(nc.psum_tensor("psX", [P, 512], F32))
        psY = ctx.enter_context(nc.psum_tensor("psY", [P, 512], F32))
        psT, psZ, psO, psG = psA, psB[0:2], [psX, psY], psB[2:4]
        banks = [psA[0], psA[1], psB[0], psB[1], psB[2], psB[3], psX]

        ring = arena[:, 0:U * U * SLOTS * (D + 2)].rearrange("p (j s d) -> p j s d", j=U, d=D + 2)
        sel_1 = early_s[:, 0:U * BT * P].bitcast(BF16).rearrange("p (j t h n) -> p j t h n", j=U, t=BT, h=2)
        sel_T = early_r[:, 0:NB * P].bitcast(BF16).rearrange("p (b h e) -> p b h e", b=NB, h=2)
        psT_b = [ps[:, 0:P].bitcast(BF16) for ps in psT]
        ident_b = sb("ident_b", [P, P], BF16)
        score_p = edge_f[:, :, :, :].rearrange("p a b c -> p (a b c)")[:, 0:3 * EB * P // 2].bitcast(BF16)\
            .rearrange("p (a t) -> p a t", a=3)
        rest = [logit_c[:, :], attr_r[:, :, :].rearrange("p b c -> p (b c)")]
        dst_e = sb("dst_e", [P, 2 * BT])
        sm_mask = early_w[0:BT, NB * D:NB * D + U * 2 * WPAIR].rearrange("t (j a e) -> t j a e", j=U, a=2)
        sm_a, sm_b, sm_e = (z_out[0:BT, n, 0:2 * P] for n in range(3))
        idx_b = sb("idx_b", [P, U, U, SLOTS], I32)
        attr_c = sb("attr_c", [P, NG, SLOTS])
        s_col = sb("s_col", [P, U, 3, BT], BF16)
        half_c = sb("half_c", [P, U, SLOTS])
        sum_e = sb("sum_e", [P, 2, BT])
        score_e = sb("score_e", [P, 2, BT])
        inv_c = sb("inv_c", [P, 2 * BT])
        w_c = sb("w_c", [P, U, 2 * BT])

        s_const = sem("s_const")
        s_w = sem("s_w")
        s_edges = sem("s_edges")
        s_edges_f = sem("s_edges_f")
        s_pads = sem("s_pads")
        s_firsts = sem("s_firsts")
        s_firsts_f = sem("s_firsts_f")
        s_chunk = sem("s_chunk")
        s_win = sem("s_win")
        s_tp = sem("s_tp")
        s_dv = sem("s_dv")
        s_mk = sem("s_mk")
        s_flag = sem("s_flag")
        s_turn = sem("s_turn")
        s_turn_a = sem("s_turn_a")
        s_turn_p = sem("s_turn_p")
        s_pl = sem("s_pl")
        ln_ld = [sem(f"ln_ld{j}") for j in range(2)]
        ln_stored = [sem(f"ln_stored{j}") for j in range(2)]
        ln_rstored = [sem(f"ln_rstored{j}") for j in range(2)]
        ln_stats = sem("ln_stats")
        ln_aggr = sem("ln_aggr")
        ln_std = sem("ln_std")
        ln_scale = sem("ln_scale")
        ln_rcp = sem("ln_rcp")
        ln_done = sem("ln_done")
        ln_tp = sem("ln_tp")
        ln_hi = sem("ln_hi")
        ln_lo = sem("ln_lo")
        ln_dense = sem("ln_dense")
        ln_r_done = sem("ln_r_done")
        ln_z_done = sem("ln_z_done")

        dve_n = [0]

        def link(eng, ins, s=s_dv, count=dve_n):
            count[0] += 1
            ins.then_inc(s, 1)
            eng.wait_ge(s, count[0])

        class Layer:

            def __init__(self, k):
                self.k = k
                self.idx = sem(f"idx_copied{k}")
                self.rows_ld = [sem(f"rows_ld{k}_{j}") for j in range(U)]
                self.xin_ld = [sem(f"xin_ld{k}_{j}") for j in range(NB)] if k == 0 else None
                self.res_ld = [sem(f"res_ld{k}_{j}") for j in range(NB)]
                self.z_st = [sem(f"z_st{k}_{j}") for j in range(NB)] if k < 2 else None
                self.own_st = [sem(f"own_st{k}_{j}") for j in range(NB)] if k == 0 else None
                self.x_st = [sem(f"x_st{k}_{j}") for j in range(NB)] if k else None
                self.hi = sem(f"row_hi_made{k}") if k == 0 else None
                self.lo = sem(f"row_lo_made{k}") if k == 0 else None
                self.sel = sem(f"sel_made{k}")
                self.aggregated = sem(f"aggregated{k}")
                self.x = sem(f"x_made{k}")
                if k < 2:
                    self.h = sem(f"h_made{k}")
                    self.transposed = sem(f"h_transposed{k}")
                    self.operand = sem(f"h_T_copied{k}")
                    self.dense = sem(f"dense{k}")
                    self.z = sem(f"z_copied{k}")
                if k == 0:
                    self.low = sem("T_lo_made")
                    self.own = sem("own_made")
                self.ready = sem(f"windows_ready{k}")

        L = [Layer(k) for k in range(3)]
        ln2_stats = sem("ln2_stats")
        ln2_aggr = sem("ln2_aggr")
        ln2_std = sem("ln2_std")
        ln2_rcp = sem("ln2_rcp")
        ln2_scale = sem("ln2_scale")
        sc_kept = sem("sc_kept")
        s_score = sem("s_score")
        s_score_v = sem("s_score_v")
        s_score_st = sem("s_score_st")
        l_idx = sem("l_idx")
        l_got = [sem(f"l_got{j}") for j in range(2)]
        l_dv = sem("l_dv")
        a_ea = [sem(f"a_ea{j}") for j in range(2)]
        a_dv = sem("a_dv")
        l_tp = sem("l_tp")
        l_rows = sem("l_rows")
        l_attr = sem("l_attr")
        a_st = sem("a_st")
        a_win = sem("a_win")
        s_parts = sem("s_parts")
        s_runs = sem("s_runs")
        s_runs_st = sem("s_runs_st")
        a_mask = [sem(f"a_mask{j}") for j in range(U)]
        a_idx = sem("a_idx")
        a_sel = sem("a_sel")
        a_tp = sem("a_tp")
        a_cp = sem("a_cp")
        a_dst = sem("a_dst")
        a_half = sem("a_half")
        a_sum = sem("a_sum")
        a_row = sem("a_row")
        a_chain = sem("a_chain")
        a_exp = sem("a_exp")
        a_cols = sem("a_cols")
        a_inv = sem("a_inv")
        a_w = sem("a_w")

        def table_written(eng, k):
            if k == 0:
                for j in range(2):
                    eng.wait_ge(ln_stored[j], 16 * uses(LB + 1, 2, j))
            else:
                for j in range(NB):
                    eng.wait_ge(L[k - 1].z_st[j], 16 * uses(NT, NB, j))

        g_inited = sem("g_inited")
        g_set = sem("g_set")
        g_indexed = sem("g_indexed")
        g_got = sem("g_got")
        g_put = sem("g_put")
        g_dve = sem("g_dve")
        g_pe = sem("g_pe")
        g_act = sem("g_act")
        g_den = sem("g_den")
        g_fin = sem("g_fin")
        GDV = 17

        def general_sync(sp, k):
            c0 = k * EC
            sp.wait_ge(g_set, 2 * k + 1)
            sp.dma_start(sums_tab[k][:, :].rearrange("(t p) d -> p t d", p=P),
                         zeros[:, :].unsqueeze(1).to_broadcast([P, NT, D])).then_inc(g_inited, 16)
            sp.dma_start(maxden[:, :].rearrange("(t p) d -> p t d", p=P),
                         g_init[:, :].unsqueeze(1).to_broadcast([P, NT, 2]),
                         allow_slow_non_contiguous=True).then_inc(g_inited, 16)
            sp.wait_ge(g_put, 32 * (c0 + EC))
            sp.wait_ge(g_fin, 3 * k + 1)
            sp.dma_start(g_all[:, 0:NT, :], maxden[:, :].rearrange("(t p) d -> p t d", p=P),
                         allow_slow_non_contiguous=True).then_inc(g_den, 16)

        def general_pool(pool, k):
            c0 = k * EC
            pool.wait_ge(g_inited, 32 * (k + 1))
            pool.wait_ge(g_set, 2 * k + 2)
            last_row = pool.to_reg(NP - 1)
            with pool.Fori(0, EC) as c:
                nc.gpsimd.tensor_copy(g_idx[:, 0:1], src_c[:, bass.ds(c, 1)])
                nc.gpsimd.tensor_copy(g_idx[:, 1:2], dst_c[:, bass.ds(c, 1)]).then_inc(g_indexed, 1)
                pool.wait_ge(g_indexed, c + (c0 + k + 1))
                pool.sem_inc(s_turn, 1)
                for buf, tab, n in ((g_msg if k == 2 else g_msg[:, 0:D], rows_tab[k], 0), (g_md, maxden, 1), (g_acc, sums_tab[k], 1)):
                    nc.gpsimd.indirect_dma_start(
                        out=buf[:, :], out_offset=None, in_=tab[:, :],
                        in_offset=bass.IndirectOffsetOnAxis(ap=g_idx[:, n:n + 1], axis=0),
                        bounds_check=last_row, oob_is_err=False).then_inc(g_got, 16)
                pool.wait_ge(g_dve, GDV * (c + (c0 + 1)))
                pool.sem_inc(s_turn, 1)
                for buf, tab in ((g_mdn, maxden), (g_new, sums_tab[k])):
                    nc.gpsimd.indirect_dma_start(
                        out=tab[:, :], out_offset=bass.IndirectOffsetOnAxis(ap=g_to[:, 0:1], axis=0),
                        in_=buf[:, :], in_offset=None,
                        bounds_check=last_row, oob_is_err=False).then_inc(g_put, 16)
                pool.wait_ge(g_put, 32 * (c + (c0 + 1)))
            pool.wait_ge(g_put, 32 * (c0 + EC))
            nc.gpsimd.memset(idx_c[:, :, :], SKIP)
            nc.gpsimd.memset(wgt_c[:, :, :], 1.0)
            nc.gpsimd.memset(g_all[:, :, :], 1.0)
            nc.gpsimd.memset(loc_c[:, :, :], -1.0).then_inc(g_indexed, 1)
            pool.wait_ge(g_indexed, c0 + k + EC + 1)
            nc.gpsimd.iota(idx_c[:, 0:QT, :], pattern=[[P, QT], [QT * P, NG]], base=0,
                           channel_multiplier=1).then_inc(g_fin, 1)

        def general_tensor(pe, k):
            c0 = k * EC
            with pe.Fori(0, EC) as c:
                pe.wait_ge(g_dve, GDV * (c + c0) + 2)
                nc.tensor.transpose(psX[:, 0:P], g_wide[:, 0, :], ident[:, :])
                nc.tensor.transpose(psX[:, P:2 * P], g_wide[:, 1, :], ident[:, :]).then_inc(g_pe, 1)
                pe.wait_ge(g_dve, GDV * (c + c0) + 11)
                pe.wait_ge(g_got, 48 * (c + (c0 + 1)))
                nc.tensor.matmul(psY[:, 0:D], g_wt[:, :], g_msg[:, 0:D], start=True, stop=True)
                nc.tensor.matmul(psY[:, D:D + 1], g_wt[:, :], ones[:, 0:1], start=True,
                                 stop=True).then_inc(g_pe, 1)

        def general_scalar(act, k):
            c0 = k * EC
            with act.Fori(0, EC) as c:
                act.wait_ge(g_dve, GDV * (c + c0) + 10)
                nc.scalar.activation(g_ex[:, :], g_df[:, :], ACT.Exp).then_inc(g_act, 1)

        def general_vector(dve, k):
            c0 = k * EC
            nc.vector.memset(g_init[:, 0:1], -BIG)
            nc.vector.memset(g_init[:, 1:2], 0.0).then_inc(g_set, 1)
            nc.vector.memset(g_msg[:, :], 0.0)
            nc.vector.memset(g_acc[:, :], 0.0)
            nc.vector.memset(g_md[:, :], 0.0)
            if k < 2:
                nc.vector.memset(logit_c[:, :], 0.0)
            nc.vector.drain().then_inc(g_set, 1)
            dve.wait_ge(g_set, 2 * k + 2)
            with dve.Fori(0, EC) as c:
                n = [0]

                def step(ins, wait=True):
                    n[0] += 1
                    ins.then_inc(g_dve, 1)
                    if wait:
                        dve.wait_ge(g_dve, GDV * (c + c0) + n[0])

                step(nc.vector.tensor_scalar(g_wide[:, 0, :], dst_f[:, bass.ds(c, 1)].to_broadcast([P, P]), 0.0,
                                             None, ALU.add), False)
                step(nc.vector.tensor_copy(g_wide[:, 1, :], logit_c[:, bass.ds(c, 1)].to_broadcast([P, P])), False)
                step(nc.vector.tensor_copy(g_dst[:, 0:1], dst_f[:, bass.ds(c, 1)]), False)
                step(nc.vector.tensor_copy(g_dst[:, 1:2], logit_c[:, bass.ds(c, 1)]))
                dve.wait_ge(g_pe, 2 * (c + c0) + 1)
                step(nc.vector.tensor_scalar(g_eq[:, :], psX[:, 0:P], g_dst[:, 0:1], None, ALU.is_equal))
                nc.vector.tensor_scalar(g_t1[:, :], g_eq[:, :], -1.0, BIG, ALU.add, ALU.mult)
                step(nc.vector.tensor_tensor(g_t2[:, :], g_eq[:, :], psX[:, P:2 * P], ALU.mult))
                step(nc.vector.tensor_tensor(g_t1[:, :], g_t1[:, :], g_t2[:, :], ALU.add))
                step(nc.vector.tensor_reduce(g_mx[:, :], g_t1[:, :], AX_X, ALU.max))
                dve.wait_ge(g_got, 48 * (c + (c0 + 1)))
                step(nc.vector.tensor_tensor(g_mdn[:, 0:1], g_mx[:, :], g_md[:, 0:1], ALU.max))
                nc.vector.tensor_tensor(g_df[:, 0:1], g_dst[:, 1:2], g_mdn[:, 0:1], ALU.subtract)
                step(nc.vector.tensor_tensor(g_df[:, 1:2], g_md[:, 0:1], g_mdn[:, 0:1], ALU.subtract))
                dve.wait_ge(g_act, c + (c0 + 1))
                step(nc.vector.tensor_scalar(g_wt[:, :], g_eq[:, :], g_ex[:, 0:1], None, ALU.mult))
                step(nc.vector.tensor_tensor(g_t2[:, :], g_eq[:, :], lower[:, :], ALU.mult))
                step(nc.vector.tensor_reduce(g_rk[:, :], g_t2[:, :], AX_X, ALU.max))
                step(nc.vector.scalar_tensor_tensor(g_to_f[:, 0:1], g_rk[:, :], SKIP, g_dst[:, 0:1],
                                                    ALU.mult, ALU.add))
                step(nc.vector.tensor_copy(g_to[:, 0:1], g_to_f[:, 0:1]))
                dve.wait_ge(g_pe, 2 * (c + c0) + 2)
                step(nc.vector.scalar_tensor_tensor(g_new[:, :], g_acc[:, :], g_ex[:, 1:2], psY[:, 0:D],
                                                    ALU.mult, ALU.add))
                step(nc.vector.scalar_tensor_tensor(g_mdn[:, 1:2], g_md[:, 1:2], g_ex[:, 1:2],
                                                    psY[:, D:D + 1], ALU.mult, ALU.add), False)
                assert n[0] == GDV
                dve.wait_ge(g_put, 32 * (c + (c0 + 1)))
            dve.wait_ge(g_den, 16 * (k + 1))
            dve.wait_ge(g_fin, 3 * k + 1)
            nc.vector.tensor_scalar(g_all[:, :, 1], g_all[:, :, 1], 0.5, None, ALU.max).then_inc(g_fin, 1)
            dve.wait_ge(g_fin, 3 * k + 2)
            by_tile = g_all[:, :, 1].rearrange("p (g b) -> p b g", b=QT)
            for b in range(QT):
                nc.vector.reciprocal(wgt_c[:, b, :], by_tile[:, b, :])
                last = nc.vector.tensor_copy(loc_c[:, 2 * b, :], part_n[:, 0:1].to_broadcast([P, NG]))
            last.then_inc(g_fin, 1)
            dve.wait_ge(g_fin, 3 * k + 3)

        def is_general(eng):
            eng.wait_ge(s_flag, 1)
            return eng.value_load(general_i[0:1, 0:1], min_val=0, max_val=1) != 0

        def layer_sync(sp, k):
            y = L[k]
            d = int(k == 1)

            def load_res(T):
                if T.reuse:
                    sp.wait_ge(y.x, T.t - NB + 1)
                tab = (own_tab[0], own_tab[1], x1_tab)[k]
                sp.dma_start(res[:, T.b, :], tab[bass.ds(T.t * P, P), :]).then_inc(y.res_ld[T.b], 16)

            def load_x(T):
                if T.reuse:
                    sp.wait_ge(y.own, T.t - NB + 1)
                last = isinstance(T.t, int) and T.t == NT - 1
                n = TAIL if last else P
                sp.dma_start(xin[0:n, T.b, :], x[bass.ds(T.t * P, n), :]).then_inc(y.xin_ld[T.b], 16)

            def store_z(T):
                sp.wait_ge(y.z, T.t + 1)
                sp.dma_start(rows_tab[k + 1][bass.ds(T.t * P, P), :], z_out[:, T.b, 0:D + 2 * k]).then_inc(y.z_st[T.b], 16)

            def store_own(T):
                sp.wait_ge(y.own, T.t + 1)
                sp.dma_start(own_tab[1][bass.ds(T.t * P, P), :], own_out[:, T.b, :]).then_inc(y.own_st[T.b], 16)

            def store_x(T):
                last = isinstance(T.t, int) and T.t == NT - 1
                n = TAIL if last and k == 2 else P
                tab = x1_tab if k == 1 else out
                sp.wait_ge(y.x, T.t + 1)
                sp.dma_start(tab[bass.ds(T.t * P, n), :], x_out[0:n, T.b, :]).then_inc(y.x_st[T.b], 16)

            def body(T):
                if T.real and k > 0:
                    store_x(T)
                if T.at(NB).real:
                    load_res(T.at(NB))
                Z = T.at(-4 - d)
                if k < 2 and Z.real:
                    store_z(Z)
                    if k == 0:
                        store_own(Z)
                if k == 0 and T.real:
                    load_x(T)

            if k == 0:
                for j in range(2):
                    sp.wait_ge(ln_rstored[j], 16 * uses(LB + 1, 2, j))
            for j in range(NB):
                if k == 1:
                    sp.wait_ge(L[0].own_st[j], 16 * uses(NT, NB, j))
                if k == 2:
                    sp.wait_ge(L[1].x_st[j], 16 * uses(NT, NB, j))
            for t in range(NB):
                load_res(Tile(0, t, NT))
            drive(sp, Tile, NT, U * QT, body, flush=4 + d)

        def layer_pool(pool, k, tab):
            y = L[k]
            last_row = pool.to_reg(NP - 1)

            def body(G):
                if G.after(U):
                    pool.wait_ge(y.rows_ld[G.j], 16 * SLOTS * G.i)
                    pool.sem_inc(s_turn, 1)
                nc.gpsimd.tensor_copy(idx_t[:, G.j, :], idx_c[:, :, bass.ds(G.t, 1)].rearrange("p s o -> p (s o)"))\
                    .then_inc(y.idx, 1)
                pool.wait_ge(y.idx, G.t + 1)
                for s in range(SLOTS):
                    if G.after(U):
                        if k == 0:
                            pool.wait_ge(y.lo, (G.t - U) * SLOTS + s + 1)
                        else:
                            pool.wait_ge(y.aggregated, (G.t - U) * QT + min(s + 1, QT))
                    pool.sem_inc(s_turn, 1)
                    nc.gpsimd.indirect_dma_start(
                        out=rows[:, G.j, s, :], out_offset=None, in_=tab[:, :],
                        in_offset=bass.IndirectOffsetOnAxis(ap=idx_t[:, G.j, s:s + 1], axis=0),
                        bounds_check=last_row, oob_is_err=False).then_inc(y.rows_ld[G.j], 16)

            pool.wait_ge(y.ready, 1)
            drive(pool, Step, NG, U, body)

        def split_slots(T):
            return ((0, 1), (2,), (3,), (4,))[T.b]

        def dense_parts(pe, par, m, bias):
            for f in range(H):
                cols = slice(f * P, (f + 1) * P)
                for n, (left, right) in enumerate(((T_hi, w_hi), (T_hi, w_lo), (T_lo, w_hi))):
                    for i, ps in enumerate((psZ, psO)):
                        nc.tensor.matmul(ps[par][:, 0:D], left[:, par, cols], right[:, m + i, f, :],
                                         start=(f == 0 and n == 0), stop=(f == H - 1 and n == 2 and i == 0))
            return nc.tensor.matmul(psO[par][:, 0:D], ones_b[:, :], bias_rows[:, bias, :], start=False, stop=True)

        def layer_tensor(pe, k):
            y = L[k]
            d = int(k == 1)

            def aggregate(T):
                pe.wait_ge(y.sel, T.t + 1)
                if k == 0:
                    pe.wait_ge(y.lo, T.g * SLOTS + T.b + 2)
                else:
                    pe.wait_ge(y.rows_ld[T.q], 16 * SLOTS * (T.i + 1))
                if T.after(2):
                    pe.wait_ge(y.x, T.t - 1)
                n = 0
                for h in range(2):
                    for part in (row_hi, row_lo) if k == 0 else (rows,):
                        mat = (sel_w if k else sel)[:, T.b, h, :]
                        last = nc.tensor.matmul(psG[T.b % 2][:, 0:D], mat, part[:, T.q, T.b + h, :],
                                                start=(n == 0), stop=(n == (3 if k == 0 else 1)))
                        n += 1
                last.then_inc(y.aggregated, 1)

            def transposes(T):
                pe.wait_ge(y.h, T.t + 1)
                if T.after(2):
                    pe.wait_ge(y.operand if k else y.low, T.t - 1)
                for f in range(H):
                    last = nc.tensor.transpose(psT[T.b % 2][:, f * P:(f + 1) * P], h_out[:, T.b, f * P:(f + 1) * P],
                                               ident[:, :])
                last.then_inc(y.transposed, 1)

            def products(T):
                pe.wait_ge(y.operand if k else y.low, T.t + 1)
                if T.after(2):
                    pe.wait_ge(y.z, T.t - 1)
                    if k == 0:
                        pe.wait_ge(y.own, T.t - 1)
                if k == 0:
                    last = dense_parts(pe, T.b % 2, 2, 1)
                else:
                    for f in range(H):
                        last = nc.tensor.matmul(psZ[T.b % 2][:, 0:D + 2], h_T[:, T.b, f * P:(f + 1) * P],
                                                w_att[:, f, :], start=(f == 0), stop=(f == H - 1))
                last.then_inc(y.dense, 1)

            def body(T):
                if T.at(1).real:
                    aggregate(T.at(1))
                if k < 2 and T.at(-1 - d).real:
                    transposes(T.at(-1 - d))
                if k < 2 and T.at(-2 - d).real:
                    products(T.at(-2 - d))

            if k:
                pe.wait_ge(L[k - 1].x, NT)
            drive(pe, Tile, NT, U * QT, body, lead=1, flush=2 + d if k < 2 else 0)

        def layer_scalar(act, k):
            y = L[k]
            d = int(k == 1)

            def split(T):
                G = T.at(QT)
                for s in split_slots(T):
                    if s == 0:
                        act.wait_ge(y.rows_ld[G.q], 16 * SLOTS * (G.i + 1))
                        if G.after(U * QT):
                            act.wait_ge(y.aggregated, (G.g - U + 1) * QT)
                        act.sem_inc(s_turn_a, 1)
                    nc.scalar.activation(row_hi[:, G.q, s, :], rows[:, G.q, s, :], ACT.Copy,
                                         scale=wgt_c[:, s, bass.ds(G.g, 1)]).then_inc(y.hi, 1)

            def std(T):
                act.wait_ge(ln2_aggr, T.t + 1)
                nc.scalar.activation(t_sd[:, T.b:T.b + 1], t_mv[:, T.b, 1:2], ACT.Sqrt,
                                     bias=eps[:, 0:1]).then_inc(ln2_std, 1)

            def make_h(T):
                act.wait_ge(ln2_scale if k else y.x, T.t + 1)
                if T.reuse:
                    act.wait_ge(y.transposed, T.t - NB + 1)
                if k:
                    nc.scalar.activation(h_out[:, T.b, :], x_out[:, T.b, :], ACT.Relu, bias=t_nm[:, T.b:T.b + 1],
                                         scale=t_rs[:, T.b:T.b + 1]).then_inc(y.h, 1)
                else:
                    nc.scalar.activation(h_out[:, T.b, :], x_out[:, T.b, :], ACT.Relu).then_inc(y.h, 1)

            def copy_operand(T):
                act.wait_ge(y.transposed, T.t + 1)
                n = NB if k else 2
                if T.after(n):
                    act.wait_ge(y.dense, T.t - n + 1)
                to = h_T[:, T.b, :] if k else T_hi[:, T.b % 2, :]
                nc.scalar.activation(to, psT[T.b % 2][:, 0:D], ACT.Copy).then_inc(y.operand, 1)

            def copy_z(T):
                n = D + 2 * k
                act.wait_ge(y.dense, T.t + 1)
                if T.reuse:
                    act.wait_ge(y.z_st[T.b], 16 * T.g)
                    if k:
                        act.wait_ge(sc_kept, T.t - NB + 1)
                nc.scalar.activation(z_out[:, T.b, 0:n], psZ[T.b % 2][:, 0:n], ACT.Copy).then_inc(y.z, 1)

            def body(T):
                if k == 0 and T.at(QT - T.b).real:
                    split(T)
                if k == 1 and T.at(-1).real:
                    std(T.at(-1))
                if T.at(-1 - d).real:
                    copy_operand(T.at(-1 - d))
                if T.at(-d).real:
                    make_h(T.at(-d))
                if T.at(-3 - d).real:
                    copy_z(T.at(-3 - d))

            if k == 1:
                act.wait_ge(L[0].dense, NT)
                table_written(act, 1)
            act.wait_ge(y.ready, 1)
            drive(act, Tile, NT, U * QT, body, lead=QT if k == 0 else 0, flush=3 + d)

        def layer_vector(dve, k):
            y = L[k]

            def split(T):
                G = T.at(QT)
                for s in split_slots(T):
                    dve.wait_ge(y.hi, G.g * SLOTS + s + 1)
                    nc.vector.scalar_tensor_tensor(row_lo[:, G.q, s, :], rows[:, G.q, s, :],
                                                   wgt_c[:, s, bass.ds(G.g, 1)],
                                                   row_hi[:, G.q, s, :].bitcast(F32),
                                                   ALU.mult, ALU.subtract).then_inc(y.lo, 1)

            def select(T):
                if T.reuse:
                    dve.wait_ge(y.aggregated, T.t - NB + 1)
                for h in range(2):
                    loc = loc_c[:, 2 * T.b + h, bass.ds(T.g, 1)]
                    if k == 0:
                        last = nc.vector.tensor_scalar(sel[:, T.b, h, :], iota_n[:, :], loc, None, ALU.is_equal)
                    else:
                        last = nc.vector.tensor_scalar(sel_w[:, T.b, h, :], iota_n[:, :], loc,
                                                       wgt_c[:, T.b + h, bass.ds(T.g, 1)], ALU.is_equal, ALU.mult)
                last.then_inc(y.sel, 1)

            def add_residual(T):
                dve.wait_ge(y.aggregated, T.t + 1)
                dve.wait_ge(y.res_ld[T.b], 16 * (T.g + 1))
                if T.reuse:
                    if k:
                        dve.wait_ge(y.x_st[T.b], 16 * T.g)
                    if k < 2:
                        dve.wait_ge(y.h, T.t - NB + 1)
                nc.vector.tensor_tensor(x_out[:, T.b, :], psG[T.b % 2][:, 0:D], res[:, T.b, :], ALU.add)\
                    .then_inc(y.x, 1)

            def make_low(T):
                dve.wait_ge(y.operand, T.t + 1)
                nc.vector.tensor_tensor(T_lo[:, T.b % 2, :], psT[T.b % 2][:, 0:D], T_hi[:, T.b % 2, :].bitcast(F32),
                                        ALU.subtract).then_inc(y.low, 1)

            def make_own(T):
                dve.wait_ge(y.dense, T.t + 1)
                dve.wait_ge(y.xin_ld[T.b], 16 * (T.g + 1))
                if T.reuse:
                    dve.wait_ge(y.own_st[T.b], 16 * T.g)
                nc.vector.tensor_tensor(own_out[:, T.b, :], psO[T.b % 2][:, 0:D], xin[:, T.b, :], ALU.add)\
                    .then_inc(y.own, 1)

            def scale(T):
                dve.wait_ge(ln2_std, T.t + 1)
                nc.vector.reciprocal(t_rs[:, T.b:T.b + 1], t_sd[:, T.b:T.b + 1]).then_inc(ln2_rcp, 1)
                dve.wait_ge(ln2_rcp, T.t + 1)
                nc.vector.scalar_tensor_tensor(t_nm[:, T.b:T.b + 1], t_mv[:, T.b, 0:1], -1.0,
                                               t_rs[:, T.b:T.b + 1], ALU.mult, ALU.mult).then_inc(ln2_scale, 1)

            def keep_scores(T):
                dve.wait_ge(y.z, T.t + 1)
                nc.vector.tensor_scalar(score_c[:, :, bass.ds(T.t, 1)].rearrange("p a o -> p (a o)"),
                                        z_out[:, T.b, D:D + 2], 0.0, None, ALU.add).then_inc(sc_kept, 1)

            def body(T):
                if T.real:
                    add_residual(T)
                if k == 1 and T.at(-1).real:
                    scale(T.at(-1))
                if k == 1 and T.real:
                    dve.wait_ge(y.x, T.t + 1)
                    nc.vector.bn_stats(t_st[:, T.b, :], x_out[:, T.b, :]).then_inc(ln2_stats, 1)
                if T.at(3).real:
                    select(T.at(3))
                if k == 1 and T.real:
                    dve.wait_ge(ln2_stats, T.t + 1)
                if k == 1 and T.at(-5).real:
                    keep_scores(T.at(-5))
                if k == 1 and T.real:
                    nc.vector.bn_aggr(t_mv[:, T.b, :], t_st[:, T.b, :]).then_inc(ln2_aggr, 1)
                if k == 0 and T.at(QT - T.b).real:
                    split(T)
                if k == 0 and T.at(-1).real:
                    make_low(T.at(-1))
                if k == 0 and T.at(-3).real:
                    make_own(T.at(-3))

            if k:
                dve.wait_ge(L[k - 1].aggregated, NT)
                dve.wait_ge(L[k - 1].h, NT)
            if k == 2:
                for j in range(NB):
                    dve.wait_ge(L[1].x_st[j], 16 * uses(NT, NB, j))
            drive(dve, Tile, NT, U * QT, body, lead=QT, flush=(3, 5, 0)[k])

        def ln_rows(T):
            last = isinstance(T.t, int) and T.t == LB
            return (1, TAIL) if last else (LN_G, P)

        def ln_slice(tab, T):
            g, n = ln_rows(T)
            return tab[bass.ds(T.t * (LN_G * P), g * n), :].rearrange("(g p) d -> p g d", p=n)

        def ln_sync(sp):
            def load(T):
                if not T.real:
                    return
                g, n = ln_rows(T)
                if T.after(2):
                    sp.wait_ge(ln_done, (T.t - 1) * LN_G)
                sp.dma_start(ln_x[0:n, T.j, 0:g, :], ln_slice(x, T)).then_inc(ln_ld[T.j], 16)

            def body(T):
                B = T.at(-1)
                if T.real:
                    load(T.at(2))
                if B.real:
                    g, n = ln_rows(B)
                    sp.wait_ge(ln_r_done, B.t * LN_G + g)
                    to = own_tab[0][bass.ds(B.t * (LN_G * P), g * P), :].rearrange("(g p) d -> p g d", p=P)
                    sp.dma_start(to, ln_r[:, B.j, 0:g, :]).then_inc(ln_rstored[B.j], 16)
                    sp.wait_ge(ln_z_done, B.t * LN_G + g)
                    to = rows_tab[0][bass.ds(B.t * (LN_G * P), g * P), :].rearrange("(g p) d -> p g d", p=P)
                    sp.dma_start(to, ln_z[:, B.j, 0:g, :]).then_inc(ln_stored[B.j], 16)

            for t in range(2):
                load(Step(0, t, LB + 1, 2))
            drive(sp, Step, LB + 1, 2, body, flush=1, peel=2)

        def ln_vector(dve):
            def copy_own(T, a):
                dve.wait_ge(ln_dense, T.t * LN_G + a + 1)
                if a == 0 and T.after(2):
                    dve.wait_ge(ln_rstored[T.j], 16 * T.i)
                nc.vector.tensor_copy(ln_r[:, T.j, a, :], psO[(T.j * LN_G + a) % 2][:, 0:D]).then_inc(ln_r_done, 1)

            def body(T):
                B = T.at(-1)
                if B.real:
                    g, n = ln_rows(B)
                    dve.wait_ge(ln_std, B.t + 1)
                    if B.after(2):
                        dve.wait_ge(ln_done, (B.t - 1) * LN_G)
                    nc.vector.reciprocal(ln_rs[0:n, B.j, 0:g], ln_sd[0:n, B.j, 0:g]).then_inc(ln_rcp, 1)
                    dve.wait_ge(ln_rcp, B.t + 1)
                    nc.vector.scalar_tensor_tensor(ln_nm[0:n, B.j, 0:g], ln_mv[0:n, B.j, 0:g, 0], -1.0,
                                                   ln_rs[0:n, B.j, 0:g], ALU.mult, ALU.mult).then_inc(ln_scale, 1)
                C, Z = T.at(-2), T.at(-3)
                for a in range(LN_G):
                    now = [b for b in ((), (0, 1), (2, 3), (4,), ())[a] if T.real and b < ln_rows(T)[0]]
                    if now:
                        g, n = ln_rows(T)
                        dve.wait_ge(ln_ld[T.j], 16 * (T.i + 1))
                        for b in now:
                            last = nc.vector.bn_stats(ln_st[0:n, T.j, b, :], ln_x[0:n, T.j, b, :])
                        if now[-1] == g - 1:
                            last.then_inc(ln_stats, 1)
                            dve.wait_ge(ln_stats, T.t + 1)
                    if C.real and a < ln_rows(C)[0]:
                        dve.wait_ge(ln_hi, C.t * LN_G + a + 1)
                        par = (C.j * LN_G + a) % 2
                        nc.vector.tensor_tensor(T_lo[:, par, :], psT[par][:, 0:D], T_hi[:, par, :].bitcast(F32),
                                                ALU.subtract).then_inc(ln_lo, 1)
                    if now and now[-1] == g - 1:
                        for b in range(g):
                            last = nc.vector.bn_aggr(ln_mv[0:n, T.j, b, :], ln_st[0:n, T.j, b, :])
                        last.then_inc(ln_aggr, 1)
                    if a == 0 and Z.real:
                        copy_own(Z, ln_rows(Z)[0] - 1)
                    if a and C.real and a < ln_rows(C)[0]:
                        copy_own(C, a - 1)

            drive(dve, Step, LB + 1, 2, body, flush=3, peel=2)

        def ln_tensor(pe):
            def transposes(T, a):
                par = (T.j * LN_G + a) % 2
                n = T.t * LN_G + a
                pe.wait_ge(ln_done, n + 1)
                if a >= 2 or T.after(1):
                    pe.wait_ge(ln_lo, n - 1)
                for f in range(H):
                    last = nc.tensor.transpose(psA[par][:, f * P:(f + 1) * P],
                                               ln_h[:, T.j, a, f * P:(f + 1) * P], ident[:, :])
                last.then_inc(ln_tp, 1)

            def product(T, a):
                par = (T.j * LN_G + a) % 2
                n = T.t * LN_G + a
                pe.wait_ge(ln_lo, n + 1)
                if a >= 2 or T.after(1):
                    pe.wait_ge(ln_r_done, n - 1)
                    pe.wait_ge(ln_z_done, n - 1)
                last = dense_parts(pe, par, 0, 0)
                last.then_inc(ln_dense, 1)

            def body(T):
                if T.real:
                    for a in range(ln_rows(T)[0]):
                        transposes(T, a)
                        if a:
                            product(T, a - 1)
                        elif T.at(-1).real:
                            product(T.at(-1), ln_rows(T.at(-1))[0] - 1)
                elif T.at(-1).real:
                    product(T.at(-1), ln_rows(T.at(-1))[0] - 1)

            drive(pe, Step, LB + 1, 2, body, flush=1, peel=2)

        def ln_scalar(act):
            def copy_z(T, a):
                act.wait_ge(ln_dense, T.t * LN_G + a + 1)
                if a == 0 and T.after(2):
                    act.wait_ge(ln_stored[T.j], 16 * T.i)
                nc.scalar.activation(ln_z[:, T.j, a, :], psZ[(T.j * LN_G + a) % 2][:, 0:D], ACT.Copy)\
                    .then_inc(ln_z_done, 1)

            def body(T):
                B, C, Z = T.at(-1), T.at(-2), T.at(-3)
                for a in range(LN_G):
                    if C.real and a < ln_rows(C)[0]:
                        n = C.t * LN_G + a
                        act.wait_ge(ln_tp, n + 1)
                        if a >= 2 or C.after(1):
                            act.wait_ge(ln_dense, n - 1)
                        par = (C.j * LN_G + a) % 2
                        nc.scalar.activation(T_hi[:, par, :], psT[par][:, 0:D], ACT.Copy).then_inc(ln_hi, 1)
                    if a == 0 and Z.real:
                        copy_z(Z, ln_rows(Z)[0] - 1)
                    if a and C.real and a < ln_rows(C)[0]:
                        copy_z(C, a - 1)
                    if a == 0 and B.real:
                        act.wait_ge(ln_scale, B.t + 1)
                        if B.after(2):
                            act.wait_ge(ln_tp, (B.t - 1) * LN_G)
                    for b in ((0, 1), (2, 3), (4,), (), ())[a]:
                        if B.real and b < ln_rows(B)[0]:
                            g, n = ln_rows(B)
                            nc.scalar.activation(ln_h[0:n, B.j, b, :], ln_x[0:n, B.j, b, :], ACT.Relu,
                                                 bias=ln_nm[0:n, B.j, b:b + 1], scale=ln_rs[0:n, B.j, b:b + 1])\
                                .then_inc(ln_done, 1)
                if T.real:
                    g, n = ln_rows(T)
                    act.wait_ge(ln_aggr, T.t + 1)
                    nc.scalar.activation(ln_sd[0:n, T.j, 0:g], ln_mv[0:n, T.j, 0:g, 1], ACT.Sqrt,
                                         bias=eps[0:n, 0:1]).then_inc(ln_std, 1)

            act.wait_ge(s_const, 1)
            drive(act, Step, LB + 1, 2, body, flush=3, peel=2)

        AR, AQ = 125, 10
        AN = E // AR // AQ
        ALINKS = ED.bit_length()
        assert AR * AQ * AN == E and AN % 2 == 0

        def attr_pool(pool):
            by_part = edge_attr.rearrange("(p c) d -> p c d", p=AR)

            def load(q, j):
                nc.gpsimd.dma_start(ea[0:AR, j, :, :], by_part[:, bass.ds(q * AQ, AQ), :]).then_inc(a_ea[j], 16)

            def step(i, j, q, more):
                pool.wait_ge(a_ea[j], 16 * (i + 1))
                nc.gpsimd.tensor_tensor(ea_p[0:AR, j, :, :], ea[0:AR, j, :, :],
                                        a_edge[0:AR, :].unsqueeze(1).to_broadcast([AR, AQ, ED]),
                                        ALU.mult).then_inc(a_dv, 1)
                n, w = 1, ED // 2
                while w:
                    pool.wait_ge(a_dv, ALINKS * q + n)
                    if w == 1:
                        pool.sem_inc(s_turn, 1)
                    to = ea_p[0:AR, j, :, 0:w] if w > 1 else attr_l[0:AR, bass.ds(q * AQ, AQ)].unsqueeze(2)
                    nc.gpsimd.tensor_tensor(to, ea_p[0:AR, j, :, 0:w], ea_p[0:AR, j, :, w:2 * w],
                                            ALU.add).then_inc(a_dv, 1)
                    n, w = n + 1, w // 2
                assert n == ALINKS
                if more:
                    load(q + 2, j)

            pool.wait_ge(s_w, 16 * 9)
            for j in range(2):
                load(j, j)
            with pool.Fori(0, AN // 2 - 1) as i:
                for j in range(2):
                    step(i, j, 2 * i + j, True)
            for j in range(2):
                step(AN // 2 - 1, j, AN - 2 + j, False)
            pool.drain().then_inc(a_dv, 1)
            pool.wait_ge(a_dv, ALINKS * AN + 1)
            lin = attr_tab[:, :].rearrange("r c -> (r c)")
            nc.gpsimd.dma_start(lin[FRONT:FRONT + E].rearrange("(p c) -> p c", p=AR), attr_l[0:AR, :])\
                .then_inc(a_st, 16)
            nc.gpsimd.dma_start(lin[0:FRONT].rearrange("(p c) -> p c", p=16), zeros[0:16, 0:FRONT // 16])\
                .then_inc(a_st, 16)
            nc.gpsimd.dma_start(lin[FRONT + E:SR * CH].rearrange("(p c) -> p c", p=16),
                                zeros[0:16, 0:PADS // 16]).then_inc(a_st, 16)
            pool.wait_ge(a_st, 48)
            windows_of(pool, attr_tab, attr_w, a_win)

        def windows_of(pool, tab, buf, s):
            last_chunk = pool.to_reg(SR - 1)
            for c in range(KCH):
                nc.gpsimd.indirect_dma_start(
                    out=buf[:, c * CH:(c + 1) * CH], out_offset=None, in_=tab[:, :],
                    in_offset=bass.IndirectOffsetOnAxis(ap=chunk[:, c:c + 1], axis=0),
                    bounds_check=last_chunk, oob_is_err=False).then_inc(s, 16)

        LN = EC // LQ
        LDV = 3

        def rows_of_edges(sp, lin, buf, s):
            full = (EC - 1) // P * P
            sp.dma_start(buf[:, 0:full // P, :],
                         lin[0:full * P].rearrange("(b p c) -> p b c", p=P, c=P)).then_inc(s, 16)
            sp.dma_start(buf[0:EC - 1 - full, full // P, :],
                         lin[full * P:(EC - 1) * P].rearrange("(p c) -> p c", c=P)).then_inc(s, 16)
            sp.dma_start(buf[EC - 1 - full:EC - full, full // P, 0:ETAIL],
                         lin[(EC - 1) * P:E].unsqueeze(0)).then_inc(s, 16)

        def logits_pool(pool):
            last_row = pool.to_reg(EB * P * P - 1)

            def step(i, j, q, reuse):
                if reuse:
                    pool.wait_ge(l_dv, LDV * (q - 1))
                    pool.sem_inc(s_turn, 1)
                nc.gpsimd.tensor_copy(idx_l[:, j, 0, :], src_c[:, bass.ds(q * LQ, LQ)])
                nc.gpsimd.tensor_copy(idx_l[:, j, 1, :], dst_c[:, bass.ds(q * LQ, LQ)]).then_inc(l_idx, 1)
                pool.wait_ge(l_idx, q + 1)
                pool.sem_inc(s_turn, 1)
                for a, tab in enumerate((score_src, score_dst)):
                    for c in range(LQ):
                        nc.gpsimd.indirect_dma_start(
                            out=got_l[:, j, a, c:c + 1], out_offset=None, in_=tab[:, :],
                            in_offset=bass.IndirectOffsetOnAxis(ap=idx_l[:, j, a, c:c + 1], axis=0),
                            bounds_check=last_row, oob_is_err=False).then_inc(l_got[j], 16)

            step(0, 0, 0, False)
            step(0, 1, 1, False)
            with pool.Fori(1, LN // 2) as i:
                for j in range(2):
                    step(i, j, 2 * i + j, True)
            step(LN // 2, 0, LN - 1, True)

        def logits_vector(dve):
            def step(i, j, q):
                n = [0]

                def chain(ins):
                    n[0] += 1
                    ins.then_inc(l_dv, 1)
                    dve.wait_ge(l_dv, LDV * q + n[0])

                dve.wait_ge(l_got[j], 2 * LQ * 16 * (i + 1))
                chain(nc.vector.tensor_tensor(got_l[:, j, 0, :], got_l[:, j, 0, :], got_l[:, j, 1, :], ALU.add))
                chain(nc.vector.tensor_tensor(got_l[:, j, 0, :], got_l[:, j, 0, :],
                                              logit_c[:, bass.ds(q * LQ, LQ)], ALU.add))
                chain(nc.vector.scalar_tensor_tensor(logit_c[:, bass.ds(q * LQ, LQ)], got_l[:, j, 0, :], ALPHA,
                                                     got_l[:, j, 0, :], ALU.mult, ALU.max))

            dve.wait_ge(l_tp, 1)
            link(dve, nc.vector.tensor_copy(logit_c[:, :], psX[:, :]))
            with dve.Fori(0, LN // 2) as i:
                for j in range(2):
                    step(i, j, 2 * i + j)
            step(LN // 2, 0, LN - 1)

        psS = psZ
        CHAIN = 5

        def tile_of(B, j, lag):
            C, jj = (B, j - lag) if j >= lag else (B.at(-1), j - lag + BT)
            t = C.t * BT + jj
            return C, jj, t, C.real and not (isinstance(t, int) and t >= NT)

        def later(C, jj, n):
            return not isinstance(C.t, int) or C.t * BT + jj >= n

        def attention_sync(sp):
            y = L[2]

            def load_res(b, t, C, jj):
                if later(C, jj, 0):
                    sp.wait_ge(y.x, t - NB + 1)
                sp.dma_start(res[:, b, :], x1_tab[bass.ds(t * P, P), :]).then_inc(y.res_ld[b], 16)

            def body(B):
                N = B.at(1)
                if N.real:
                    if N.after(U):
                        sp.wait_ge(a_chain, (N.t - U + 1) * CHAIN)
                    sp.dma_start(sm_mask[:, N.j, :, :], pair_tab[bass.ds(N.t * BT, BT), :, :]).then_inc(a_mask[N.j], 16)
                for j in range(BT):
                    C, jj, t, real = tile_of(B, j, 3)
                    if real:
                        last = isinstance(t, int) and t == NT - 1
                        n = TAIL if last else P
                        sp.wait_ge(y.x, t + 1)
                        sp.dma_start(out[bass.ds(t * P, n), :], x_out[0:n, jj % NB, :]).then_inc(y.x_st[jj % NB], 16)
                        if not (isinstance(t, int) and t + NB >= NT):
                            load_res(jj % NB, t + NB, C, jj)

            for j in range(NB):
                sp.wait_ge(L[1].x_st[j], 16 * uses(NT, NB, j))
            sp.wait_ge(s_runs_st, 16 * 2 * QT)
            table_written(sp, 2)
            for b in range(NB):
                sp.dma_start(res[:, b, :], x1_tab[b * P:(b + 1) * P, :]).then_inc(y.res_ld[b], 16)
            drive(sp, Step, NBAT, U, body, lead=1, flush=1)

        def attention_pool(pool):
            y = L[2]
            last_row = pool.to_reg(NP - 1)

            def body(G):
                if G.after(U):
                    pool.wait_ge(y.rows_ld[G.j], 16 * U * SLOTS * G.i)
                    pool.sem_inc(s_turn, 1)
                nc.gpsimd.tensor_copy(idx_b[:, G.j, :, :],
                                      idx_c[:, :, bass.ds(G.t * U, U)].rearrange("p s g -> p g s")).then_inc(a_idx, 1)
                pool.wait_ge(a_idx, G.t + 1)
                for q in range(U):
                    for s in range(SLOTS):
                        if G.after(U):
                            pool.wait_ge(y.aggregated, (G.t - U) * BT + q * QT + min(s + 1, QT))
                        pool.sem_inc(s_turn, 1)
                        nc.gpsimd.indirect_dma_start(
                            out=ring[:, G.j, q * SLOTS + s, :], out_offset=None, in_=rows_tab[2][:, :],
                            in_offset=bass.IndirectOffsetOnAxis(ap=idx_b[:, G.j, q, s:s + 1], axis=0),
                            bounds_check=last_row, oob_is_err=False).then_inc(y.rows_ld[G.j], 16)

            drive(pool, Step, NBAT, U, body)

        def attention_tensor(pe):
            y = L[2]

            def aggregate(C, jj, t):
                pe.wait_ge(y.sel, t + 1)
                if later(C, jj, 2):
                    pe.wait_ge(y.x, t - 1)
                for h in range(2):
                    last = nc.tensor.matmul(psG[jj % 2][:, 0:D], sel_w[:, jj % NB, h, :],
                                            ring[:, C.j, jj // QT * SLOTS + jj % QT + h, 0:D],
                                            start=(h == 0), stop=(h == 1))
                last.then_inc(y.aggregated, 1)

            def body(B):
                N = B.at(1)
                for j in range(BT):
                    if j == 0 and B.real:
                        pe.wait_ge(a_chain, (B.t + 1) * CHAIN)
                        pe.sem_inc(s_turn_p, 1)
                        for n, buf in enumerate((sm_e, sm_b)):
                            for h in range(2):
                                last = nc.tensor.transpose(psY[:, (2 * n + h) * BT:(2 * n + h + 1) * BT],
                                                           buf[:, h * P:(h + 1) * P], ident[0:BT, 0:BT])
                        last.then_inc(a_cols, 1)
                    if j == 5 and N.real:
                        pe.wait_ge(a_sum, N.t + 1)
                        for h in range(2):
                            last = nc.tensor.transpose(psX[0:BT, h * P:(h + 1) * P], score_e[:, h, :], ident[:, :])
                        last.then_inc(a_row, 1)
                    C, jj, t, real = tile_of(B, j, 2)
                    if real:
                        aggregate(C, jj, t)
                    if j < 4 and N.real:
                        for n in (2 * j, 2 * j + 1):
                            pe.wait_ge(a_sel, N.t * BT + n + 1)
                            if later(N, n, 2):
                                pe.wait_ge(a_cp, N.t * BT + n - 1)
                            for h in range(2):
                                last = nc.tensor.transpose(psT_b[n % 2][:, h * P:(h + 1) * P], sel_1[:, N.j, n, h, :],
                                                           ident_b[:, :])
                            last.then_inc(a_tp, 1)
                    if 1 <= j < 5 and N.real:
                        for n in (2 * j - 2, 2 * j - 1):
                            pe.wait_ge(a_cp, N.t * BT + n + 1)
                            for h in range(2):
                                c = h * BT + n
                                last = nc.tensor.matmul(psS[N.j][:, 3 * c:3 * c + 3], sel_T[:, n % NB, h, :],
                                                        s_col[:, N.j, :, n], start=True, stop=True)
                            last.then_inc(a_dst, 1)

            pe.wait_ge(L[1].x, NT)
            drive(pe, Step, NBAT, U, body, lead=1, flush=1)

        def attention_scalar(act):
            y = L[2]

            def body(B):
                N = B.at(1)
                for j in range(BT):
                    if j == 6 and N.real:
                        act.wait_ge(a_chain, N.t * CHAIN + 3)
                        nc.scalar.activation(sm_e, sm_a, ACT.Exp).then_inc(a_exp, 1)
                    C, jj, t, real = tile_of(B, j, 1)
                    if real:
                        act.wait_ge(a_w, C.t + 1)
                        if later(C, jj, NB):
                            act.wait_ge(y.aggregated, t - NB + 1)
                        for h in range(2):
                            last = nc.scalar.activation(sel_w[:, jj % NB, h, :], sel_1[:, C.j, jj, h, :], ACT.Copy,
                                                        scale=w_c[:, C.j, h * BT + jj:h * BT + jj + 1])
                        last.then_inc(y.sel, 1)
                    if j < 4 and N.real:
                        for n in (2 * j, 2 * j + 1):
                            act.wait_ge(a_tp, N.t * BT + n + 1)
                            if later(N, n, NB):
                                act.wait_ge(a_dst, N.t * BT + n - NB + 1)
                            nc.scalar.activation(sel_T[:, n % NB, :, :].rearrange("p h e -> p (h e)"),
                                                 psT_b[n % 2], ACT.Copy).then_inc(a_cp, 1)

            drive(act, Step, NBAT, U, body, lead=1, flush=1)

        def attention_vector(dve):
            y = L[2]

            def add_residual(C, jj, t):
                b = jj % NB
                dve.wait_ge(y.aggregated, t + 1)
                dve.wait_ge(y.res_ld[b], 16 * (C.t * U + jj // NB + 1))
                if later(C, jj, NB):
                    dve.wait_ge(y.x_st[b], 16 * (C.t * U + jj // NB))
                nc.vector.tensor_tensor(x_out[:, b, :], psG[jj % 2][:, 0:D], res[:, b, :], ALU.add).then_inc(y.x, 1)

            def select(N, n):
                if N.after(U):
                    dve.wait_ge(y.sel, (N.t - U) * BT + n + 1)
                for h in range(2):
                    last = nc.vector.tensor_scalar(sel_1[:, N.j, n, h, :], iota_n[:, :],
                                                   loc_c[:, 2 * (n % QT) + h, bass.ds(N.t * U + n // QT, 1)],
                                                   None, ALU.is_equal)
                last.then_inc(a_sel, 1)

            def chain(N, n, ins):
                ins.then_inc(a_chain, 1)
                dve.wait_ge(a_chain, N.t * CHAIN + n)

            def softmax(N, j):
                rst = sm_mask[:, N.j, 1, :]
                if j == 4:
                    dve.wait_ge(y.rows_ld[N.j], 16 * U * SLOTS * (N.i + 1))
                    nc.vector.tensor_tensor(half_c[:, :, :], ring[:, N.j, :, D].rearrange("p (g s) -> p g s", g=U),
                                            attr_c[:, bass.ds(N.t * U, U), :], ALU.add).then_inc(a_half, 1)
                    dve.wait_ge(a_dst, (N.t + 1) * BT)
                    nc.vector.tensor_reduce(dst_e[:, :], psS[N.j][:, 0:6 * BT].rearrange("p (c a) -> p c a", a=3),
                                            AX_X, ALU.add).then_inc(a_half, 1)
                    dve.wait_ge(a_half, 3 * N.t + 2)
                    for h in range(2):
                        last = nc.vector.tensor_tensor(
                            sum_e[:, h, :].rearrange("p (g b) -> p g b", g=U), half_c[:, :, h:h + QT],
                            dst_e[:, h * BT:(h + 1) * BT].rearrange("p (g b) -> p g b", g=U), ALU.add)
                    last.then_inc(a_half, 1)
                    dve.wait_ge(a_half, 3 * N.t + 3)
                    nc.vector.scalar_tensor_tensor(score_e[:, :, :], sum_e[:, :, :], ALPHA, sum_e[:, :, :],
                                                   ALU.mult, ALU.max).then_inc(a_sum, 1)
                if j == 5:
                    dve.wait_ge(a_row, N.t + 1)
                    dve.wait_ge(a_mask[N.j], 16 * (N.i + 1))
                    chain(N, 1, nc.vector.tensor_tensor_scan(sm_a, rst[:, 0:2 * P], psX[0:BT, 0:2 * P], -BIG,
                                                             ALU.add, ALU.max))
                    chain(N, 2, nc.vector.tensor_tensor_scan(sm_b[:, ::-1], rst[:, 2 * P:0:-1], sm_a[:, ::-1], -BIG,
                                                             ALU.add, ALU.max))
                    chain(N, 3, nc.vector.tensor_tensor(sm_a, psX[0:BT, 0:2 * P], sm_b, ALU.subtract))

            def sums(B):
                same = sm_mask[:, B.j, 0, :]
                dve.wait_ge(a_exp, B.t + 1)
                chain(B, 4, nc.vector.tensor_tensor_scan(sm_a, same[:, 0:2 * P], sm_e, 0.0, ALU.mult, ALU.add))
                chain(B, 5, nc.vector.tensor_tensor_scan(sm_b[:, ::-1], same[:, 2 * P:0:-1], sm_a[:, ::-1], 0.0,
                                                         ALU.mult, ALU.max))

            def body(B):
                N = B.at(1)
                for j in range(BT):
                    C, jj, t, real = tile_of(B, j, 3)
                    if real:
                        add_residual(C, jj, t)
                    if j == 7 and N.real:
                        sums(N)
                    if j == 0 and B.real:
                        dve.wait_ge(a_cols, B.t + 1)
                        nc.vector.reciprocal(inv_c[:, :], psY[:, 2 * BT:4 * BT]).then_inc(a_inv, 1)
                        dve.wait_ge(a_inv, B.t + 1)
                        nc.vector.tensor_tensor(w_c[:, B.j, :], psY[:, 0:2 * BT], inv_c[:, :], ALU.mult)\
                            .then_inc(a_w, 1)
                    if N.real:
                        if j == 0:
                            nc.vector.tensor_scalar(s_col[:, N.j, :, :], score_p[:, :, bass.ds(N.t * BT, BT)], 0.0,
                                                    None, ALU.add)
                        if j < 4:
                            select(N, 2 * j)
                            select(N, 2 * j + 1)
                        softmax(N, j)

            dve.wait_ge(sc_kept, NT)
            parts_n = [0]

            def part(ins):
                link(dve, ins, s_parts, parts_n)

            part(nc.vector.tensor_copy(score_p[:, 0, :], score_c[:, 1, :]))
            part(nc.vector.tensor_tensor(rest[0], score_c[:, 1, :], score_p[:, 0, :], ALU.subtract))
            part(nc.vector.tensor_copy(score_p[:, 1, :], rest[0]))
            part(nc.vector.tensor_tensor(rest[1], rest[0], score_p[:, 1, :], ALU.subtract))
            part(nc.vector.tensor_copy(score_p[:, 2, :], rest[1]))
            dve.wait_ge(s_runs_st, 16 * 2 * QT)
            dve.wait_ge(L[1].aggregated, NT)
            table_written(dve, 2)
            for j in range(NB):
                dve.wait_ge(L[1].x_st[j], 16 * uses(NT, NB, j))
            drive(dve, Step, NBAT, U, body, lead=1, flush=1)

        def spread(dve, last_of_run, total):
            link(dve, nc.vector.tensor_tensor_scan(total[:, ::-1], next_w[:, ::-1], last_of_run[:, ::-1], 0.0,
                                                   ALU.mult, ALU.max))

        def to_columns(pe, parts):
            for bank, n, source in parts:
                last = nc.tensor.transpose(bank[:, n * NG:(n + 1) * NG], source, ident[0:NG, 0:NG])
            last.then_inc(s_tp, 1)

        TP_SRC, TP_DST, TP_W, TP_V, TP_FIRST, TP_IDX, TP_LOC, TP_WGT, TP_ATTR, TP_TALLY = range(1, 11)

        block = ctx.enter_context(nc.Block())

        @block.sync
        def _(sp):
            sp.wait_ge(s_const, 1)
            for tab, pad, fill, front in ((dst, dst_pad, pad_i, pad_f), (src, src_pad, pad_z, pad_z)):
                lin = pad[:, :].rearrange("r c -> (r c)")
                sp.dma_start(lin[FRONT:FRONT + E].rearrange("(a c) -> a c", a=16),
                             tab[0:E].rearrange("(a c) -> a c", a=16)).then_inc(s_pads, 16)
                sp.dma_start(lin[FRONT + E:SR * CH].rearrange("(a c) -> a c", a=16), fill[:, :]).then_inc(s_pads, 16)
                sp.dma_start(lin[0:FRONT].rearrange("(a c) -> a c", a=16), front[:, 0:FRONT // 16])\
                    .then_inc(s_pads, 16)
            for n, m in enumerate(mats):
                sp.dma_start(w_nat[:, n, :, :], m.rearrange("(h p) d -> p h d", p=P)).then_inc(s_w, 16)
            for n, b in enumerate((b1, b2)):
                sp.dma_start(bias_full[:, n, :], b.unsqueeze(0).to_broadcast([P, D])).then_inc(s_w, 16)
            sp.dma_start(a_col[:, :], A[0, 0:2 * D].rearrange("(q p) -> p q", p=P),
                         allow_slow_non_contiguous=True).then_inc(s_w, 16)
            sp.dma_start(a_edge[:, :], A[0:1, 2 * D:2 * D + ED].to_broadcast([P, ED])).then_inc(s_w, 16)
            sp.wait_ge(s_pads, 96)
            sp.dma_start(firsts_i[:, :], dst_pad[FRONT // CH:SR, 0:1].rearrange("r o -> o r"),
                         allow_slow_non_contiguous=True).then_inc(s_firsts, 16)
            for tab, buf in ((src, src_rows), (dst, dst_rows)):
                rows_of_edges(sp, tab, buf, s_edges)
            ln_sync(sp)
            sp.wait_ge(s_runs, 1)
            for b in range(QT):
                for a, w in enumerate((same_w, rst_w)):
                    sp.dma_start(pair_tab[:, a, :].rearrange("(g b) e -> b g e", b=QT)[b], w[:, b * P:b * P + WPAIR])\
                        .then_inc(s_runs_st, 16)
            general = is_general(sp)
            for k in range(3):
                with sp.If(general):
                    if k == 2:
                        sp.wait_ge(s_score_v, 2)
                        for a, tab in enumerate((score_src, score_dst)):
                            for b in range(EB):
                                sp.dma_start(tab[b * P * P:(b + 1) * P * P, :].rearrange("(r c) o -> r (c o)", c=P),
                                             score_r[:, a, b, :]).then_inc(s_score_st, 16)
                        sp.wait_ge(a_st, 48)
                        sp.wait_ge(l_attr, 1)
                        rows_of_edges(sp, attr_tab[:, :].rearrange("r c -> (r c)")[FRONT:FRONT + E], attr_r, l_rows)
                    general_sync(sp, k)
                    if k == 2:
                        layer_sync(sp, k)
                if k < 2:
                    layer_sync(sp, k)
                else:
                    with sp.Else():
                        attention_sync(sp)
            sp.wait_ge(s_runs_st, 16 * 2 * QT)
            for j in range(NB):
                sp.wait_ge(L[2].x_st[j], 16 * uses(NT, NB, j))

        @block.gpsimd
        def _(pool):
            pool_n = [0]

            def chain(ins):
                link(pool, ins, s_pl, pool_n)

            nc.gpsimd.memset(zeros[:, :], 0.0)
            nc.gpsimd.memset(eps[:, :], EPS)
            nc.gpsimd.memset(pad_i[:, :], PAD_DST)
            nc.gpsimd.memset(pad_f[:, :], -1)
            nc.gpsimd.memset(pad_z[:, :], 0)
            nc.gpsimd.memset(src_rows[:, :, :], 0)
            chain(nc.gpsimd.memset(dst_rows[:, :, :], PAD_DST))
            pool.sem_inc(s_const, 1)
            nc.gpsimd.memset(lower[:, :], 1.0)
            chain(nc.gpsimd.memset(ident[:, :], 0.0))
            nc.gpsimd.affine_select(out=ident[:, :], in_=ident[:, :], compare_op=ALU.not_equal, fill=1.0,
                                    base=0, pattern=[[-1, P]], channel_multiplier=1)
            chain(nc.gpsimd.drain())
            nc.gpsimd.tensor_copy(ident_b[:, :], ident[:, :])
            nc.gpsimd.affine_select(out=lower[:, :], in_=lower[:, :], compare_op=ALU.is_gt, fill=0.0,
                                    base=0, pattern=[[-1, P]], channel_multiplier=1)
            nc.gpsimd.memset(ones[:, :], 1.0)
            nc.gpsimd.memset(ones_b[:, :], 1.0)
            nc.gpsimd.iota(iota_i[:, :], pattern=[[1, P]], base=0, channel_multiplier=0)
            nc.gpsimd.iota(part_i[:, :], pattern=[[0, 1]], base=0, channel_multiplier=1)
            nc.gpsimd.iota(tile0_i[:, :], pattern=[[P, QT + 1]], base=0, channel_multiplier=QT * P)
            chain(nc.gpsimd.memset(bias_rows[:, :, :], 0.0))
            pool.sem_inc(s_const, 1)
            nc.gpsimd.memset(got_l[:, :, :, :], 0.0)
            nc.gpsimd.memset(arena[:, 8 * WIN:8 * WIN + 4 * P], 0.0)
            chain(nc.gpsimd.memset(score_c[:, :, :], 0.0))
            pool.wait_ge(s_chunk, 1)
            pool.wait_ge(s_pads, 96)
            windows_of(pool, dst_pad, dst_w, s_win)
            windows_of(pool, src_pad, src_w, s_win)
            attr_pool(pool)
            general = is_general(pool)
            for k in range(3):
                table_written(pool, k)
                with pool.If(general):
                    if k == 2:
                        pool.wait_ge(s_score_st, 32 * EB)
                        logits_pool(pool)
                    general_pool(pool, k)
                    layer_pool(pool, k, sums_tab[k])
                with pool.Else():
                    if k < 2:
                        layer_pool(pool, k, rows_tab[k])
                    else:
                        attention_pool(pool)

        @block.scalar
        def _(act):
            ln_scalar(act)
            general = is_general(act)
            for k in range(3):
                with act.If(general):
                    general_scalar(act, k)
                if k < 2:
                    layer_scalar(act, k)
                else:
                    with act.Else():
                        attention_scalar(act)

        @block.tensor
        def _(pe):
            pe.wait_ge(s_const, 2)
            pe.wait_ge(s_edges_f, 1)
            for a in range(2):
                for b in range(EB):
                    last = nc.tensor.transpose((psX, psY)[a][:, b * P:(b + 1) * P], edge_f[:, a, b, :], ident[:, :])
                last.then_inc(s_tp, 1)
            pe.wait_ge(s_w, 16 * 9)
            for n in range(5):
                for ih in range(H):
                    for oh in range(H):
                        last = nc.tensor.transpose(banks[n][:, ih * D + oh * P:ih * D + (oh + 1) * P],
                                                   w_nat[:, n, oh, ih * P:(ih + 1) * P], ident[:, :])
            last.then_inc(s_tp, 1)
            for a in range(2):
                for ih in range(H):
                    for oh in range(H):
                        last = nc.tensor.matmul(psB[3][:, 2 * ih + a:2 * ih + a + 1],
                                                w_nat[:, 4, oh, ih * P:(ih + 1) * P],
                                                a_col[:, a * H + oh:a * H + oh + 1],
                                                start=(oh == 0), stop=(oh == H - 1))
            last.then_inc(s_tp, 1)
            pe.wait_ge(s_firsts_f, 1)
            for c in range(FB):
                n = min(512, FC - 512 * c)
                last = nc.tensor.matmul(banks[c][0:NG, 0:n], ones[0:1, 0:NG], firsts[0:1, 512 * c:512 * c + n],
                                        start=True, stop=True)
            last.then_inc(s_tp, 1)
            pe.wait_ge(s_chunk, 1)
            ln_tensor(pe)
            pe.wait_ge(ln_z_done, NT)
            pe.wait_ge(s_mk, 1)
            to_columns(pe, [(psA[0], s, srcf_w[:, s * P:(s + 1) * P]) for s in range(SLOTS)])
            to_columns(pe, [((psA[1], psB[0])[n // 5], n % 5, loc_w[:, n, :]) for n in range(2 * QT)])
            pe.wait_ge(s_mk, 2)
            to_columns(pe, [(psB[1], s, weight_w[:, s * P:(s + 1) * P]) for s in range(SLOTS)])
            pe.wait_ge(a_win, 16 * KCH)
            to_columns(pe, [(psB[2], s, attr_w[:, s * P:(s + 1) * P]) for s in range(SLOTS)])
            nc.tensor.matmul(psX[0:1, 0:2], ones[0:NG, 0:1], tally[:, :], start=True, stop=True).then_inc(s_tp, 1)
            general = is_general(pe)
            for k in range(3):
                with pe.If(general):
                    if k == 2:
                        pe.wait_ge(s_score, 1)
                        for a in range(2):
                            for b in range(EB):
                                last = nc.tensor.transpose((psX, psY)[a][:, b * P:(b + 1) * P],
                                                           score_c[:, a, b * P:(b + 1) * P], ident[:, :])
                        last.then_inc(s_score, 1)
                        pe.wait_ge(l_attr, 2)
                        for b in range(EB):
                            last = nc.tensor.transpose(psX[:, b * P:(b + 1) * P], attr_r[:, b, :], ident[:, :])
                        last.then_inc(l_tp, 1)
                    general_tensor(pe, k)
                    if k == 2:
                        layer_tensor(pe, k)
                if k < 2:
                    layer_tensor(pe, k)
                else:
                    with pe.Else():
                        attention_tensor(pe)

        @block.vector
        def _(dve):
            def mark(ins, s):
                ins.then_inc(s, 1)

            dve.wait_ge(s_const, 2)
            nc.vector.tensor_copy(iota_n[:, :], iota_i[:, :])
            nc.vector.tensor_copy(part_n[:, :], part_i[:, :])
            link(dve, nc.vector.tensor_copy(tile0[:, :], tile0_i[:, :]))
            dve.wait_ge(s_w, 16 * 9)
            link(dve, nc.vector.tensor_copy(bias_part[:, 0, :, :], bias_full[:, :, :]))
            link(dve, nc.vector.tensor_tensor(bias_rest[:, :, :], bias_full[:, :, :], bias_part[:, 0, :, :],
                                              ALU.subtract))
            link(dve, nc.vector.tensor_copy(bias_part[:, 1, :, :], bias_rest[:, :, :]))
            link(dve, nc.vector.tensor_tensor(bias_rest[:, :, :], bias_rest[:, :, :], bias_part[:, 1, :, :],
                                              ALU.subtract))
            link(dve, nc.vector.tensor_copy(bias_part[:, 2, :, :], bias_rest[:, :, :]))
            for n in range(3):
                nc.vector.tensor_copy(bias_rows[32 * n:32 * n + 1, :, :], bias_part[32 * n:32 * n + 1, n, :, :])
            dve.wait_ge(s_edges, 16 * 6)
            nc.vector.tensor_copy(edge_f[:, 0, :, :], src_rows[:, :, :])
            nc.vector.tensor_copy(edge_f[:, 1, :, :], dst_rows[:, :, :]).then_inc(s_edges_f, 1)
            dve.wait_ge(s_firsts, 16)
            link(dve, nc.vector.tensor_copy(firsts[:, :], firsts_i[:, :]))
            link(dve, nc.vector.memset(firsts[:, E // CH:LAST // CH], float(LAST - 1)))
            dve.wait_ge(s_tp, TP_SRC)
            nc.vector.tensor_copy(src_c[:, :], psX[:, :])
            dve.wait_ge(s_tp, TP_DST)
            nc.vector.tensor_copy(dst_c[:, :], psY[:, :])
            nc.vector.tensor_copy(dst_f[:, :], psY[:, :])
            dve.wait_ge(s_tp, TP_W)
            for n in range(4):
                last = nc.vector.tensor_copy(w_hi[:, n, :, :].rearrange("p h d -> p (h d)"), banks[n][:, :])
            link(dve, last)
            for n in range(4):
                nc.vector.tensor_tensor(w_lo[:, n, :, :].rearrange("p h d -> p (h d)"), banks[n][:, :],
                                        w_hi[:, n, :, :].rearrange("p h d -> p (h d)").bitcast(F32), ALU.subtract)
            nc.vector.tensor_copy(w_att[:, :, 0:D], banks[4][:, :].rearrange("p (h d) -> p h d", h=H))
            dve.wait_ge(s_tp, TP_V)
            link(dve, nc.vector.tensor_copy(w_att[:, :, D:D + 2],
                                            psB[3][:, 0:2 * H].rearrange("p (h a) -> p h a", h=H)))
            dve.sem_inc(s_firsts_f, 1)
            dve.wait_ge(s_tp, TP_FIRST)
            for c in range(FB):
                n = min(512, FC - 512 * c)
                for h in range(2):
                    link(dve, nc.vector.tensor_scalar(below[:, h, 0:n], banks[c][0:NG, 0:n],
                                                      tile0[:, QT * h:QT * h + 1], 0.0, ALU.is_lt, ALU.add,
                                                      accum_out=counts[:, h, c:c + 1]))
            link(dve, nc.vector.tensor_reduce(count2[:, :], counts[:, :, :], AX_X, ALU.add))
            link(dve, nc.vector.tensor_tensor(start_f[:, :], count2[:, 0:1], count2[:, 1:2], ALU.add))
            link(dve, nc.vector.tensor_scalar(start_f[:, :], start_f[:, :], 0.5,
                                              float(FRONT // CH - KCH // 2) - 0.5, ALU.mult, ALU.add))
            link(dve, nc.vector.tensor_scalar(start_f[:, :], start_f[:, :], 0.0, None, ALU.max))
            link(dve, nc.vector.tensor_copy(start_i[:, :], start_f[:, :]))
            link(dve, nc.vector.tensor_copy(start_f[:, :], start_i[:, :]))
            link(dve, nc.vector.tensor_scalar(chunk_f[:, :], iota_n[0:NG, 0:KCH], start_f[:, 0:1], None, ALU.add))
            nc.vector.tensor_copy(chunk[:, :], chunk_f[:, :]).then_inc(s_chunk, 1)

            ln_vector(dve)

            dve.wait_ge(s_win, 16 * 2 * KCH)
            table_written(dve, 0)
            nc.vector.tensor_copy(srcf_w[:, :], src_w[:, :])
            link(dve, nc.vector.tensor_copy(dstf_w[:, :], dst_w[:, :]))
            for n, (s, b) in enumerate(PAIRS):
                last = nc.vector.tensor_scalar(loc_w[:, n, :], dstf_w[:, s * P:(s + 1) * P], tile0[:, b:b + 1],
                                               None, ALU.subtract)
            link(dve, last)
            link(dve, nc.vector.tensor_scalar(in_w[:, :, :], loc_w[:, :, :], 0.0, None, ALU.is_ge))
            link(dve, nc.vector.scalar_tensor_tensor(valid_w[:, :, :], loc_w[:, :, :], float(P), in_w[:, :, :],
                                                     ALU.is_lt, ALU.mult))
            nc.vector.tensor_copy(any_w[:, 0:P], valid_w[:, 0, :])
            nc.vector.tensor_copy(any_w[:, WIN - P:WIN], valid_w[:, 2 * QT - 1, :])
            link(dve, nc.vector.tensor_tensor(any_w[:, P:WIN - P].rearrange("g (s c) -> g s c", c=P),
                                              valid_w[:, 1:2 * QT - 1:2, :], valid_w[:, 2:2 * QT - 1:2, :], ALU.add))
            link(dve, nc.vector.tensor_scalar(any_w[:, :], any_w[:, :], -SKIP, SKIP, ALU.mult, ALU.add))
            mark(nc.vector.tensor_tensor(srcf_w[:, :], srcf_w[:, :], any_w[:, :], ALU.add), s_mk)
            link(dve, nc.vector.tensor_reduce(tally[:, 0:1], valid_w[:, :, :].rearrange("g n c -> g (n c)"),
                                              AX_X, ALU.add))
            nc.vector.memset(same_w[:, 0:1], 0.0)
            nc.vector.memset(same_w[:, WIN:WIN + 1], 0.0)
            nc.vector.memset(next_w[:, WIN - 1:WIN], 0.0)
            link(dve, nc.vector.tensor_tensor(same_w[:, 1:WIN], dstf_w[:, 1:WIN], dstf_w[:, 0:WIN - 1],
                                              ALU.is_equal))
            link(dve, nc.vector.tensor_copy(next_w[:, 0:WIN - 1], same_w[:, 1:WIN]))
            mark(nc.vector.tensor_scalar(rst_w[:, :], same_w[:, :], -1.0, BIG, ALU.add, ALU.mult), s_runs)
            link(dve, nc.vector.tensor_tensor(run_b[:, 1:WIN], dstf_w[:, 0:WIN - 1], dstf_w[:, 1:WIN], ALU.is_gt))
            link(dve, nc.vector.tensor_reduce(tally[:, 1:2], run_b[:, 1:WIN], AX_X, ALU.add))
            link(dve, nc.vector.memset(run_b[:, :], 1.0))
            link(dve, nc.vector.tensor_tensor_scan(run_a[:, :], same_w[:, 0:WIN], run_b[:, :], 0.0, ALU.mult, ALU.add))
            spread(dve, run_a, run_b)
            mark(nc.vector.reciprocal(weight_w[:, :], run_b[:, :]), s_mk)
            dve.wait_ge(s_tp, TP_IDX)
            nc.vector.tensor_copy(idx_c[:, :, :].rearrange("p s g -> p (s g)"), psA[0][:, 0:SLOTS * NG])
            dve.wait_ge(s_tp, TP_LOC)
            nc.vector.tensor_copy(loc_c[:, 0:5, :].rearrange("p s g -> p (s g)"), psA[1][:, 0:5 * NG])
            nc.vector.tensor_copy(loc_c[:, 5:2 * QT, :].rearrange("p s g -> p (s g)"),
                                  psB[0][:, 0:(2 * QT - 5) * NG])
            dve.wait_ge(s_tp, TP_WGT)
            link(dve, nc.vector.tensor_copy(wgt_c[:, :, :].rearrange("p s g -> p (s g)"), psB[1][:, 0:SLOTS * NG]))
            dve.wait_ge(s_tp, TP_ATTR)
            nc.vector.tensor_copy(attr_c[:, :, :].rearrange("p g s -> p s g"),
                                  psB[2][:, 0:SLOTS * NG].rearrange("p (s g) -> p s g", s=SLOTS))
            dve.wait_ge(s_tp, TP_TALLY)
            link(dve, nc.vector.tensor_scalar(tally1[:, 0:1], psX[0:1, 0:1], float(E), None, ALU.not_equal))
            link(dve, nc.vector.tensor_scalar(tally1[:, 1:2], psX[0:1, 1:2], 0.0, None, ALU.is_gt))
            mark(nc.vector.tensor_tensor(general_i[:, :], tally1[:, 0:1], tally1[:, 1:2], ALU.max), s_flag)
            general = is_general(dve)
            for k in range(3):
                with dve.If(general):
                    if k == 2:
                        dve.wait_ge(sc_kept, NT)
                        dve.sem_inc(s_score, 1)
                        dve.wait_ge(s_score, 2)
                        for a in range(2):
                            nc.vector.tensor_copy(score_r[:, a, :, :].rearrange("p b c -> p (b c)"),
                                                  (psX, psY)[a][:, :]).then_inc(s_score_v, 1)
                        nc.vector.memset(attr_r[:, :, :], 0.0).then_inc(l_attr, 1)
                        dve.wait_ge(l_rows, 48)
                        dve.sem_inc(l_attr, 1)
                        logits_vector(dve)
                        nc.vector.drain().then_inc(l_attr, 1)
                        dve.wait_ge(l_attr, 3)
                    general_vector(dve, k)
                    if k == 2:
                        nc.vector.drain().then_inc(L[k].ready, 1)
                        layer_vector(dve, k)
                if k < 2:
                    nc.vector.drain().then_inc(L[k].ready, 1)
                    layer_vector(dve, k)
                else:
                    with dve.Else():
                        attention_vector(dve)


_INS = ['x', 'src', 'dst', 'edge_attr_64', 'L0_gnn_W1l', 'L0_gnn_b1', 'L0_gnn_W1r', 'L0_gnn_W2l', 'L0_gnn_b2',
        'L0_gnn_W2r', 'L1_gnn_W', 'L1_gnn_A']


def kernel(**inputs):
    import concourse.bacc as _bacc
    from concourse.bass_utils import run_bass_kernel_spmd as _run

    nc = _bacc.Bacc("TRN2", target_bir_lowering=False, num_devices=1)
    arrays, args = {}, []
    for name in _INS:
        a = np.ascontiguousarray(inputs[name])
        arrays[f"in_{name}"] = a
        args.append(nc.dram_tensor(f"in_{name}", a.shape, mybir.dt.from_np(a.dtype), kind="ExternalInput").ap())
    shape = inputs['x'].shape
    args.append(nc.dram_tensor("out", tuple(shape), F32, kind="ExternalOutput").ap())
    gnn_program(nc, *args)
    r = _run(nc, [arrays], core_ids=[0])
    return r.results[0]["out"]
```
